# Optimizing a Trainium2 kernel written in Bass

```python
import numpy as np
import jax
import jax.numpy as jnp

def _softmax(x, axis=-1):
    return jax.nn.softmax(x, axis=axis)

def _gelu(x):
    return jax.nn.gelu(x, approximate=True)

def _silu(x):
    return jax.nn.silu(x)

def _sigmoid(x):
    return jax.nn.sigmoid(x)

def _layernorm(x, axis=-1, eps=1e-05):
    m = jnp.mean(x, axis=axis, keepdims=True)
    v = jnp.var(x, axis=axis, keepdims=True)
    return (x - m) / jnp.sqrt(v + eps)

def _scatter_add(tgt, idx, src, axis=0):
    return tgt.at[idx].add(src)

def _segment_sum(src, seg, n):
    return jax.ops.segment_sum(src, seg, n)
kernel_name = 'mk_pixart_seq_d4_seqx_r4_e988e0'

def setup_inputs(seed: int=0):
    np.random.seed(seed)
    _w = jnp.asarray

    def _rec_inputs():
        import jax
        import jax.numpy as jnp
        _rk = jax.random.key(seed)
        x = -0.0002928 + 1 * jax.random.normal(jax.random.fold_in(_rk, 1), (4, 512, 256), jnp.float32)
        _lenS = 512 - jax.random.randint(jax.random.fold_in(_rk, 7), (4,), 0, max(1, 512 // 4) + 1, jnp.int32)
        _lenS2 = 512 - jax.random.randint(jax.random.fold_in(_rk, 8), (4,), 0, max(1, 512 // 4) + 1, jnp.int32)
        cond_1024 = 0.000887014 + 1.03683 * jax.random.normal(jax.random.fold_in(_rk, 11), (4, 256), jnp.float32)
        _ctx_1024P = jax.random.normal(jax.random.fold_in(_rk, 12), (4, 16, 256), jnp.float32)
        _ctx_1024c = jax.random.dirichlet(jax.random.fold_in(_rk, 512), 0.3 * jnp.ones((16,), jnp.float32), (4, 512))
        _ctx_1024t = jnp.einsum('bsk,bkd->bsd', _ctx_1024c, _ctx_1024P)
        _ctx_1024t = _ctx_1024t * jax.lax.rsqrt(jnp.mean(jnp.square(_ctx_1024t)) + 1e-12) * 0.953939
        ctx_1024 = 0.00086875 + 0.999764 * (_ctx_1024t + 0.3 * jax.random.normal(jax.random.fold_in(_rk, 612), (4, 512, 256), jnp.float32))
        return (x, cond_1024, ctx_1024)
    x, cond_1024, ctx_1024 = _rec_inputs()

    def _L0_xcond_setup():
        import jax, jax.numpy as jnp
        import numpy as np
        import math
        D_MODEL = 256
        N_HEADS = 16
        HEAD_DIM = D_MODEL // N_HEADS
        D_FF = 1024
        EPS = 1e-05
        ROPE_BASE = 10000.0

        def _rope(t):
            L, Dh = (t.shape[1], t.shape[-1])
            half = Dh // 2
            inv_freq = 1.0 / ROPE_BASE ** (jnp.arange(half, dtype=t.dtype) / half)
            ang = jnp.arange(L, dtype=t.dtype)[:, None] * inv_freq[None, :]
            cos = jnp.cos(ang)[None, :, None, :]
            sin = jnp.sin(ang)[None, :, None, :]
            t1, t2 = (t[..., :half], t[..., half:])
            return jnp.concatenate([t1 * cos - t2 * sin, t2 * cos + t1 * sin], axis=-1)

        def _adaln(x, emb, w, b):
            e = emb[:, 0, :]
            gb = e @ w.T + b
            gamma, beta = jnp.split(gb, 2, axis=-1)
            mu = x.mean(-1, keepdims=True)
            var = x.var(-1, keepdims=True)
            xn = (x - mu) * jax.lax.rsqrt(var + EPS)
            return xn * (1.0 + gamma[:, None, :]) + beta[:, None, :]

        def _attn(q, k, v):
            scale = 1.0 / math.sqrt(HEAD_DIM)
            scores = jnp.einsum('bqhd,bkhd->bhqk', q, k) * scale
            w = jax.nn.softmax(scores, axis=-1)
            out = jnp.einsum('bhqk,bkhd->bqhd', w, v)
            B, Lq = (out.shape[0], out.shape[1])
            return out.reshape(B, Lq, D_MODEL)
        key = jax.random.key(seed)
        ks = jax.random.split(key, 24)
        s = 0.02
        inp = {'x': jax.random.normal(ks[0], (2, 512, D_MODEL), jnp.float32), 'noise_emb': jax.random.normal(ks[1], (2, 1, D_MODEL), jnp.float32), 'context': jax.random.normal(ks[2], (2, 256, D_MODEL), jnp.float32), 'ln1_w': jax.random.normal(ks[3], (2 * D_MODEL, D_MODEL), jnp.float32) * s, 'ln1_b': jax.random.normal(ks[4], (2 * D_MODEL,), jnp.float32) * s, 'ln2_w': jax.random.normal(ks[5], (2 * D_MODEL, D_MODEL), jnp.float32) * s, 'ln2_b': jax.random.normal(ks[6], (2 * D_MODEL,), jnp.float32) * s, 'ln3_w': jax.random.normal(ks[7], (2 * D_MODEL, D_MODEL), jnp.float32) * s, 'ln3_b': jax.random.normal(ks[8], (2 * D_MODEL,), jnp.float32) * s, 'qkv_w': jax.random.normal(ks[9], (3 * D_MODEL, D_MODEL), jnp.float32) * s, 'sa_out_w': jax.random.normal(ks[10], (D_MODEL, D_MODEL), jnp.float32) * s, 'q_w': jax.random.normal(ks[11], (D_MODEL, D_MODEL), jnp.float32) * s, 'k_w': jax.random.normal(ks[12], (D_MODEL, D_MODEL), jnp.float32) * s, 'v_w': jax.random.normal(ks[13], (D_MODEL, D_MODEL), jnp.float32) * s, 'ca_out_w': jax.random.normal(ks[14], (D_MODEL, D_MODEL), jnp.float32) * s, 'ffn_w1': jax.random.normal(ks[15], (D_FF, D_MODEL), jnp.float32) * s, 'ffn_b1': jax.random.normal(ks[16], (D_FF,), jnp.float32) * s, 'ffn_w2': jax.random.normal(ks[17], (D_MODEL, D_FF), jnp.float32) * s, 'ffn_b2': jax.random.normal(ks[18], (D_MODEL,), jnp.float32) * s}
        return inp
    _L0_xcond_all = _L0_xcond_setup()
    _L0_xcond_in = {k: v for k, v in _L0_xcond_all.items() if k in ('ln1_w', 'ln1_b', 'ln2_w', 'ln2_b', 'ln3_w', 'ln3_b', 'qkv_w', 'sa_out_w', 'q_w', 'k_w', 'v_w', 'ca_out_w', 'ffn_w1', 'ffn_b1', 'ffn_w2', 'ffn_b2')}
    del _L0_xcond_all

    def _L1_xcond_setup():
        import jax, jax.numpy as jnp
        import numpy as np
        H = 256
        RH = 2 * H
        E = 3
        B, T, P = (8, 512, 64)
        LN_EPS = 1e-05

        def _layer_norm(x, gamma, beta):
            mu = jnp.mean(x, axis=-1, keepdims=True)
            var = jnp.mean(jnp.square(x - mu), axis=-1, keepdims=True)
            return (x - mu) * jax.lax.rsqrt(var + LN_EPS) * gamma + beta
        key = jax.random.key(seed)
        ks = jax.random.split(key, 24)
        s = lambda fan_in: 1.0 / np.sqrt(fan_in)
        inp = {'mix_hidden_states': jax.random.normal(ks[0], (B, T, H), jnp.float32), 'global_anchor': jax.random.normal(ks[1], (B, H), jnp.float32), 'prototype_bank': jax.random.normal(ks[2], (B, P, H), jnp.float32), 'ln_gamma': jnp.ones((H,), jnp.float32), 'ln_beta': jnp.zeros((H,), jnp.float32), 'Wq': jax.random.normal(ks[3], (H, H), jnp.float32) * s(H), 'Wk': jax.random.normal(ks[4], (H, H), jnp.float32) * s(H), 'Wv': jax.random.normal(ks[5], (H, H), jnp.float32) * s(H), 'router_W': jax.random.normal(ks[6], (3 * H, E), jnp.float32) * s(3 * H), 'router_b': jnp.zeros((E,), jnp.float32), 'e_w1': jax.random.normal(ks[7], (E, 3 * H, RH), jnp.float32) * s(3 * H), 'e_b1': jnp.zeros((E, RH), jnp.float32), 'e_w2': jax.random.normal(ks[8], (E, RH, H), jnp.float32) * s(RH), 'e_b2': jnp.zeros((E, H), jnp.float32), 'gate_w1': jax.random.normal(ks[9], (3 * H, H), jnp.float32) * s(3 * H), 'gate_b1': jnp.zeros((H,), jnp.float32), 'gate_w2': jax.random.normal(ks[10], (H, H), jnp.float32) * s(H), 'gate_b2': jnp.zeros((H,), jnp.float32), 'out_w': jax.random.normal(ks[11], (H, H), jnp.float32) * s(H), 'out_b': jnp.zeros((H,), jnp.float32)}
        return inp
    _L1_xcond_all = _L1_xcond_setup()
    _L1_xcond_in = {k: v for k, v in _L1_xcond_all.items() if k in ('ln_gamma', 'ln_beta', 'Wq', 'Wk', 'Wv', 'router_W', 'router_b', 'e_w1', 'e_b1', 'e_w2', 'e_b2', 'gate_w1', 'gate_b1', 'gate_w2', 'gate_b2', 'out_w', 'out_b')}
    del _L1_xcond_all

    def _L2_xcond_setup():
        import jax, jax.numpy as jnp
        import numpy as np
        LN_EPS = 1e-06

        def _ln(x):
            mu = jnp.mean(x, axis=-1, keepdims=True)
            var = jnp.var(x, axis=-1, keepdims=True)
            return (x - mu) * jax.lax.rsqrt(var + LN_EPS)
        key = jax.random.key(seed)
        H, NH = (256, 16)
        B, N, S = (4, 256, 77)
        MLP = int(H * 4.0)
        ks = jax.random.split(key, 20)
        s = 1.0 / np.sqrt(H)
        return {'x': jax.random.normal(ks[0], (B, N, H), jnp.float32), 'c': jax.random.normal(ks[1], (B, H), jnp.float32), 'context': jax.random.normal(ks[2], (B, S, H), jnp.float32), 'W_mod': jax.random.normal(ks[3], (H, 6 * H), jnp.float32) * s, 'b_mod': jnp.zeros((6 * H,), jnp.float32), 'W_qkv': jax.random.normal(ks[4], (H, 3 * H), jnp.float32) * s, 'b_qkv': jnp.zeros((3 * H,), jnp.float32), 'W_proj': jax.random.normal(ks[5], (H, H), jnp.float32) * s, 'b_proj': jnp.zeros((H,), jnp.float32), 'W_qc': jax.random.normal(ks[6], (H, H), jnp.float32) * s, 'b_qc': jnp.zeros((H,), jnp.float32), 'W_kvc': jax.random.normal(ks[7], (H, 2 * H), jnp.float32) * s, 'b_kvc': jnp.zeros((2 * H,), jnp.float32), 'W_cproj': jax.random.normal(ks[8], (H, H), jnp.float32) * s, 'b_cproj': jnp.zeros((H,), jnp.float32), 'W_mlp1': jax.random.normal(ks[9], (H, MLP), jnp.float32) * s, 'b_mlp1': jnp.zeros((MLP,), jnp.float32), 'W_mlp2': jax.random.normal(ks[10], (MLP, H), jnp.float32) * (1.0 / np.sqrt(MLP)), 'b_mlp2': jnp.zeros((H,), jnp.float32)}
    _L2_xcond_all = _L2_xcond_setup()
    _L2_xcond_in = {k: v for k, v in _L2_xcond_all.items() if k in ('W_mod', 'b_mod', 'W_qkv', 'b_qkv', 'W_proj', 'b_proj', 'W_qc', 'b_qc', 'W_kvc', 'b_kvc', 'W_cproj', 'b_cproj', 'W_mlp1', 'b_mlp1', 'W_mlp2', 'b_mlp2')}
    del _L2_xcond_all

    def _L3_xcond_setup():
        import jax, jax.numpy as jnp
        import numpy as np
        C = 256
        H = 16
        D = C // H
        WIN = 128
        SHIFT = 64
        TOPK = 16
        HID = 1024
        EPS = 1e-06

        def _ln(x):
            x32 = x.astype(jnp.float32)
            m = x32.mean(-1, keepdims=True)
            v = jnp.mean((x32 - m) ** 2, axis=-1, keepdims=True)
            return ((x32 - m) * jax.lax.rsqrt(v + EPS)).astype(x.dtype)

        def _self_attn(h, w_qkv, b_qkv, w_so, b_so):
            B, L, _ = h.shape
            qkv = h @ w_qkv + b_qkv
            qkv = jnp.roll(qkv, -SHIFT, axis=1)
            nw = L // WIN
            qkv = qkv.reshape(B, nw, WIN, 3, H, D)
            q, k, v = (qkv[:, :, :, 0], qkv[:, :, :, 1], qkv[:, :, :, 2])
            scores = jnp.einsum('bnqhd,bnkhd->bnhqk', q, k) / jnp.sqrt(jnp.float32(D)).astype(h.dtype)
            attn = jax.nn.softmax(scores, axis=-1)
            o = jnp.einsum('bnhqk,bnkhd->bnqhd', attn, v).reshape(B, L, C)
            o = jnp.roll(o, SHIFT, axis=1)
            return o @ w_so + b_so

        def _topk_cross_attn(h, ctx, w_q, b_q, w_kv, b_kv, w_co, b_co):
            B, L, _ = h.shape
            Lc = ctx.shape[1]
            q = (h @ w_q + b_q).reshape(B, L, H, D)
            kv = (ctx @ w_kv + b_kv).reshape(B, Lc, 2, H, D)
            k, v = (kv[:, :, 0], kv[:, :, 1])
            scores = jnp.einsum('bqhd,bkhd->bhqk', q, k) / jnp.sqrt(jnp.float32(D)).astype(h.dtype)
            top_s, top_i = jax.lax.top_k(scores, TOPK)
            attn = jax.nn.softmax(top_s, axis=-1)
            v_bh = jnp.transpose(v, (0, 2, 1, 3))
            vg = jnp.take_along_axis(v_bh[:, :, None, :, :], top_i[..., None], axis=3)
            o = jnp.einsum('bhqk,bhqkd->bqhd', attn, vg).reshape(B, L, C)
            return o @ w_co + b_co

        def _swiglu(h, w_m1, b_m1, w_m2, b_m2):
            u = h @ w_m1 + b_m1
            a, b = (u[..., :HID], u[..., HID:])
            return jax.nn.silu(a) * b @ w_m2 + b_m2
        key = jax.random.key(seed)
        ks = jax.random.split(key, 24)
        s = 0.02
        inp = {'x': jax.random.normal(ks[0], (2, 1024, C), jnp.float32), 'mod': jax.random.normal(ks[1], (2, C), jnp.float32), 'context': jax.random.normal(ks[2], (2, 256, C), jnp.float32), 'w_ada': jax.random.normal(ks[3], (C, 9 * C), jnp.float32) * s, 'b_ada': jnp.zeros((9 * C,), jnp.float32), 'w_qkv': jax.random.normal(ks[4], (C, 3 * C), jnp.float32) * s, 'b_qkv': jnp.zeros((3 * C,), jnp.float32), 'w_so': jax.random.normal(ks[5], (C, C), jnp.float32) * s, 'b_so': jnp.zeros((C,), jnp.float32), 'w_q': jax.random.normal(ks[6], (C, C), jnp.float32) * s, 'b_q': jnp.zeros((C,), jnp.float32), 'w_kv': jax.random.normal(ks[7], (C, 2 * C), jnp.float32) * s, 'b_kv': jnp.zeros((2 * C,), jnp.float32), 'w_co': jax.random.normal(ks[8], (C, C), jnp.float32) * s, 'b_co': jnp.zeros((C,), jnp.float32), 'w_m1': jax.random.normal(ks[9], (C, 2 * HID), jnp.float32) * s, 'b_m1': jnp.zeros((2 * HID,), jnp.float32), 'w_m2': jax.random.normal(ks[10], (HID, C), jnp.float32) * s, 'b_m2': jnp.zeros((C,), jnp.float32)}
        return inp
    _L3_xcond_all = _L3_xcond_setup()
    _L3_xcond_in = {k: v for k, v in _L3_xcond_all.items() if k in ('w_ada', 'b_ada', 'w_qkv', 'b_qkv', 'w_so', 'b_so', 'w_q', 'b_q', 'w_kv', 'b_kv', 'w_co', 'b_co', 'w_m1', 'b_m1', 'w_m2', 'b_m2')}
    del _L3_xcond_all
    return {'x': x, 'cond_1024': cond_1024, 'ctx_1024': ctx_1024, 'L0_xcond_ln1_w': _L0_xcond_in['ln1_w'], 'L0_xcond_ln1_b': _L0_xcond_in['ln1_b'], 'L0_xcond_ln2_w': _L0_xcond_in['ln2_w'], 'L0_xcond_ln2_b': _L0_xcond_in['ln2_b'], 'L0_xcond_ln3_w': _L0_xcond_in['ln3_w'], 'L0_xcond_ln3_b': _L0_xcond_in['ln3_b'], 'L0_xcond_qkv_w': _L0_xcond_in['qkv_w'], 'L0_xcond_sa_out_w': _L0_xcond_in['sa_out_w'], 'L0_xcond_q_w': _L0_xcond_in['q_w'], 'L0_xcond_k_w': _L0_xcond_in['k_w'], 'L0_xcond_v_w': _L0_xcond_in['v_w'], 'L0_xcond_ca_out_w': _L0_xcond_in['ca_out_w'], 'L0_xcond_ffn_w1': _L0_xcond_in['ffn_w1'], 'L0_xcond_ffn_b1': _L0_xcond_in['ffn_b1'], 'L0_xcond_ffn_w2': _L0_xcond_in['ffn_w2'], 'L0_xcond_ffn_b2': _L0_xcond_in['ffn_b2'], 'L1_xcond_ln_gamma': _L1_xcond_in['ln_gamma'], 'L1_xcond_ln_beta': _L1_xcond_in['ln_beta'], 'L1_xcond_Wq': _L1_xcond_in['Wq'], 'L1_xcond_Wk': _L1_xcond_in['Wk'], 'L1_xcond_Wv': _L1_xcond_in['Wv'], 'L1_xcond_router_W': _L1_xcond_in['router_W'], 'L1_xcond_router_b': _L1_xcond_in['router_b'], 'L1_xcond_e_w1': _L1_xcond_in['e_w1'], 'L1_xcond_e_b1': _L1_xcond_in['e_b1'], 'L1_xcond_e_w2': _L1_xcond_in['e_w2'], 'L1_xcond_e_b2': _L1_xcond_in['e_b2'], 'L1_xcond_gate_w1': _L1_xcond_in['gate_w1'], 'L1_xcond_gate_b1': _L1_xcond_in['gate_b1'], 'L1_xcond_gate_w2': _L1_xcond_in['gate_w2'], 'L1_xcond_gate_b2': _L1_xcond_in['gate_b2'], 'L1_xcond_out_w': _L1_xcond_in['out_w'], 'L1_xcond_out_b': _L1_xcond_in['out_b'], 'L2_xcond_W_mod': _L2_xcond_in['W_mod'], 'L2_xcond_b_mod': _L2_xcond_in['b_mod'], 'L2_xcond_W_qkv': _L2_xcond_in['W_qkv'], 'L2_xcond_b_qkv': _L2_xcond_in['b_qkv'], 'L2_xcond_W_proj': _L2_xcond_in['W_proj'], 'L2_xcond_b_proj': _L2_xcond_in['b_proj'], 'L2_xcond_W_qc': _L2_xcond_in['W_qc'], 'L2_xcond_b_qc': _L2_xcond_in['b_qc'], 'L2_xcond_W_kvc': _L2_xcond_in['W_kvc'], 'L2_xcond_b_kvc': _L2_xcond_in['b_kvc'], 'L2_xcond_W_cproj': _L2_xcond_in['W_cproj'], 'L2_xcond_b_cproj': _L2_xcond_in['b_cproj'], 'L2_xcond_W_mlp1': _L2_xcond_in['W_mlp1'], 'L2_xcond_b_mlp1': _L2_xcond_in['b_mlp1'], 'L2_xcond_W_mlp2': _L2_xcond_in['W_mlp2'], 'L2_xcond_b_mlp2': _L2_xcond_in['b_mlp2'], 'L3_xcond_w_ada': _L3_xcond_in['w_ada'], 'L3_xcond_b_ada': _L3_xcond_in['b_ada'], 'L3_xcond_w_qkv': _L3_xcond_in['w_qkv'], 'L3_xcond_b_qkv': _L3_xcond_in['b_qkv'], 'L3_xcond_w_so': _L3_xcond_in['w_so'], 'L3_xcond_b_so': _L3_xcond_in['b_so'], 'L3_xcond_w_q': _L3_xcond_in['w_q'], 'L3_xcond_b_q': _L3_xcond_in['b_q'], 'L3_xcond_w_kv': _L3_xcond_in['w_kv'], 'L3_xcond_b_kv': _L3_xcond_in['b_kv'], 'L3_xcond_w_co': _L3_xcond_in['w_co'], 'L3_xcond_b_co': _L3_xcond_in['b_co'], 'L3_xcond_w_m1': _L3_xcond_in['w_m1'], 'L3_xcond_b_m1': _L3_xcond_in['b_m1'], 'L3_xcond_w_m2': _L3_xcond_in['w_m2'], 'L3_xcond_b_m2': _L3_xcond_in['b_m2']}

def reference(x, cond_1024, ctx_1024, L0_xcond_ln1_w, L0_xcond_ln1_b, L0_xcond_ln2_w, L0_xcond_ln2_b, L0_xcond_ln3_w, L0_xcond_ln3_b, L0_xcond_qkv_w, L0_xcond_sa_out_w, L0_xcond_q_w, L0_xcond_k_w, L0_xcond_v_w, L0_xcond_ca_out_w, L0_xcond_ffn_w1, L0_xcond_ffn_b1, L0_xcond_ffn_w2, L0_xcond_ffn_b2, L1_xcond_ln_gamma, L1_xcond_ln_beta, L1_xcond_Wq, L1_xcond_Wk, L1_xcond_Wv, L1_xcond_router_W, L1_xcond_router_b, L1_xcond_e_w1, L1_xcond_e_b1, L1_xcond_e_w2, L1_xcond_e_b2, L1_xcond_gate_w1, L1_xcond_gate_b1, L1_xcond_gate_w2, L1_xcond_gate_b2, L1_xcond_out_w, L1_xcond_out_b, L2_xcond_W_mod, L2_xcond_b_mod, L2_xcond_W_qkv, L2_xcond_b_qkv, L2_xcond_W_proj, L2_xcond_b_proj, L2_xcond_W_qc, L2_xcond_b_qc, L2_xcond_W_kvc, L2_xcond_b_kvc, L2_xcond_W_cproj, L2_xcond_b_cproj, L2_xcond_W_mlp1, L2_xcond_b_mlp1, L2_xcond_W_mlp2, L2_xcond_b_mlp2, L3_xcond_w_ada, L3_xcond_b_ada, L3_xcond_w_qkv, L3_xcond_b_qkv, L3_xcond_w_so, L3_xcond_b_so, L3_xcond_w_q, L3_xcond_b_q, L3_xcond_w_kv, L3_xcond_b_kv, L3_xcond_w_co, L3_xcond_b_co, L3_xcond_w_m1, L3_xcond_b_m1, L3_xcond_w_m2, L3_xcond_b_m2):
    import jax
    import jax.numpy as jnp

    def _L0_xcond_ref(x, noise_emb, context, ln1_w, ln1_b, ln2_w, ln2_b, ln3_w, ln3_b, qkv_w, sa_out_w, q_w, k_w, v_w, ca_out_w, ffn_w1, ffn_b1, ffn_w2, ffn_b2):
        import jax, jax.numpy as jnp
        import numpy as np
        import math
        D_MODEL = 256
        N_HEADS = 16
        HEAD_DIM = D_MODEL // N_HEADS
        D_FF = 1024
        EPS = 1e-05
        ROPE_BASE = 10000.0

        def _rope(t):
            L, Dh = (t.shape[1], t.shape[-1])
            half = Dh // 2
            inv_freq = 1.0 / ROPE_BASE ** (jnp.arange(half, dtype=t.dtype) / half)
            ang = jnp.arange(L, dtype=t.dtype)[:, None] * inv_freq[None, :]
            cos = jnp.cos(ang)[None, :, None, :]
            sin = jnp.sin(ang)[None, :, None, :]
            t1, t2 = (t[..., :half], t[..., half:])
            return jnp.concatenate([t1 * cos - t2 * sin, t2 * cos + t1 * sin], axis=-1)

        def _adaln(x, emb, w, b):
            e = emb[:, 0, :]
            gb = e @ w.T + b
            gamma, beta = jnp.split(gb, 2, axis=-1)
            mu = x.mean(-1, keepdims=True)
            var = x.var(-1, keepdims=True)
            xn = (x - mu) * jax.lax.rsqrt(var + EPS)
            return xn * (1.0 + gamma[:, None, :]) + beta[:, None, :]

        def _attn(q, k, v):
            scale = 1.0 / math.sqrt(HEAD_DIM)
            scores = jnp.einsum('bqhd,bkhd->bhqk', q, k) * scale
            w = jax.nn.softmax(scores, axis=-1)
            out = jnp.einsum('bhqk,bkhd->bqhd', w, v)
            B, Lq = (out.shape[0], out.shape[1])
            return out.reshape(B, Lq, D_MODEL)
        B, L, D = x.shape
        L_ctx = context.shape[1]
        res = x
        xn = _adaln(x, noise_emb, ln1_w, ln1_b)
        qkv = xn @ qkv_w.T
        q, k, v = jnp.split(qkv, 3, axis=-1)
        q = _rope(q.reshape(B, L, N_HEADS, HEAD_DIM))
        k = _rope(k.reshape(B, L, N_HEADS, HEAD_DIM))
        v = v.reshape(B, L, N_HEADS, HEAD_DIM)
        sa = _attn(q, k, v) @ sa_out_w.T
        x = res + sa
        res = x
        xn = _adaln(x, noise_emb, ln2_w, ln2_b)
        q = _rope((xn @ q_w.T).reshape(B, L, N_HEADS, HEAD_DIM))
        k = _rope((context @ k_w.T).reshape(B, L_ctx, N_HEADS, HEAD_DIM))
        v = (context @ v_w.T).reshape(B, L_ctx, N_HEADS, HEAD_DIM)
        ca = _attn(q, k, v) @ ca_out_w.T
        x = res + ca
        res = x
        xn = _adaln(x, noise_emb, ln3_w, ln3_b)
        h = jax.nn.gelu(xn @ ffn_w1.T + ffn_b1, approximate=False)
        x = res + (h @ ffn_w2.T + ffn_b2)
        return x

    def _L1_xcond_ref(mix_hidden_states, global_anchor, prototype_bank, ln_gamma, ln_beta, Wq, Wk, Wv, router_W, router_b, e_w1, e_b1, e_w2, e_b2, gate_w1, gate_b1, gate_w2, gate_b2, out_w, out_b):
        import jax, jax.numpy as jnp
        import numpy as np
        H = 256
        RH = 2 * H
        E = 3
        B, T, P = (8, 512, 64)
        LN_EPS = 1e-05

        def _layer_norm(x, gamma, beta):
            mu = jnp.mean(x, axis=-1, keepdims=True)
            var = jnp.mean(jnp.square(x - mu), axis=-1, keepdims=True)
            return (x - mu) * jax.lax.rsqrt(var + LN_EPS) * gamma + beta
        x = mix_hidden_states
        nx = _layer_norm(x, ln_gamma, ln_beta)
        q = nx @ Wq
        k = prototype_bank @ Wk
        v = prototype_bank @ Wv
        scores = jnp.einsum('bth,bph->btp', q, k) * H ** (-0.5)
        weights = jax.nn.softmax(scores, axis=-1)
        evidence = jnp.einsum('btp,bph->bth', weights, v)
        anchor = jnp.broadcast_to(global_anchor[:, None, :], nx.shape)
        combined = jnp.concatenate([nx, evidence, anchor], axis=-1)
        router_logits = combined @ router_W + router_b
        router_probs = jax.nn.softmax(router_logits, axis=-1)
        h = jax.nn.silu(jnp.einsum('btc,ecr->bter', combined, e_w1) + e_b1)
        expert_out = jnp.einsum('bter,erh->bteh', h, e_w2) + e_b2
        routed = jnp.sum(expert_out * router_probs[..., None], axis=-2)
        g = jax.nn.sigmoid(jax.nn.silu(combined @ gate_w1 + gate_b1) @ gate_w2 + gate_b2)
        refined_delta = g * (routed @ out_w + out_b)
        return x + refined_delta

    def _L2_xcond_ref(x, c, context, W_mod, b_mod, W_qkv, b_qkv, W_proj, b_proj, W_qc, b_qc, W_kvc, b_kvc, W_cproj, b_cproj, W_mlp1, b_mlp1, W_mlp2, b_mlp2):
        import jax, jax.numpy as jnp
        import numpy as np
        LN_EPS = 1e-06

        def _ln(x):
            mu = jnp.mean(x, axis=-1, keepdims=True)
            var = jnp.var(x, axis=-1, keepdims=True)
            return (x - mu) * jax.lax.rsqrt(var + LN_EPS)
        B, N, H = x.shape
        NH = 16
        hd = H // NH
        scale = hd ** (-0.5)
        c_proj = jax.nn.silu(c) @ W_mod + b_mod
        shift_a, scale_a, gate_a, shift_m, scale_m, gate_m = jnp.split(c_proj, 6, axis=-1)

        def modulate(t, shift, sc):
            return t * (1 + sc[:, None]) + shift[:, None]
        x_norm = modulate(_ln(x), shift_a, scale_a)
        qkv = x_norm @ W_qkv + b_qkv
        q, k, v = jnp.split(qkv, 3, axis=-1)
        q = q.reshape(B, N, NH, hd).transpose(0, 2, 1, 3)
        k = k.reshape(B, N, NH, hd).transpose(0, 2, 1, 3)
        v = v.reshape(B, N, NH, hd).transpose(0, 2, 1, 3)
        attn_w = jax.nn.softmax(jnp.einsum('bhqd,bhkd->bhqk', q, k) * scale, axis=-1)
        attn_out = jnp.einsum('bhqk,bhkd->bhqd', attn_w, v)
        attn_out = attn_out.transpose(0, 2, 1, 3).reshape(B, N, H)
        attn_out = attn_out @ W_proj + b_proj
        x = x + gate_a[:, None] * attn_out
        S = context.shape[1]
        q_c = _ln(x) @ W_qc + b_qc
        kv_c = _ln(context) @ W_kvc + b_kvc
        k_c, v_c = jnp.split(kv_c, 2, axis=-1)
        q_c = q_c.reshape(B, N, NH, hd).transpose(0, 2, 1, 3)
        k_c = k_c.reshape(B, S, NH, hd).transpose(0, 2, 1, 3)
        v_c = v_c.reshape(B, S, NH, hd).transpose(0, 2, 1, 3)
        c_attn_w = jax.nn.softmax(jnp.einsum('bhqd,bhsd->bhqs', q_c, k_c) * scale, axis=-1)
        c_attn_out = jnp.einsum('bhqs,bhsd->bhqd', c_attn_w, v_c)
        c_attn_out = c_attn_out.transpose(0, 2, 1, 3).reshape(B, N, H)
        c_attn_out = c_attn_out @ W_cproj + b_cproj
        x = x + c_attn_out
        x_norm2 = modulate(_ln(x), shift_m, scale_m)
        h = jax.nn.gelu(x_norm2 @ W_mlp1 + b_mlp1)
        h = h @ W_mlp2 + b_mlp2
        x = x + gate_m[:, None] * h
        return x

    def _L3_xcond_ref(x, mod, context, w_ada, b_ada, w_qkv, b_qkv, w_so, b_so, w_q, b_q, w_kv, b_kv, w_co, b_co, w_m1, b_m1, w_m2, b_m2):
        import jax, jax.numpy as jnp
        import numpy as np
        C = 256
        H = 16
        D = C // H
        WIN = 128
        SHIFT = 64
        TOPK = 16
        HID = 1024
        EPS = 1e-06

        def _ln(x):
            x32 = x.astype(jnp.float32)
            m = x32.mean(-1, keepdims=True)
            v = jnp.mean((x32 - m) ** 2, axis=-1, keepdims=True)
            return ((x32 - m) * jax.lax.rsqrt(v + EPS)).astype(x.dtype)

        def _self_attn(h, w_qkv, b_qkv, w_so, b_so):
            B, L, _ = h.shape
            qkv = h @ w_qkv + b_qkv
            qkv = jnp.roll(qkv, -SHIFT, axis=1)
            nw = L // WIN
            qkv = qkv.reshape(B, nw, WIN, 3, H, D)
            q, k, v = (qkv[:, :, :, 0], qkv[:, :, :, 1], qkv[:, :, :, 2])
            scores = jnp.einsum('bnqhd,bnkhd->bnhqk', q, k) / jnp.sqrt(jnp.float32(D)).astype(h.dtype)
            attn = jax.nn.softmax(scores, axis=-1)
            o = jnp.einsum('bnhqk,bnkhd->bnqhd', attn, v).reshape(B, L, C)
            o = jnp.roll(o, SHIFT, axis=1)
            return o @ w_so + b_so

        def _topk_cross_attn(h, ctx, w_q, b_q, w_kv, b_kv, w_co, b_co):
            B, L, _ = h.shape
            Lc = ctx.shape[1]
            q = (h @ w_q + b_q).reshape(B, L, H, D)
            kv = (ctx @ w_kv + b_kv).reshape(B, Lc, 2, H, D)
            k, v = (kv[:, :, 0], kv[:, :, 1])
            scores = jnp.einsum('bqhd,bkhd->bhqk', q, k) / jnp.sqrt(jnp.float32(D)).astype(h.dtype)
            top_s, top_i = jax.lax.top_k(scores, TOPK)
            attn = jax.nn.softmax(top_s, axis=-1)
            v_bh = jnp.transpose(v, (0, 2, 1, 3))
            vg = jnp.take_along_axis(v_bh[:, :, None, :, :], top_i[..., None], axis=3)
            o = jnp.einsum('bhqk,bhqkd->bqhd', attn, vg).reshape(B, L, C)
            return o @ w_co + b_co

        def _swiglu(h, w_m1, b_m1, w_m2, b_m2):
            u = h @ w_m1 + b_m1
            a, b = (u[..., :HID], u[..., HID:])
            return jax.nn.silu(a) * b @ w_m2 + b_m2
        m = jax.nn.silu(mod) @ w_ada + b_ada
        sh_msa, sc_msa, g_msa, sh_mca, sc_mca, g_mca, sh_mlp, sc_mlp, g_mlp = [m[:, i * C:(i + 1) * C][:, None, :] for i in range(9)]
        h = _ln(x) * (1 + sc_msa) + sh_msa
        h = _self_attn(h, w_qkv, b_qkv, w_so, b_so)
        x = x + h * g_msa
        h = _ln(x) * (1 + sc_mca) + sh_mca
        h = _topk_cross_attn(h, context, w_q, b_q, w_kv, b_kv, w_co, b_co)
        x = x + h * g_mca
        h = _ln(x) * (1 + sc_mlp) + sh_mlp
        h = _swiglu(h, w_m1, b_m1, w_m2, b_m2)
        x = x + h * g_mlp
        return x
    x = _L0_xcond_ref(x, cond_1024[:, None, :], ctx_1024, L0_xcond_ln1_w, L0_xcond_ln1_b, L0_xcond_ln2_w, L0_xcond_ln2_b, L0_xcond_ln3_w, L0_xcond_ln3_b, L0_xcond_qkv_w, L0_xcond_sa_out_w, L0_xcond_q_w, L0_xcond_k_w, L0_xcond_v_w, L0_xcond_ca_out_w, L0_xcond_ffn_w1, L0_xcond_ffn_b1, L0_xcond_ffn_w2, L0_xcond_ffn_b2)
    x = _L1_xcond_ref(x, cond_1024, ctx_1024, L1_xcond_ln_gamma, L1_xcond_ln_beta, L1_xcond_Wq, L1_xcond_Wk, L1_xcond_Wv, L1_xcond_router_W, L1_xcond_router_b, L1_xcond_e_w1, L1_xcond_e_b1, L1_xcond_e_w2, L1_xcond_e_b2, L1_xcond_gate_w1, L1_xcond_gate_b1, L1_xcond_gate_w2, L1_xcond_gate_b2, L1_xcond_out_w, L1_xcond_out_b)
    x = _L2_xcond_ref(x, cond_1024, ctx_1024, L2_xcond_W_mod, L2_xcond_b_mod, L2_xcond_W_qkv, L2_xcond_b_qkv, L2_xcond_W_proj, L2_xcond_b_proj, L2_xcond_W_qc, L2_xcond_b_qc, L2_xcond_W_kvc, L2_xcond_b_kvc, L2_xcond_W_cproj, L2_xcond_b_cproj, L2_xcond_W_mlp1, L2_xcond_b_mlp1, L2_xcond_W_mlp2, L2_xcond_b_mlp2)
    x = _L3_xcond_ref(x, cond_1024, ctx_1024, L3_xcond_w_ada, L3_xcond_b_ada, L3_xcond_w_qkv, L3_xcond_b_qkv, L3_xcond_w_so, L3_xcond_b_so, L3_xcond_w_q, L3_xcond_b_q, L3_xcond_w_kv, L3_xcond_b_kv, L3_xcond_w_co, L3_xcond_b_co, L3_xcond_w_m1, L3_xcond_b_m1, L3_xcond_w_m2, L3_xcond_b_m2)
    return x

_drawn_inputs = setup_inputs


def setup_inputs(seed=0):
    import zlib

    import numpy as np

    out = dict(_drawn_inputs(seed))
    spreads = {'L1_xcond_ln_gamma': (1.0, 0.6),
     'L1_xcond_ln_beta': (0.0, 0.583),
     'L1_xcond_router_b': (0.0, 0.374),
     'L1_xcond_e_b1': (0.0, 0.439),
     'L1_xcond_e_b2': (0.0, 0.1),
     'L1_xcond_gate_b1': (0.0, 0.8),
     'L1_xcond_gate_b2': (0.0, 0.8),
     'L1_xcond_out_b': (0.0, 0.1),
     'L2_xcond_b_mod': (0.0, 0.1),
     'L2_xcond_b_qkv': (0.0, 0.1),
     'L2_xcond_b_proj': (0.0, 0.1),
     'L2_xcond_b_qc': (0.0, 0.637),
     'L2_xcond_b_kvc': (0.0, 0.1),
     'L2_xcond_b_cproj': (0.0, 0.1),
     'L2_xcond_b_mlp1': (0.0, 0.1),
     'L2_xcond_b_mlp2': (0.0, 0.1),
     'L3_xcond_b_ada': (0.0, 0.488),
     'L3_xcond_b_qkv': (0.0, 0.8),
     'L3_xcond_b_so': (0.0, 0.478),
     'L3_xcond_b_q': (0.0, 0.8),
     'L3_xcond_b_kv': (0.0, 0.8),
     'L3_xcond_b_co': (0.0, 0.457),
     'L3_xcond_b_m1': (0.0, 0.8),
     'L3_xcond_b_m2': (0.0, 2.0)}
    factors = {'L0_xcond_ln1_b': 22.675,
     'L0_xcond_ln2_w': 8.0,
     'L0_xcond_ln2_b': 8.0,
     'L0_xcond_ln3_b': 8.0,
     'L0_xcond_q_w': 8.0,
     'L0_xcond_k_w': 8.0,
     'L0_xcond_ffn_b1': 8.0,
     'L0_xcond_ffn_b2': 2.734,
     'L3_xcond_w_qkv': 5.289,
     'L3_xcond_w_so': 4.805,
     'L3_xcond_w_q': 5.698,
     'L3_xcond_w_kv': 4.343,
     'L3_xcond_w_co': 4.0,
     'L3_xcond_w_m1': 8.0,
     'L3_xcond_w_m2': 8.0}
    for name, (base, spread) in spreads.items():
        noise = np.random.default_rng([zlib.crc32(name.encode()), seed]).standard_normal(out[name].shape)
        drawn = base * np.exp(spread * noise) if base else spread * noise
        out[name] = jnp.asarray(drawn.astype(out[name].dtype))
    for name, factor in factors.items():
        out[name] = (out[name] * factor).astype(out[name].dtype)
    return out
```

```python
import numpy as np
import concourse.bass as bass
from concourse import mybir
from contextlib import ExitStack

F32 = mybir.dt.float32
BF16 = mybir.dt.bfloat16
ACT = mybir.ActivationFunctionType
ALU = mybir.AluOpType
AX = mybir.AxisListType

P = 128
B = 4
N = 512
C = 256
KC = C // P
NT = N // P
H = 16
D = C // H
HID = 1024
NH = HID // P
E = 3
RH = 2 * C
NR = RH // P
ROLL = 64
STACK = 6 * D
QSC = D ** -0.5
QSC1 = C ** -0.5
LOWEST = -3.0e38
NS = 3
LAG = 3
U = KC * C

WCOLS = [dict(q=0, k=U, v=2 * U, o=3 * U, q2=4 * U, k2=5 * U, v2=6 * U, o2=7 * U, w1=8 * U, w2=12 * U, end=16 * U)] * 4
WCOLS = [dict(w) for w in WCOLS]
WCOLS[1] = dict(q=0, k=U, v=2 * U, e1=3 * U, e2=15 * U, g1=21 * U, g2=23 * U, o=24 * U, r=25 * U, end=25 * U + 4 * E)
WCOLS[3] = dict(WCOLS[0], w2=16 * U, end=20 * U)
WMAX = max(w["end"] for w in WCOLS)
MOD = [12, 14, 8, 12]
GATE = [0, E, 2 * C, 3 * C]
BCOLS = [dict(m2=0, end=C),
         dict(e2=0, g2=E * C, o=(E + 1) * C, gate=(E + 2) * C, end=(E + 2) * C + E),
         dict(qkv=0, qkv2=3 * C, o=6 * C, o2=7 * C, m2=8 * C, gate=9 * C, end=11 * C),
         dict(qkv=0, qkv2=3 * C, o=6 * C, o2=7 * C, m2=8 * C, gate=9 * C, end=12 * C)]
BMAX = max(w["end"] for w in BCOLS)
SCOLS = [dict(mod=0, m1=12, end=20), dict(mod=0, ln=14, end=18), dict(mod=0, m1=8, end=16), dict(mod=0, m1=12, end=28)]
SMAX = max(w["end"] for w in SCOLS)
LAYERS = 4
EPS = [1e-5, 1e-5, 1e-6, 1e-6]


class Progress:

    def __init__(self, handle, per, pre=(0, 0, 0, 0), start=0, unit=1):
        self.handle, self.per, self.pre, self.start, self.unit = handle, per, pre, start, unit

    def base(self, L):
        return self.start + sum(self.pre[i] + B * self.per[i] for i in range(L))

    def before(self, L, k):
        return (self.base(L) + k) * self.unit

    def at(self, L, b, k):
        return b * (self.per[L] * self.unit) + (self.base(L) + self.pre[L] + k) * self.unit


class Steps:

    def __init__(self, eng, handle):
        self.eng, self.handle, self.n = eng, handle, 0

    def did(self, ins):
        self.n += 1
        ins.then_inc(self.handle, 1)

    def wait(self):
        if self.n:
            self.eng.wait_ge(self.handle, self.n)

    def reset(self, waited=False):
        if self.n:
            if not waited:
                self.eng.wait_ge(self.handle, self.n)
            self.eng.sem_clear(self.handle)
            self.n = 0


def four_layers(nc, ins, out):
    ctx = ExitStack()
    with ctx:
        def sb(name, shape, dt=F32):
            return ctx.enter_context(nc.sbuf_tensor(name, shape, dt))

        def sem(name):
            return ctx.enter_context(nc.semaphore(name))

        x_all = sb("x_all", [P, B * NT, C])
        W = sb("W", [P, WMAX])
        BB = sb("BB", [P, BMAX])
        SV = sb("SV", [P, SMAX])
        mod = sb("mod", [P, B, max(MOD)])
        modc = sb("modc", [P, max(MOD)])
        gates = sb("gates", [P, B, max(GATE)])
        stk = sb("stk", [P, 2 * H * N // 2])
        qkst = stk[:, :].bitcast(BF16).rearrange("p (h n) -> p h n", h=2 * H)
        qk_tok = sb("qk_tok", [P, 2, 2 * H, STACK], BF16)
        tmp = sb("tmp", [P, 9 * C])
        qkf, ra, rb = (tmp[:, i * 2 * C:(i + 1) * 2 * C] for i in range(3))
        parts = tmp[:, 6 * C:9 * C].bitcast(BF16).rearrange("p (s n) -> p s n", s=3)
        rest = tmp[:, 0:8 * C].rearrange("p (a i n) -> p a i n", a=2, i=2)
        vz = sb("vz", [P, NT, H, 32])
        xn = sb("xn", [P, NT, C])
        xnT = sb("xnT", [P, KC, N])
        cx = sb("cx", [P, KC * N])
        cxT = cx[:, :].rearrange("p (k n) -> p k n", k=KC)
        cxt = cx[:, :].rearrange("p (t c) -> p t c", t=NT)
        atT = sb("atT", [P, KC, N])
        probs = sb("probs", [P, 2, N])
        probs2 = sb("probs2", [P, 2, N])
        cnT = probs2[:, :, :]
        pn = sb("pn", [P, 3, N])
        pT = sb("pT", [P, 2, NT, N])
        hT = pT[:, :, :, :].rearrange("p a t n -> p (a t) n")
        condB = hT[:, 0:2, :].rearrange("p k (b n) -> p k b n", b=B)
        top = sb("top", [P, 4, 16])
        nmax = sb("nmax", [P, H * NT])
        ssum = sb("ssum", [P, H * NT])
        rsum = sb("rsum", [P, H * NT])
        st = sb("st", [P, NT, 6])
        mv = sb("mv", [P, NT, 2])
        rstd = sb("rstd", [P, 2, NT])
        mhalf = sb("mhalf", [P, NT])
        sil = probs[:, :, :]
        res = sb("res", [P, 2, C])
        rlog = sb("rlog", [P, NT, 4])
        rpr = sb("rpr", [P, NT, 4])
        rsm = sb("rsm", [P, 2, NT])
        condT = sb("condT", [P, KC, B])
        condS = sb("condS", [P, KC, B])
        rope = sb("rope", [P, 2, NT, 2, D])
        ident = sb("ident", [P, P])
        identh = sb("identh", [P, P], BF16)
        def part(i):
            return stk[:, i * KC * N:(i + 1) * KC * N]
        q1T = part(0).rearrange("p (k n) -> p k n", k=KC)
        k1T = part(1).rearrange("p (k n) -> p k n", k=KC)
        v1 = part(2).rearrange("p (t c) -> p t c", t=NT)
        routed = part(3).rearrange("p (t c) -> p t c", t=NT)
        roT = part(4).rearrange("p (k n) -> p k n", k=KC)
        g1 = part(5).rearrange("p (t c) -> p t c", t=NT)

        def bank(name):
            return ctx.enter_context(nc.psum_tensor(name, [P, N], F32))
        S = [bank(f"S{i}") for i in range(NS)]
        T = [bank(f"T{i}") for i in range(2)]
        Th = [t[:, :].bitcast(BF16) for t in T]
        A = [bank(f"A{i}") for i in range(2)]
        O = bank("O")
        OB = [O, A[0]]

        def prog(name, per, pre=(0, 0, 0, 0), start=0, unit=1):
            return Progress(sem(name), per, pre, start, unit)
        tiles = [2 * 64, 4, 2 * 64, H + 64]
        heads = [2 * H, KC, 2 * H, 2 * H]
        dve_ev = [64, 2, 64, H // 2]
        act_ev = [64, 2, 64, H // 2 + 64]
        lns = [3, 1, 4, 3]
        qkvs = [2, 0, 2, 2]
        loaded = prog("loaded", [0] * 4, [4] * 4, start=0, unit=16)
        first_in = sem("first_in")
        consts = sem("consts")
        cond_ready = sem("cond_ready")
        condB_ready = prog("condB_ready", [0] * 4, [1 if g else 0 for g in GATE])
        prep_psum = prog("prep_psum", [0] * 4, [1 + (B if g else 0) for g in GATE])
        prep_read = prog("prep_read", [0] * 4, [1 + (B if g else 0) for g in GATE])
        modc_ready = prog("modc_ready", [1] * 4)
        cx_loaded = prog("cx_loaded", [1] * 4, unit=16)
        cx_used = prog("cx_used", [1] * 4, start=1)
        stats_ready = prog("stats_ready", [NT * n for n in lns])
        rstd_ready = prog("rstd_ready", lns)
        xn_ready = prog("xn_ready", [NT * n for n in lns])
        xT_psum = prog("xT_psum", lns)
        xT_dve = prog("xT_dve", lns)
        xT_act = prog("xT_act", lns)
        qk_psum = prog("qk_psum", [NT * n for n in qkvs])
        qk_read = prog("qk_read", [NT * n for n in qkvs])
        v_psum = prog("v_psum", [NT, NT, NT, NT] and [NT * 2, NT, NT * 2, NT * 2])
        v_ready = prog("v_ready", [NT * 2, NT, NT * 2, NT * 2])
        stack_ready = prog("stack_ready", [NT * n for n in qkvs])
        stackT_psum = prog("stackT_psum", [4 * NT * n for n in qkvs])
        stackT_ready = prog("stackT_ready", [4 * NT * n for n in qkvs])
        scores_ready = prog("scores_ready", tiles)
        max_ready = prog("max_ready", tiles)
        exp_ready = prog("exp_ready", tiles)
        rest_ready = prog("rest_ready", [0, 0, 0, 64])
        rsum_ready = prog("rsum_ready", tiles)
        pn_ready = prog("pn_ready", tiles)
        pT_psum = prog("pT_psum", tiles)
        pT_dve = prog("pT_dve", dve_ev)
        pT_act = prog("pT_act", act_ev)
        pv_done = prog("pv_done", heads)
        atT_ready = prog("atT_ready", [4, 2, 4, 4])
        out_psum = prog("out_psum", [2 * NT, NT, 2 * NT, 2 * NT])
        out_read = prog("out_read", [2 * NT, NT, 2 * NT, 2 * NT])
        hid_psum = prog("hid_psum", [NH, 0, NH, 2 * NH])
        hid_ready = prog("hid_ready", [NH, 0, NH, NH])
        sil_ready = prog("sil_ready", [0, 0, 0, NH])
        ffn_psum = prog("ffn_psum", [NT, 0, NT, NT])
        ffn_read = prog("ffn_read", [NT, 0, NT, NT])
        qk1_psum = prog("qk1_psum", [0, 2 * KC, 0, 0])
        qk1_ready = prog("qk1_ready", [0, 2 * KC, 0, 0])
        rl_psum = prog("rl_psum", [0, 1, 0, 0])
        rl_shift = prog("rl_shift", [0, 1, 0, 0])
        rl_exp = prog("rl_exp", [0, 1, 0, 0])
        eh_psum = prog("eh_psum", [0, E * NR + KC, 0, 0])
        eh_ready = prog("eh_ready", [0, E * NR + KC, 0, 0])
        eo_psum = prog("eo_psum", [0, (E + 1) * NT, 0, 0])
        eo_read = prog("eo_read", [0, (E + 1) * NT, 0, 0])
        gate_ready = prog("gate_ready", [0, NT, 0, 0])
        roT_psum = prog("roT_psum", [0, 1, 0, 0])
        roT_ready = prog("roT_ready", [0, 1, 0, 0])
        x_done = prog("x_done", [1] * 4)
        stored = sem("stored")
        passed = sem("passed")
        dve_step, act_step, pool_step = sem("dve_step"), sem("act_step"), sem("pool_step")

        block = ctx.enter_context(nc.Block())

        def w(L, name, k, lo=0, hi=C, width=C):
            o = WCOLS[L][name] + k * width
            return W[:, o + lo:o + hi]

        def n_ev(L, variant, j):
            return variant != "topk" and j % 2 == 0

        def evs(variant, j):
            return (0, j) if variant == "topk" else ((j + 1) // 2, j // 2)

        ATT = [
            [("soft", 0, 0, 0, 0, 0), ("soft", 64, H, 32, 32, 1)],
            [("one", 0, 0, 0, 0, 0)],
            [("soft", 0, 0, 0, 0, 0), ("soft", 64, H, 32, 32, 1)],
            [("window", 0, 0, 0, 0, 0), ("topk", H, H, H // 2, H // 2, 1)],
        ]
        NTILES = dict(soft=64, topk=64, one=4, window=H)
        PER = dict(soft=NT, topk=NT, one=NT, window=1)

        def scale_shift(L, mi, half):
            if mi is None:
                return None, None
            if L == 1:
                o = SCOLS[1]["ln"]
                return SV[:, o + half:o + half + 1], SV[:, o + 2 + half:o + 3 + half]
            return modc[:, 4 * mi + half:4 * mi + half + 1], modc[:, 4 * mi + 2 + half:4 * mi + 3 + half]

        def copy_probs(eng, L, b, att, j):
            variant, t0, h0, _, _, _ = att
            per = PER[variant]
            h = j // per
            eng.wait_ge(pT_psum.handle, pT_psum.at(L, b, t0 + j + 1))
            if h >= 2:
                eng.wait_ge(pv_done.handle, pv_done.at(L, b, h0 + h - 1))
            src = T[j % 2][:, :].rearrange("p (k q) -> p k q", k=NT)
            q = (j % per) * P
            dst = pT[:, h % 2, :, q:q + P]
            if n_ev(L, variant, j):
                eng.tensor_copy(dst, src).then_inc(pT_dve.handle, 1)
            else:
                eng.activation(dst, src, ACT.Copy).then_inc(pT_act.handle, 1)

        @block.sync
        def _(sp):
            for t in range(B):
                sp.dma_start(x_all[:, t * NT:(t + 1) * NT, :], ins["x"][t].rearrange("(t p) c -> p t c", p=P)).then_inc(first_in, 16)
            sp.dma_start(condT[:, :, :], ins["condT"]).then_inc(first_in, 16)
            sp.dma_start(rope[:, :, :, :, :].rearrange("p a t q d -> p (a t q d)"), ins["rope"]).then_inc(first_in, 16)
            sp.sem_inc(cx_used.handle, 1)
            for L in range(LAYERS):
                pw = KC * (MOD[L] * P + GATE[L])
                if L:
                    sp.wait_ge(x_done.handle, x_done.at(L - 1, B - 1, 1))
                sp.dma_start(SV[:, 0:SCOLS[L]["end"]], ins[f"sv{L}"]).then_inc(loaded.handle, 16)
                sp.dma_start(stk[:, 0:pw], ins[f"pw{L}"]).then_inc(loaded.handle, 16)
                sp.dma_start(BB[:, 0:BCOLS[L]["end"]], ins[f"bb{L}"].to_broadcast([P, BCOLS[L]["end"]])).then_inc(loaded.handle, 16)
                sp.dma_start(W[:, 0:WCOLS[L]["end"]], ins[f"w{L}"]).then_inc(loaded.handle, 16)
                with sp.Fori(0, B) as b:
                    sp.wait_ge(cx_used.handle, cx_used.at(L, b, 0))
                    if L == 2:
                        sp.dma_start(cxt, ins["ctx"][bass.ds(b * NT, NT)].rearrange("t p c -> p t c")).then_inc(cx_loaded.handle, 16)
                    else:
                        sp.dma_start(cxT, ins["ctxT"][bass.ds(b * KC, KC)].rearrange("k p n -> p k n")).then_inc(cx_loaded.handle, 16)
                    if L == LAYERS - 1:
                        sp.wait_ge(x_done.handle, x_done.at(L, b, 1))
                        sp.dma_start(out[bass.ds(b * NT, NT)].rearrange("t p c -> p t c"),
                                     x_all[:, bass.ds(b * NT, NT), :]).then_inc(stored, 16)
            sp.wait_ge(stored, 16 * B)

        @block.gpsimd
        def _(pool):
            pool.memset(ident[:, :], 0.0).then_inc(consts, 1)
            pool.memset(identh[:, :], 0.0).then_inc(consts, 1)
            pool.memset(mhalf[:, :], -0.5).then_inc(consts, 1)
            pool.memset(vz[:, :, :, :], 0.0).then_inc(consts, 1)
            pool.wait_ge(consts, 4)
            for m in (ident, identh):
                pool.affine_select(out=m[:, :], in_=m[:, :], compare_op=ALU.not_equal, fill=1.0, base=0,
                                   pattern=[[-1, P]], channel_multiplier=1).then_inc(consts, 1)
            step = Steps(pool, pool_step)

            def ln(L, b, n):
                pool.wait_ge(stats_ready.handle, stats_ready.at(L, b, NT * (n + 1)))
                pool.sem_inc(passed, 1)
                step.did(pool.tensor_scalar(rstd[:, 0, :], mv[:, :, 1], EPS[L], None, ALU.add))
                step.wait()
                pool.tensor_tensor(rstd[:, 1, :], rstd[:, 0, :], mhalf[:, :], ALU.pow).then_inc(rstd_ready.handle, 1)

            def attention(L, b, att):
                variant, t0, _, _, _, _ = att
                for i in range(NTILES[variant]):
                    if variant == "topk":
                        pool.wait_ge(exp_ready.handle, exp_ready.at(L, b, t0 + i + 1))
                        step.did(pool.tensor_tensor(probs[:, i % 2, :], probs[:, i % 2, :], probs2[:, i % 2, :], ALU.subtract))
                        step.wait()
                    if i >= 3:
                        pool.wait_ge(pT_psum.handle, pT_psum.at(L, b, t0 + i - 2))
                    pool.wait_ge(rsum_ready.handle, rsum_ready.at(L, b, t0 + i + 1))
                    pool.sem_inc(passed, 1)
                    if variant == "window":
                        pool.tensor_tensor(pn[:, i % 3, :].rearrange("p (w k) -> p w k", w=NT),
                                           probs[:, i % 2, :].rearrange("p (w k) -> p w k", w=NT),
                                           rsum[:, NT * i:NT * i + NT].rearrange("p (w o) -> p w o", o=1).to_broadcast([P, NT, P]),
                                           ALU.mult).then_inc(pn_ready.handle, 1)
                    else:
                        pool.tensor_scalar(pn[:, i % 3, :], probs[:, i % 2, :], rsum[:, i:i + 1], 1.0, ALU.mult, ALU.mult).then_inc(pn_ready.handle, 1)

            for L in range(LAYERS):
                with pool.Fori(0, B) as b:
                    for a, att in enumerate(ATT[L]):
                        ln(L, b, a if L != 2 or a == 0 else 1)
                        if L == 2 and a == 1:
                            ln(L, b, 2)
                        attention(L, b, att)
                    if L != 1:
                        ln(L, b, lns[L] - 1)
                    step.reset()

        @block.scalar
        def _(act):
            act.wait_ge(first_in, 16 * 6)
            act.activation(condS[:, :, :], condT[:, :, :], ACT.Silu).then_inc(cond_ready, 1)

            def ln(L, b, n, dst, mi, roll=0):
                act.wait_ge(xT_psum.handle, xT_psum.at(L, b, n + 1))
                sc, sh = scale_shift(L, mi, 1)
                pieces = [(0, N, 0)] if not roll else [(roll, N, 0), (0, roll, N - roll)]
                for i, (lo, hi, to) in enumerate(pieces):
                    o, s = dst[:, 1, to:to + hi - lo], A[1][:, lo:hi]
                    if sc is None:
                        x = act.activation(o, s, ACT.Copy)
                    else:
                        x = act.activation(o, s, ACT.Identity, bias=sh, scale=sc)
                x.then_inc(xT_act.handle, 1)

            def stacks(L, b, n):
                for t in range(NT):
                    for j in range(4):
                        i = NT * 4 * n + 4 * t + j
                        act.wait_ge(stackT_psum.handle, stackT_psum.at(L, b, i + 1))
                        act.activation(qkst[0:STACK, 8 * j:8 * j + 8, t * P:(t + 1) * P],
                                       Th[j % 2][0:STACK, :].rearrange("p (h n) -> p h n", h=8), ACT.Copy).then_inc(stackT_ready.handle, 1)

            def attention(L, b, att):
                variant, t0, h0, _, _, n = att
                nt, per = NTILES[variant], PER[variant]

                def out_copy(g):
                    act.wait_ge(pv_done.handle, pv_done.at(L, b, h0 + (g + 1) * (1 if variant == "one" else H // 2)))
                    pieces = [(0, N, 0)] if variant != "window" else [(0, N - ROLL, ROLL), (N - ROLL, N, 0)]
                    for lo, hi, to in pieces:
                        x = act.activation(atT[:, g, to:to + hi - lo], OB[g][:, lo:hi], ACT.Copy)
                    x.then_inc(atT_ready.handle, 1)

                for i in range(nt + LAG + 1):
                    if i < nt:
                        if i >= 2:
                            act.wait_ge(pn_ready.handle, pn_ready.at(L, b, t0 + i - 1))
                        act.wait_ge(max_ready.handle, max_ready.at(L, b, t0 + i + 1))
                        if variant == "window":
                            act.activation(probs[:, i % 2, :], rest[:, 0, i % 2, :], ACT.Exp).then_inc(exp_ready.handle, 1)
                        elif variant == "topk":
                            act.activation(probs[:, i % 2, :], S[i % NS][:, :], ACT.Exp, bias=nmax[:, i:i + 1]).then_inc(act_step, 1)
                            act.wait_ge(rest_ready.handle, rest_ready.at(L, b, i + 1))
                            act.activation(probs2[:, i % 2, :], rest[:, 1, i % 2, :], ACT.Exp, bias=nmax[:, i:i + 1]).then_inc(act_step, 1)
                            act.activation(top[:, 2 + i % 2, :], top[:, i % 2, :], ACT.Exp, bias=nmax[:, i:i + 1],
                                           accum_out=ssum[:, i:i + 1]).then_inc(exp_ready.handle, 1)
                        else:
                            act.activation(probs[:, i % 2, :], S[i % NS][:, :], ACT.Exp, bias=nmax[:, i:i + 1],
                                           accum_out=ssum[:, i:i + 1]).then_inc(exp_ready.handle, 1)
                    j = i - LAG
                    if 0 <= j < nt and not n_ev(L, variant, j):
                        copy_probs(act, L, b, att, j)
                    if variant != "one" and j >= 0 and j == nt // 2 + LAG - 1:
                        out_copy(0)
                if variant == "one":
                    out_copy(0)
                out_copy(1)

            def ffn(L, b):
                fn = {0: ACT.Gelu, 2: ACT.Gelu_apprx_tanh, 3: ACT.Silu}[L]
                m1 = SCOLS[L]["m1"]
                for j in range(NH):
                    if L == 3:
                        act.wait_ge(hid_psum.handle, hid_psum.at(L, b, 2 * j + 1))
                        if j >= 2:
                            act.wait_ge(hid_ready.handle, hid_ready.at(L, b, j - 1))
                        act.activation(sil[:, j % 2, :], A[0][:, :], fn, bias=SV[:, m1 + j:m1 + j + 1]).then_inc(sil_ready.handle, 1)
                    else:
                        act.wait_ge(hid_psum.handle, hid_psum.at(L, b, j + 1))
                        act.activation(hT[:, j, :], A[j % 2][:, :], fn, bias=SV[:, m1 + j:m1 + j + 1]).then_inc(hid_ready.handle, 1)

            def router_layer(b):
                L = 1
                for m in range(KC):
                    act.wait_ge(qk1_psum.handle, qk1_psum.at(L, b, 2 * m + 1))
                    act.activation(q1T[:, m, :], A[m][:, :], ACT.Copy, scale=QSC1).then_inc(qk1_ready.handle, 1)
                    act.wait_ge(qk1_psum.handle, qk1_psum.at(L, b, 2 * m + 2))
                    act.activation(k1T[:, m, :], S[m][:, :], ACT.Copy).then_inc(qk1_ready.handle, 1)
                attention(L, b, ATT[1][0])
                act.wait_ge(rl_shift.handle, rl_shift.at(L, b, 1))
                act.activation(rpr[:, :, 0:E], rlog[:, :, 0:E], ACT.Exp).then_inc(rl_exp.handle, 1)
                for i in range(E * NR + KC):
                    act.wait_ge(eh_psum.handle, eh_psum.at(L, b, i + 1))
                    if i >= 2 * NR and i % NR == 0:
                        act.wait_ge(eo_psum.handle, eo_psum.at(L, b, NT * (i // NR - 1)))
                    act.activation(hT[:, i % (2 * NR), :], A[i % 2][:, :], ACT.Silu, bias=modc[:, i:i + 1]).then_inc(eh_ready.handle, 1)
                for t in range(NT):
                    act.wait_ge(eo_read.handle, eo_read.at(L, b, E * NT + t + 1))
                    act.activation(g1[:, t, :], g1[:, t, :], ACT.Sigmoid).then_inc(gate_ready.handle, 1)

            for L in range(LAYERS):
                with act.Fori(0, B) as b:
                    act.wait_ge(modc_ready.handle, modc_ready.at(L, b, 1))
                    ln(L, b, 0, xnT, 0, roll=ROLL if L == 3 else 0)
                    if L == 1:
                        router_layer(b)
                    else:
                        stacks(L, b, 0)
                        attention(L, b, ATT[L][0])
                        ln(L, b, 1, xnT, None if L == 2 else 1)
                        if L == 2:
                            ln(L, b, 2, cnT, None)
                        stacks(L, b, 1)
                        attention(L, b, ATT[L][1])
                        ln(L, b, lns[L] - 1, xnT, 1 if L == 2 else 2)
                        ffn(L, b)

        @block.tensor
        def _(pe):
            mm = pe.matmul

            def prepare(L):
                pe.wait_ge(loaded.handle, loaded.before(L, 4))
                cols = MOD[L] * P + GATE[L]
                c = condT if L < 2 else condS
                for m in range(MOD[L]):
                    for k in range(KC):
                        x = mm(S[0][:, m * B:(m + 1) * B], stk[:, k * cols + m * P:k * cols + (m + 1) * P], c[:, k, :],
                               start=k == 0, stop=k == KC - 1)
                x.then_inc(prep_psum.handle, 1)
                if GATE[L]:
                    pe.wait_ge(condB_ready.handle, condB_ready.before(L, 1))
                for b in range(B if GATE[L] else 0):
                    pe.wait_ge(prep_read.handle, prep_read.before(L, b + 1))
                    lo = MOD[L] * P
                    for g in range(0, GATE[L], 512):
                        g1_ = min(g + 512, GATE[L])
                        for k in range(KC):
                            x = mm(S[1 + g // 512][:, 0:g1_ - g], condB[:, k, b, :],
                                   stk[:, k * cols + lo + g:k * cols + lo + g1_], start=k == 0, stop=k == KC - 1)
                    x.then_inc(prep_psum.handle, 1)
                pe.wait_ge(prep_read.handle, prep_read.before(L, 1 + (B if GATE[L] else 0)))

            def ln(L, b, n):
                for t in range(NT):
                    pe.wait_ge(xn_ready.handle, xn_ready.at(L, b, NT * n + t + 1))
                    for k in range(KC):
                        x = pe.transpose(A[k][:, t * P:(t + 1) * P], xn[:, t, k * P:(k + 1) * P], ident[:, :])
                x.then_inc(xT_psum.handle, 1)
                pe.wait_ge(xT_dve.handle, xT_dve.at(L, b, n + 1))
                pe.wait_ge(xT_act.handle, xT_act.at(L, b, n + 1))

            def qkv(L, b, n, src_kv):
                sfx = "2" if n else ""
                for t in range(NT + 1):
                    if t < NT:
                        if t >= 2:
                            pe.wait_ge(qk_read.handle, qk_read.at(L, b, NT * n + t - 1))
                        tok = slice(t * P, (t + 1) * P)
                        for name, src, o in (("q", xnT, 0), ("k", src_kv, C)):
                            for k in range(KC):
                                x = mm(A[t % 2][:, o:o + C], src[:, k, tok], w(L, name + sfx, k), start=k == 0, stop=k == KC - 1)
                        x.then_inc(qk_psum.handle, 1)
                        if t >= 2:
                            pe.wait_ge(v_ready.handle, v_ready.at(L, b, NT * n + t - 1))
                        for k in range(KC):
                            x = mm(S[t % 2][:, 0:C], src_kv[:, k, tok], w(L, "v" + sfx, k), start=k == 0, stop=k == KC - 1)
                        x.then_inc(v_psum.handle, 1)
                    if t:
                        pe.wait_ge(stack_ready.handle, stack_ready.at(L, b, NT * n + t))
                        for j in range(4):
                            i = NT * 4 * n + 4 * (t - 1) + j
                            if 4 * (t - 1) + j >= 2:
                                pe.wait_ge(stackT_ready.handle, stackT_ready.at(L, b, i - 1))
                            for h in range(8):
                                x = pe.transpose(Th[j % 2][0:STACK, h * P:(h + 1) * P], qk_tok[:, (t - 1) % 2, 8 * j + h, :], identh[:, :])
                            x.then_inc(stackT_psum.handle, 1)
                pe.wait_ge(stackT_ready.handle, stackT_ready.at(L, b, NT * 4 * (n + 1)))
                pe.wait_ge(v_ready.handle, v_ready.at(L, b, NT * (n + 1)))

            def attention(L, b, att):
                variant, t0, h0, d0, a0, n = att
                nt, per = NTILES[variant], PER[variant]

                def wait_copied(j):
                    d, a = evs(variant, j + 1)
                    if n_ev(L, variant, j):
                        pe.wait_ge(pT_dve.handle, pT_dve.at(L, b, d0 + d))
                    else:
                        pe.wait_ge(pT_act.handle, pT_act.at(L, b, a0 + a))

                def scores(i):
                    if i >= NS:
                        r = max_ready if variant == "window" else exp_ready
                        pe.wait_ge(r.handle, r.at(L, b, t0 + i - NS + 1))
                    s = S[i % NS]
                    if variant == "one":
                        for k in range(KC):
                            x = mm(s[:, :], q1T[:, k, i * P:(i + 1) * P], k1T[:, k, :], start=k == 0, stop=k == KC - 1)
                    elif variant == "window":
                        for v in range(NT):
                            blk = slice(v * P, (v + 1) * P)
                            x = mm(s[:, blk], qkst[0:STACK, i, blk], qkst[0:STACK, H + i, blk], start=True, stop=True)
                    else:
                        h, t = i // NT, i % NT
                        x = mm(s[:, :], qkst[0:STACK, h, t * P:(t + 1) * P], qkst[0:STACK, H + h, :], start=True, stop=True)
                    x.then_inc(scores_ready.handle, 1)

                def product(h):
                    last = (h + 1) * per - 1
                    wait_copied(last)
                    if last:
                        wait_copied(last - 1)
                    if variant == "one":
                        for m in range(KC):
                            for k in range(NT):
                                x = mm(OB[m][:, :], v1[:, k, m * P:(m + 1) * P], pT[:, 0, k, :], start=k == 0, stop=k == NT - 1)
                            x.then_inc(pv_done.handle, 1)
                        return
                    g, r = h // 8, (h % 8) // 2
                    o = OB[g][32 * r:32 * r + 32, :]
                    for k in range(NT):
                        v = vz[:, k, h, :]
                        if variant == "window":
                            x = mm(o[:, k * P:(k + 1) * P], v, pT[:, h % 2, k, 0:P], start=k == 0 and h % 2 == 0,
                                   stop=h % 2 == 1, skip_group_check=True)
                        else:
                            x = mm(o, v, pT[:, h % 2, k, :], start=k == 0 and h % 2 == 0, stop=k == NT - 1 and h % 2 == 1)
                    x.then_inc(pv_done.handle, 1)

                for i in range(nt + LAG + 1):
                    if i < nt:
                        scores(i)
                    j = i - LAG
                    if 0 <= j < nt:
                        pe.wait_ge(pn_ready.handle, pn_ready.at(L, b, t0 + j + 1))
                        if j >= 2:
                            wait_copied(j - 2)
                        for k in range(NT):
                            x = pe.transpose(T[j % 2][:, k * P:(k + 1) * P], pn[:, j % 3, k * P:(k + 1) * P], ident[:, :])
                        x.then_inc(pT_psum.handle, 1)
                    if j >= 1 and j % per == 0:
                        product(j // per - 1)
                pe.wait_ge(atT_ready.handle, atT_ready.at(L, b, 2 * n + 2))

            def project_out(L, b, n):
                for t in range(NT):
                    if t >= 2:
                        pe.wait_ge(out_read.handle, out_read.at(L, b, NT * n + t - 1))
                    for k in range(KC):
                        x = mm(A[t % 2][:, 0:C], atT[:, k, t * P:(t + 1) * P], w(L, "o2" if n else "o", k), start=k == 0, stop=k == KC - 1)
                    x.then_inc(out_psum.handle, 1)

            def ffn(L, b):
                if L == 3:
                    for j in range(NH):
                        for half in range(2):
                            if j >= 1:
                                if half == 0:
                                    pe.wait_ge(sil_ready.handle, sil_ready.at(L, b, j))
                                else:
                                    pe.wait_ge(hid_ready.handle, hid_ready.at(L, b, j))
                            lo = half * HID + j * P
                            for k in range(KC):
                                x = mm(A[half][:, :], w(L, "w1", k, lo, lo + P, 2 * HID), xnT[:, k, :], start=k == 0, stop=k == KC - 1)
                            x.then_inc(hid_psum.handle, 1)
                else:
                    for j in range(NH):
                        if j >= 2:
                            pe.wait_ge(hid_ready.handle, hid_ready.at(L, b, j - 1))
                        for k in range(KC):
                            x = mm(A[j % 2][:, :], w(L, "w1", k, j * P, (j + 1) * P, HID), xnT[:, k, :], start=k == 0, stop=k == KC - 1)
                        x.then_inc(hid_psum.handle, 1)
                pe.wait_ge(hid_ready.handle, hid_ready.at(L, b, NH))
                for t in range(NT):
                    if t >= 2:
                        pe.wait_ge(ffn_read.handle, ffn_read.at(L, b, t - 1))
                    for j in range(NH):
                        x = mm(T[t % 2][:, 0:C], hT[:, j, t * P:(t + 1) * P], w(L, "w2", j), start=j == 0, stop=j == NH - 1)
                    x.then_inc(ffn_psum.handle, 1)

            def router_layer(b):
                L = 1
                for m in range(KC):
                    for name, src, dst in (("q", xnT, A[m]), ("k", cxT, S[m])):
                        for k in range(KC):
                            x = mm(dst[:, :], w(L, name, k, m * P, (m + 1) * P), src[:, k, :], start=k == 0, stop=k == KC - 1)
                        x.then_inc(qk1_psum.handle, 1)
                for t in range(NT):
                    if t >= 2:
                        pe.wait_ge(v_ready.handle, v_ready.at(L, b, t - 1))
                    for k in range(KC):
                        x = mm(T[t % 2][:, 0:C], cxT[:, k, t * P:(t + 1) * P], w(L, "v", k), start=k == 0, stop=k == KC - 1)
                    x.then_inc(v_psum.handle, 1)
                pe.wait_ge(qk1_ready.handle, qk1_ready.at(L, b, 2 * KC))
                pe.wait_ge(v_ready.handle, v_ready.at(L, b, NT))
                pe.nop().then_inc(cx_used.handle, 1)
                attention(L, b, ATT[1][0])
                comb = [xnT[:, 0, :], xnT[:, 1, :], atT[:, 0, :], atT[:, 1, :]]
                for t in range(NT):
                    for k in range(4):
                        x = mm(S[0][:, 4 * t:4 * t + E], comb[k][:, t * P:(t + 1) * P], w(L, "r", k, 0, E, E), start=k == 0, stop=k == 3)
                x.then_inc(rl_psum.handle, 1)

                def hidden(i, name, off, width):
                    if i >= 2:
                        pe.wait_ge(eh_ready.handle, eh_ready.at(L, b, i - 1))
                    for k in range(4):
                        o = WCOLS[1][name] + k * width + off
                        x = mm(A[i % 2][:, :], W[:, o:o + P], comb[k], start=k == 0, stop=k == 3)
                    x.then_inc(eh_psum.handle, 1)

                def down(e, chunks, name, col):
                    for t in range(NT):
                        i = e * NT + t
                        if i >= 2:
                            pe.wait_ge(eo_read.handle, eo_read.at(L, b, i - 1))
                        for j in range(chunks):
                            o = WCOLS[1][name] + col + j * C
                            x = mm(T[t % 2][:, 0:C], hT[:, (e % 2) * NR + j, t * P:(t + 1) * P], W[:, o:o + C], start=j == 0, stop=j == chunks - 1)
                        x.then_inc(eo_psum.handle, 1)

                for e in range(E + 1):
                    for j in range(NR if e < E else KC):
                        if e < E:
                            hidden(e * NR + j, "e1", e * 4 * RH + j * P, RH)
                        else:
                            hidden(e * NR + j, "g1", j * P, C)
                    if e:
                        pe.wait_ge(eh_ready.handle, eh_ready.at(L, b, e * NR))
                        down(e - 1, NR, "e2", (e - 1) * NR * C)
                pe.wait_ge(eh_ready.handle, eh_ready.at(L, b, E * NR + KC))
                down(E, KC, "g2", 0)
                pe.wait_ge(eo_read.handle, eo_read.at(L, b, (E + 1) * NT))
                for t in range(NT):
                    for k in range(KC):
                        x = pe.transpose(A[k][:, t * P:(t + 1) * P], routed[:, t, k * P:(k + 1) * P], ident[:, :])
                x.then_inc(roT_psum.handle, 1)
                pe.wait_ge(roT_ready.handle, roT_ready.at(L, b, 1))
                for t in range(NT):
                    if t >= 2:
                        pe.wait_ge(out_read.handle, out_read.at(L, b, t - 1))
                    for k in range(KC):
                        x = mm(A[t % 2][:, 0:C], roT[:, k, t * P:(t + 1) * P], w(L, "o", k), start=k == 0, stop=k == KC - 1)
                    x.then_inc(out_psum.handle, 1)

            pe.wait_ge(consts, 6)
            pe.wait_ge(cond_ready, 1)
            for L in range(LAYERS):
                prepare(L)
                with pe.Fori(0, B) as b:
                    ln(L, b, 0)
                    if L == 1:
                        pe.wait_ge(cx_loaded.handle, cx_loaded.at(L, b, 1))
                        router_layer(b)
                    else:
                        qkv(L, b, 0, xnT)
                        attention(L, b, ATT[L][0])
                        project_out(L, b, 0)
                        ln(L, b, 1)
                        if L == 2:
                            ln(L, b, 2)
                            qkv(L, b, 1, cnT)
                        else:
                            pe.wait_ge(cx_loaded.handle, cx_loaded.at(L, b, 1))
                            qkv(L, b, 1, cxT)
                        pe.nop().then_inc(cx_used.handle, 1)
                        attention(L, b, ATT[L][1])
                        project_out(L, b, 1)
                        ln(L, b, lns[L] - 1)
                        ffn(L, b)

        @block.vector
        def _(dve):
            step = Steps(dve, dve_step)

            def prepare(L):
                dve.wait_ge(loaded.handle, loaded.before(L, 4))
                if GATE[L]:
                    c = condT if L < 2 else condS
                    dve.tensor_copy(condB, c[:, :, :].rearrange("p k (b o) -> p k b o", o=1).to_broadcast([P, KC, B, P])).then_inc(condB_ready.handle, 1)
                if L >= 2:
                    for name in ("qkv", "qkv2"):
                        o = BCOLS[L][name]
                        step.did(dve.tensor_scalar(BB[:, o:o + C], BB[:, o:o + C], QSC, None, ALU.mult))
                dve.wait_ge(prep_psum.handle, prep_psum.before(L, 1))
                step.did(dve.tensor_tensor(mod[:, :, 0:MOD[L]], S[0][:, 0:MOD[L] * B].rearrange("p (m b) -> p b m", b=B),
                                           SV[:, 0:MOD[L]].rearrange("p (o m) -> p o m", o=1).to_broadcast([P, B, MOD[L]]), ALU.add))
                step.wait()
                if L != 1:
                    v = mod[:, :, 0:MOD[L]].rearrange("p b (n s) -> p b n s", s=4)[:, :, :, 0:2]
                    dve.tensor_scalar(v, v, 1.0, None, ALU.add).then_inc(prep_read.handle, 1)
                else:
                    dve.engine_nop().then_inc(prep_read.handle, 1)
                for b in range(B if GATE[L] else 0):
                    dve.wait_ge(prep_psum.handle, prep_psum.before(L, b + 2))
                    bo = BCOLS[L]["gate"]
                    for g in range(0, GATE[L], 512):
                        hi = min(g + 512, GATE[L])
                        x = dve.tensor_tensor(gates[:, b, g:hi], S[1 + g // 512][:, 0:hi - g], BB[:, bo + g:bo + hi], ALU.add)
                        if hi < GATE[L]:
                            step.did(x)
                            step.wait()
                    x.then_inc(prep_read.handle, 1)
                dve.wait_ge(prep_read.handle, prep_read.before(L, 1 + (B if GATE[L] else 0)))
                step.reset()

            def ln(L, b, n, src, dst, mi, roll=0):
                step.wait()
                dve.sem_inc(passed, 1)
                for t in range(NT):
                    step.did(dve.bn_stats(st[:, t, :], src(t)))
                step.wait()
                for t in range(NT):
                    dve.bn_aggr(mv[:, t, :], st[:, t, :]).then_inc(stats_ready.handle, 1)
                dve.wait_ge(rstd_ready.handle, rstd_ready.at(L, b, n + 1))
                for t in range(NT):
                    dve.tensor_scalar(xn[:, t, :], src(t), mv[:, t, 0:1], rstd[:, 1, t:t + 1], ALU.subtract, ALU.mult).then_inc(xn_ready.handle, 1)
                dve.wait_ge(xT_psum.handle, xT_psum.at(L, b, n + 1))
                sc, sh = scale_shift(L, mi, 0)
                pieces = [(0, N, 0)] if not roll else [(roll, N, 0), (0, roll, N - roll)]
                for lo, hi, to in pieces:
                    o, s = dst[:, 0, to:to + hi - lo], A[0][:, lo:hi]
                    x = dve.tensor_copy(o, s) if sc is None else dve.tensor_scalar(o, s, sc, sh, ALU.mult, ALU.add)
                x.then_inc(xT_dve.handle, 1)

            def v_view(t):
                return vz[:, t, :, :].rearrange("p h c -> p (h c)").rearrange("p (r f c) -> p r f c", f=4, c=D)[:, :, 0:4:3, :]

            def qkv(L, b, n):
                for t in range(NT):
                    i = NT * n + t
                    a = A[t % 2]
                    dve.wait_ge(qk_psum.handle, qk_psum.at(L, b, i + 1))
                    if L == 0:
                        def heads4(ap):
                            return ap.rearrange("p (q h d) -> p q h d", q=2, d=D)
                        def table(s, lo, hi):
                            tb = rope[:, s, t, :, lo:hi].rearrange("p q (o d) -> p q o d", o=1)
                            return tb.to_broadcast([P, 2, H, hi - lo])
                        hd = D // 2
                        step.did(dve.tensor_tensor(heads4(ra), heads4(a[:, :]), table(0, 0, D), ALU.mult))
                        step.did(dve.tensor_tensor(heads4(rb)[:, :, :, 0:hd], heads4(a[:, :])[:, :, :, hd:D], table(1, 0, hd), ALU.mult))
                        dve.tensor_tensor(heads4(rb)[:, :, :, hd:D], heads4(a[:, :])[:, :, :, 0:hd], table(1, hd, D), ALU.mult).then_inc(qk_read.handle, 1)
                        step.wait()
                        dve.wait_ge(qk_read.handle, qk_read.at(L, b, i + 1))
                        step.did(dve.tensor_tensor(qkf, ra, rb, ALU.add))
                    else:
                        bo = BCOLS[L]["qkv2" if n else "qkv"]
                        step.did(dve.scalar_tensor_tensor(out=qkf[:, 0:C], in0=a[:, 0:C], scalar=QSC, in1=BB[:, bo:bo + C], op0=ALU.mult, op1=ALU.add))
                        dve.tensor_tensor(qkf[:, C:2 * C], a[:, C:2 * C], BB[:, bo + C:bo + 2 * C], ALU.add).then_inc(qk_read.handle, 1)
                        dve.wait_ge(qk_read.handle, qk_read.at(L, b, i + 1))
                    step.wait()
                    step.did(dve.tensor_copy(parts[:, 0, :], qkf))
                    step.wait()
                    step.did(dve.tensor_tensor(ra, qkf, parts[:, 0, :], ALU.subtract))
                    dve.wait_ge(v_psum.handle, v_psum.at(L, b, i + 1))
                    sv = S[t % 2][:, 0:C].rearrange("p (r e d) -> p r e d", e=2, d=D)
                    if L == 0:
                        dve.tensor_copy(v_view(t), sv).then_inc(v_ready.handle, 1)
                    else:
                        bv = BB[:, bo + 2 * C:bo + 3 * C].rearrange("p (r e d) -> p r e d", e=2, d=D)
                        dve.tensor_tensor(v_view(t), sv, bv, ALU.add).then_inc(v_ready.handle, 1)
                    step.wait()
                    step.did(dve.tensor_copy(parts[:, 1, :], ra))
                    step.wait()
                    step.did(dve.tensor_tensor(parts[:, 2, :], ra, parts[:, 1, :], ALU.subtract))
                    step.wait()
                    if t >= 2:
                        dve.wait_ge(stackT_psum.handle, stackT_psum.at(L, b, NT * 4 * n + 4 * (t - 1)))
                    qs = qk_tok[:, t % 2, 0:H, :].rearrange("p h (s d) -> p s h d", d=D)
                    ks = qk_tok[:, t % 2, H:2 * H, :].rearrange("p h (s d) -> p s h d", d=D)
                    pq = parts[:, :, 0:C].rearrange("p s (h d) -> p s h d", d=D)
                    pk = parts[:, :, C:2 * C].rearrange("p s (h d) -> p s h d", d=D)
                    step.did(dve.tensor_copy(qs[:, 0:3], pq[:, 0:3]))
                    step.did(dve.tensor_copy(qs[:, 3:5], pq[:, 0:2]))
                    step.did(dve.tensor_copy(qs[:, 5], pq[:, 0]))
                    step.did(dve.tensor_copy(ks[:, 0:3], pk[:, 0:1].to_broadcast([P, 3, H, D])))
                    step.did(dve.tensor_copy(ks[:, 3:5], pk[:, 1:2].to_broadcast([P, 2, H, D])))
                    step.did(dve.tensor_copy(ks[:, 5], pk[:, 2]))
                    step.wait()
                    dve.engine_nop().then_inc(stack_ready.handle, 1)

            def attention(L, b, att):
                variant, t0, h0, _, _, n = att
                nt = NTILES[variant]
                for i in range(nt + LAG):
                    if i < nt:
                        s = S[i % NS]
                        dve.wait_ge(scores_ready.handle, scores_ready.at(L, b, t0 + i + 1))
                        if variant == "window":
                            s4 = s[:, :].rearrange("p (w k) -> p w k", w=NT)
                            step.did(dve.tensor_reduce(nmax[:, NT * i:NT * i + NT], s4, AX.X, ALU.max))
                            if i >= 2:
                                dve.wait_ge(exp_ready.handle, exp_ready.at(L, b, t0 + i - 1))
                            step.wait()
                            m = nmax[:, NT * i:NT * i + NT].rearrange("p (w o) -> p w o", o=1).to_broadcast([P, NT, P])
                            dve.tensor_tensor(rest[:, 0, i % 2, :].rearrange("p (w k) -> p w k", w=NT), s4, m, ALU.subtract).then_inc(max_ready.handle, 1)
                        elif variant == "topk":
                            r1, r2, tp = rest[:, 0, i % 2, :], rest[:, 1, i % 2, :], top[:, i % 2, :]
                            if i >= 2:
                                dve.wait_ge(exp_ready.handle, exp_ready.at(L, b, t0 + i - 1))
                            dve.sem_inc(passed, 1)
                            step.did(dve.max(tp[:, 0:8], s[:, :]))
                            step.wait()
                            step.did(dve.match_replace(r1, tp[:, 0:8], s[:, :], LOWEST))
                            dve.tensor_scalar(nmax[:, i:i + 1], tp[:, 0:1], -1.0, None, ALU.mult).then_inc(max_ready.handle, 1)
                            step.wait()
                            step.did(dve.max(tp[:, 8:16], r1))
                            step.wait()
                            dve.match_replace(r2, tp[:, 8:16], r1, LOWEST).then_inc(rest_ready.handle, 1)
                        else:
                            dve.tensor_reduce(nmax[:, i:i + 1], s[:, :], AX.X, ALU.max, negate=True).then_inc(max_ready.handle, 1)
                    j = i - 1
                    if 0 <= j < nt:
                        dve.wait_ge(exp_ready.handle, exp_ready.at(L, b, t0 + j + 1))
                        if variant == "window":
                            cols = slice(NT * j, NT * j + NT)
                            step.did(dve.tensor_reduce(ssum[:, cols], probs[:, j % 2, :].rearrange("p (w k) -> p w k", w=NT), AX.X, ALU.add))
                            step.wait()
                        else:
                            cols = slice(j, j + 1)
                        dve.reciprocal(rsum[:, cols], ssum[:, cols]).then_inc(rsum_ready.handle, 1)
                    j = i - LAG
                    if 0 <= j < nt and n_ev(L, variant, j):
                        copy_probs(dve, L, b, att, j)

            def residual(L, b, t, src, bias, gate, last):
                x = x_all[:, b * NT + t, :]
                r = res[:, t % 2, :]
                if bias is None and gate is None:
                    step.did(dve.tensor_tensor(x, src, x, ALU.add))
                    return
                step.wait()
                if bias is not None:
                    last(dve.tensor_tensor(r, src, bias, ALU.add))
                if gate is not None:
                    step.did(dve.tensor_tensor(r, r, gate, ALU.mult))
                    step.wait()
                step.did(dve.tensor_tensor(x, x, r, ALU.add))

            def project_out(L, b, n):
                for t in range(NT):
                    dve.wait_ge(out_psum.handle, out_psum.at(L, b, NT * n + t + 1))
                    bias = BB[:, BCOLS[L]["o2" if n else "o"]:][:, 0:C] if L else None
                    gate = None
                    if L == 2 and n == 0:
                        gate = gates[:, b, 0:C]
                    if L == 3:
                        gate = gates[:, b, n * C:(n + 1) * C]
                    x = x_all[:, b * NT + t, :]
                    r = res[:, t % 2, :]
                    if bias is None:
                        dve.tensor_tensor(x, A[t % 2][:, 0:C], x, ALU.add).then_inc(out_read.handle, 1)
                        dve.wait_ge(out_read.handle, out_read.at(L, b, NT * n + t + 1))
                        continue
                    dve.tensor_tensor(r, A[t % 2][:, 0:C], bias, ALU.add).then_inc(out_read.handle, 1)
                    dve.wait_ge(out_read.handle, out_read.at(L, b, NT * n + t + 1))
                    if gate is not None:
                        step.did(dve.tensor_tensor(r, r, gate, ALU.mult))
                        step.wait()
                    step.did(dve.tensor_tensor(x, x, r, ALU.add))
                    step.wait()

            def ffn(L, b):
                if L == 3:
                    m1 = SCOLS[L]["m1"] + NH
                    for j in range(NH):
                        dve.wait_ge(hid_psum.handle, hid_psum.at(L, b, 2 * j + 2))
                        dve.wait_ge(sil_ready.handle, sil_ready.at(L, b, j + 1))
                        dve.scalar_tensor_tensor(out=hT[:, j, :], in0=A[1][:, :], scalar=SV[:, m1 + j:m1 + j + 1],
                                                 in1=sil[:, j % 2, :], op0=ALU.add, op1=ALU.mult).then_inc(hid_ready.handle, 1)
                for t in range(NT):
                    dve.wait_ge(ffn_psum.handle, ffn_psum.at(L, b, t + 1))
                    o = BCOLS[L]["m2"]
                    x = x_all[:, b * NT + t, :]
                    r = res[:, t % 2, :]
                    dve.tensor_tensor(r, T[t % 2][:, 0:C], BB[:, o:o + C], ALU.add).then_inc(ffn_read.handle, 1)
                    dve.wait_ge(ffn_read.handle, ffn_read.at(L, b, t + 1))
                    if L:
                        g = (1 if L == 2 else 2) * C
                        step.did(dve.tensor_tensor(r, r, gates[:, b, g:g + C], ALU.mult))
                        step.wait()
                    if t == NT - 1:
                        step.wait()
                        dve.tensor_tensor(x, x, r, ALU.add).then_inc(x_done.handle, 1)
                    else:
                        step.did(dve.tensor_tensor(x, x, r, ALU.add))
                        step.wait()

            def router_layer(b):
                L = 1
                for t in range(NT):
                    dve.wait_ge(v_psum.handle, v_psum.at(L, b, t + 1))
                    dve.tensor_copy(v1[:, t, :], T[t % 2][:, 0:C]).then_inc(v_ready.handle, 1)
                attention(L, b, ATT[1][0])
                dve.wait_ge(rl_psum.handle, rl_psum.at(L, b, 1))
                rl, rp = rlog[:, :, 0:E], rpr[:, :, 0:E]

                def over(ap, n=E):
                    return ap.rearrange("p (t o) -> p t o", o=1).to_broadcast([P, NT, n])
                step.did(dve.tensor_tensor(rl, S[0][:, 0:4 * NT].rearrange("p (t e) -> p t e", e=4)[:, :, 0:E],
                                           gates[:, bass.ds(b, 1), 0:E].to_broadcast([P, NT, E]), ALU.add))
                step.wait()
                step.did(dve.tensor_reduce(rsm[:, 0, :], rl, AX.X, ALU.max))
                step.wait()
                dve.tensor_tensor(rl, rl, over(rsm[:, 0, :]), ALU.subtract).then_inc(rl_shift.handle, 1)
                dve.wait_ge(rl_exp.handle, rl_exp.at(L, b, 1))
                step.did(dve.tensor_reduce(rsm[:, 0, :], rp, AX.X, ALU.add))
                step.wait()
                step.did(dve.reciprocal(rsm[:, 1, :], rsm[:, 0, :]))
                step.wait()
                step.did(dve.tensor_tensor(rp, rp, over(rsm[:, 1, :]), ALU.mult))
                step.wait()
                for e in range(E):
                    for t in range(NT):
                        bo = BCOLS[L]["e2"] + e * C
                        pe_ = rpr[:, t, e:e + 1]
                        if e == 0:
                            step.did(dve.tensor_scalar(routed[:, t, :], BB[:, bo:bo + C], pe_, None, ALU.mult))
                        else:
                            step.did(dve.scalar_tensor_tensor(out=routed[:, t, :], in0=BB[:, bo:bo + C], scalar=pe_, in1=routed[:, t, :], op0=ALU.mult, op1=ALU.add))
                    step.wait()
                for e in range(E):
                    for t in range(NT):
                        i = e * NT + t
                        dve.wait_ge(eo_psum.handle, eo_psum.at(L, b, i + 1))
                        if e:
                            dve.wait_ge(eo_read.handle, eo_read.at(L, b, i - NT + 1))
                        dve.scalar_tensor_tensor(out=routed[:, t, :], in0=T[t % 2][:, 0:C], scalar=rpr[:, t, e:e + 1],
                                                 in1=routed[:, t, :], op0=ALU.mult, op1=ALU.add).then_inc(eo_read.handle, 1)
                for t in range(NT):
                    i = E * NT + t
                    dve.wait_ge(eo_psum.handle, eo_psum.at(L, b, i + 1))
                    bo = BCOLS[L]["g2"]
                    dve.tensor_tensor(g1[:, t, :], T[t % 2][:, 0:C], BB[:, bo:bo + C], ALU.add).then_inc(eo_read.handle, 1)
                dve.wait_ge(roT_psum.handle, roT_psum.at(L, b, 1))
                step.did(dve.tensor_copy(roT[:, 0, :], A[0][:, :]))
                step.wait()
                dve.tensor_copy(roT[:, 1, :], A[1][:, :]).then_inc(roT_ready.handle, 1)
                for t in range(NT):
                    dve.wait_ge(out_psum.handle, out_psum.at(L, b, t + 1))
                    bo = BCOLS[L]["o"]
                    r = res[:, t % 2, :]
                    x = x_all[:, b * NT + t, :]
                    dve.tensor_tensor(r, A[t % 2][:, 0:C], BB[:, bo:bo + C], ALU.add).then_inc(out_read.handle, 1)
                    dve.wait_ge(out_read.handle, out_read.at(L, b, t + 1))
                    dve.wait_ge(gate_ready.handle, gate_ready.at(L, b, t + 1))
                    step.did(dve.tensor_tensor(r, r, g1[:, t, :], ALU.mult))
                    step.wait()
                    if t == NT - 1:
                        dve.tensor_tensor(x, x, r, ALU.add).then_inc(x_done.handle, 1)
                    else:
                        step.did(dve.tensor_tensor(x, x, r, ALU.add))
                        step.wait()

            dve.wait_ge(first_in, 16 * 6)
            dve.wait_ge(consts, 6)
            dve.wait_ge(cond_ready, 1)
            for L in range(LAYERS):
                prepare(L)
                with dve.Fori(0, B) as b:
                    def x_tile(t):
                        return x_all[:, b * NT + t, :]
                    dve.tensor_copy(modc[:, 0:MOD[L]], mod[:, b, 0:MOD[L]]).then_inc(modc_ready.handle, 1)
                    dve.wait_ge(modc_ready.handle, modc_ready.at(L, b, 1))
                    ln(L, b, 0, x_tile, xnT, 0, roll=ROLL if L == 3 else 0)
                    if L == 1:
                        router_layer(b)
                    else:
                        qkv(L, b, 0)
                        attention(L, b, ATT[L][0])
                        project_out(L, b, 0)
                        ln(L, b, 1, x_tile, xnT, None if L == 2 else 1)
                        if L == 2:
                            dve.wait_ge(cx_loaded.handle, cx_loaded.at(L, b, 1))
                            ln(L, b, 2, lambda t: cxt[:, t, :], cnT, None)
                        qkv(L, b, 1)
                        attention(L, b, ATT[L][1])
                        project_out(L, b, 1)
                        ln(L, b, lns[L] - 1, x_tile, xnT, 1 if L == 2 else 2)
                        ffn(L, b)
                    step.wait()
                    dve.wait_ge(x_done.handle, x_done.at(L, b, 1))
                    step.reset(waited=True)


def kernel(**inputs):
    import numpy as _np
    import concourse.bacc as _bacc
    from concourse import mybir as _mybir
    from concourse.bass_utils import run_bass_kernel_spmd as _run

    g = {k: _np.asarray(v) for k, v in inputs.items()}

    def t(name):
        return g[name]

    def cm(a):
        r, c = a.shape
        return a.reshape(r // P, P, c).transpose(1, 0, 2).reshape(P, -1)

    def cv(v):
        return v.reshape(-1, P).T

    def cat(parts):
        return _np.ascontiguousarray(_np.concatenate(parts, axis=1))

    def row(parts):
        return _np.ascontiguousarray(_np.concatenate([p.reshape(-1) for p in parts]).reshape(1, -1))

    a = {"x": _np.ascontiguousarray(t("x"))}
    a["ctx"] = _np.ascontiguousarray(t("ctx_1024").reshape(B * NT, P, C))
    a["ctxT"] = _np.ascontiguousarray(t("ctx_1024").transpose(0, 2, 1).reshape(B * KC, P, N))
    a["condT"] = _np.ascontiguousarray(t("cond_1024").T.reshape(KC, P, B).transpose(1, 0, 2))
    half = D // 2
    f32 = _np.float32
    inv = (f32(1.0) / _np.power(f32(10000.0), _np.arange(half, dtype=f32) / f32(half))).astype(f32)
    ang = (_np.arange(N, dtype=f32)[:, None] * inv[None, :]).astype(f32)
    cos, sin = _np.cos(ang), _np.sin(ang)
    tab = _np.stack([_np.concatenate([cos, cos], 1), _np.concatenate([-sin, sin], 1)])
    tab = _np.stack([tab * f32(QSC), tab], 2).astype(f32)
    a["rope"] = _np.ascontiguousarray(tab.reshape(2, NT, P, 2, D).transpose(2, 0, 1, 3, 4).reshape(P, -1))

    L0, L1, L2, L3 = (f"L{i}_xcond_" for i in range(4))
    qkv = t(L0 + "qkv_w").T
    a["w0"] = cat([cm(qkv[:, 0:C]), cm(qkv[:, C:2 * C]), cm(qkv[:, 2 * C:]), cm(t(L0 + "sa_out_w").T), cm(t(L0 + "q_w").T), cm(t(L0 + "k_w").T),
                   cm(t(L0 + "v_w").T), cm(t(L0 + "ca_out_w").T), cm(t(L0 + "ffn_w1").T), cm(t(L0 + "ffn_w2").T)])
    a["pw0"] = cat([cm(_np.concatenate([t(L0 + f"ln{i}_w").T for i in (1, 2, 3)], axis=1))])
    a["bb0"] = row([t(L0 + "ffn_b2")])
    a["sv0"] = cat([cv(t(L0 + f"ln{i}_b")) for i in (1, 2, 3)] + [cv(t(L0 + "ffn_b1"))])

    e1, g1w, rw = t(L1 + "e_w1"), t(L1 + "gate_w1"), t(L1 + "router_W")
    a["w1"] = cat([cm(t(L1 + "Wq")), cm(t(L1 + "Wk")), cm(t(L1 + "Wv"))] + [cm(e1[e, 0:2 * C]) for e in range(E)]
                  + [cm(t(L1 + "e_w2")[e]) for e in range(E)] + [cm(g1w[0:2 * C]), cm(t(L1 + "gate_w2")), cm(t(L1 + "out_w")), cm(rw[0:2 * C])])
    a["pw1"] = cat([cm(_np.concatenate([e1[e, 2 * C:] for e in range(E)] + [g1w[2 * C:], rw[2 * C:]], axis=1))])
    a["bb1"] = row([t(L1 + "e_b2"), t(L1 + "gate_b2"), t(L1 + "out_b"), t(L1 + "router_b")])
    a["sv1"] = cat([cv(t(L1 + "e_b1").reshape(-1)), cv(t(L1 + "gate_b1")), cv(t(L1 + "ln_gamma")), cv(t(L1 + "ln_beta"))])

    def cols(m, order):
        return _np.concatenate([m[..., i * C:(i + 1) * C] for i in order], axis=-1)

    wq, kv = t(L2 + "W_qkv"), t(L2 + "W_kvc")
    a["w2"] = cat([cm(wq[:, 0:C]), cm(wq[:, C:2 * C]), cm(wq[:, 2 * C:]), cm(t(L2 + "W_proj")), cm(t(L2 + "W_qc")), cm(kv[:, 0:C]), cm(kv[:, C:]),
                   cm(t(L2 + "W_cproj")), cm(t(L2 + "W_mlp1")), cm(t(L2 + "W_mlp2"))])
    a["pw2"] = cat([cm(cols(t(L2 + "W_mod"), (1, 0, 4, 3, 2, 5)))])
    bm = t(L2 + "b_mod")
    a["bb2"] = row([t(L2 + "b_qkv"), t(L2 + "b_qc"), t(L2 + "b_kvc"), t(L2 + "b_proj"), t(L2 + "b_cproj"), t(L2 + "b_mlp2"), cols(bm, (2, 5))])
    a["sv2"] = cat([cv(cols(bm, (1, 0, 4, 3))), cv(t(L2 + "b_mlp1"))])

    wq, kv = t(L3 + "w_qkv"), t(L3 + "w_kv")
    a["w3"] = cat([cm(wq[:, 0:C]), cm(wq[:, C:2 * C]), cm(wq[:, 2 * C:]), cm(t(L3 + "w_so")), cm(t(L3 + "w_q")), cm(kv[:, 0:C]), cm(kv[:, C:]),
                   cm(t(L3 + "w_co")), cm(t(L3 + "w_m1")), cm(t(L3 + "w_m2"))])
    a["pw3"] = cat([cm(cols(t(L3 + "w_ada"), (1, 0, 4, 3, 7, 6, 2, 5, 8)))])
    bm = t(L3 + "b_ada")
    a["bb3"] = row([t(L3 + "b_qkv"), t(L3 + "b_q"), t(L3 + "b_kv"), t(L3 + "b_so"), t(L3 + "b_co"), t(L3 + "b_m2"), cols(bm, (2, 5, 8))])
    a["sv3"] = cat([cv(cols(bm, (1, 0, 4, 3, 7, 6))), cv(t(L3 + "b_m1"))])

    nc = _bacc.Bacc("TRN2", target_bir_lowering=False, num_devices=1)
    ins = {k: nc.dram_tensor(f"in_{k}", v.shape, _mybir.dt.from_np(v.dtype), kind="ExternalInput").ap() for k, v in a.items()}
    out = nc.dram_tensor("out_0", (B * NT, P, C), _mybir.dt.float32, kind="ExternalOutput").ap()
    four_layers(nc, ins, out)
    r = _run(nc, [{f"in_{k}": v for k, v in a.items()}], core_ids=[0])
    return r.results[0]["out_0"].reshape(B, N, C)
```

```python
import numpy as np
import concourse.bass as bass
from concourse import mybir
from contextlib import ExitStack

F32 = mybir.dt.float32
BF16 = mybir.dt.bfloat16
ACT = mybir.ActivationFunctionType
ALU = mybir.AluOpType
AX = mybir.AxisListType

P = 128
B = 4
N = 512
C = 256
KC = C // P
NT = N // P
H = 16
D = C // H
HID = 1024
NH = HID // P
E = 3
RH = 2 * C
NR = RH // P
ROLL = 64
STACK = 6 * D
QSC = D ** -0.5
QSC1 = C ** -0.5
LOWEST = -3.0e38
NS = 3
LAG = 3
G = 4
TLAG = 2
AHEAD = 6
AUG = 2
U = KC * C

WCOLS = [dict(q=0, k=U, v=2 * U, o=3 * U, q2=4 * U, k2=5 * U, v2=6 * U, o2=7 * U, w1=8 * U, w2=12 * U, end=16 * U)] * 4
WCOLS = [dict(w) for w in WCOLS]
WCOLS[1] = dict(q=0, k=U, v=2 * U, e1=3 * U, e2=15 * U, g1=21 * U, g2=23 * U, o=24 * U, r=25 * U, end=25 * U + 4 * E)
WCOLS[3] = dict(WCOLS[0], w2=16 * U, end=20 * U)
WMAX = max(w["end"] for w in WCOLS)
MOD = [12, 14, 8, 12]
GATE = [0, E, 2 * C, 3 * C]
BCOLS = [dict(m2=0, end=C),
         dict(e2=0, g2=E * C, o=(E + 1) * C, gate=(E + 2) * C, end=(E + 2) * C + E),
         dict(qkv=0, qkv2=3 * C, o=6 * C, o2=7 * C, m2=8 * C, gate=9 * C, end=11 * C),
         dict(qkv=0, qkv2=3 * C, o=6 * C, o2=7 * C, m2=8 * C, gate=9 * C, end=12 * C)]
BMAX = max(w["end"] for w in BCOLS)
SCOLS = [dict(mod=0, m1=12, end=20), dict(mod=0, ln=14, end=18), dict(mod=0, m1=8, end=16), dict(mod=0, m1=12, end=28)]
SMAX = max(w["end"] for w in SCOLS)
LAYERS = 4
EPS = [1e-5, 1e-5, 1e-6, 1e-6]


class Progress:

    def __init__(self, handle, per, pre=(0, 0, 0, 0), start=0, unit=1):
        self.handle, self.per, self.pre, self.start, self.unit = handle, per, pre, start, unit

    def base(self, L):
        return self.start + sum(self.pre[i] + B * self.per[i] for i in range(L))

    def before(self, L, k):
        return (self.base(L) + k) * self.unit

    def at(self, L, b, k):
        return b * (self.per[L] * self.unit) + (self.base(L) + self.pre[L] + k) * self.unit


class Steps:

    def __init__(self, eng, handle):
        self.eng, self.handle, self.n = eng, handle, 0

    def did(self, ins):
        self.n += 1
        ins.then_inc(self.handle, 1)

    def wait(self):
        if self.n:
            self.eng.wait_ge(self.handle, self.n)

    def reset(self, waited=False):
        if self.n:
            if not waited:
                self.eng.wait_ge(self.handle, self.n)
            self.eng.sem_clear(self.handle)
            self.n = 0


def four_layers(nc, ins, out):
    ctx = ExitStack()
    with ctx:
        def sb(name, shape, dt=F32):
            return ctx.enter_context(nc.sbuf_tensor(name, shape, dt))

        def sem(name):
            return ctx.enter_context(nc.semaphore(name))

        x_all = sb("x_all", [P, B * NT, C])
        W = sb("W", [P, WMAX])
        BB = sb("BB", [P, BMAX])
        SV = sb("SV", [P, SMAX])
        mod = sb("mod", [P, B, max(MOD)])
        modc = sb("modc", [P, max(MOD)])
        gates = sb("gates", [P, B, max(GATE)])
        stk = sb("stk", [P, 2 * H * N // 2])
        qkst = stk[:, :].bitcast(BF16).rearrange("p (h n) -> p h n", h=2 * H)
        qk_tok = sb("qk_tok", [P, 2, 2 * H, STACK], BF16)
        tmp = sb("tmp", [P, 8 * C])
        qkf = tmp[:, 0:4 * C].rearrange("p (i n) -> p i n", i=2)
        left = tmp[:, 4 * C:8 * C].rearrange("p (i n) -> p i n", i=2)
        rest = tmp[:, 0:8 * C].rearrange("p (a i n) -> p a i n", a=2, i=2)
        vz = sb("vz", [P, NT, H, 32])
        xn = sb("xn", [P, NT, C])
        xnT = sb("xnT", [P, KC, N])
        cx = sb("cx", [P, KC * N])
        cxT = cx[:, :].rearrange("p (k n) -> p k n", k=KC)
        cxt = cx[:, :].rearrange("p (t c) -> p t c", t=NT)
        atT = sb("atT", [P, KC, N])
        probs = sb("probs", [P, 2, N])
        probs2 = sb("probs2", [P, 2, N])
        cnT = probs2[:, :, :]
        pn = sb("pn", [P, 3, N])
        pT = sb("pT", [P, 2, NT, N])
        hT = pT[:, :, :, :].rearrange("p a t n -> p (a t) n")
        mparts = sb("mparts", [P, H * NT, AUG], BF16)
        mrest = sb("mrest", [P, G * NT])
        ou = sb("ou", [P, 2, N])
        rden = sb("rden", [P, NT, G])
        condB = hT[:, 0:2, :].rearrange("p k (b n) -> p k b n", b=B)
        top = sb("top", [P, 2, 16])
        nmax = sb("nmax", [P, H * NT])
        ssum = sb("ssum", [P, NT])
        rsum = sb("rsum", [P, NT])
        st = sb("st", [P, NT, 6])
        mv = sb("mv", [P, NT, 2])
        rstd = sb("rstd", [P, 2, NT])
        mhalf = sb("mhalf", [P, NT])
        sil = probs[:, :, :]
        res = sb("res", [P, 2, C])
        rlog = sb("rlog", [P, NT, 4])
        rpr = sb("rpr", [P, NT, 4])
        rsm = sb("rsm", [P, 2, NT])
        condT = sb("condT", [P, KC, B])
        condS = sb("condS", [P, KC, B])
        rope = sb("rope", [P, 2, NT, 2, D])
        ident = sb("ident", [P, P])
        identh = sb("identh", [P, P], BF16)
        def part(i):
            return stk[:, i * KC * N:(i + 1) * KC * N]
        q1T = part(0).rearrange("p (k n) -> p k n", k=KC)
        k1T = part(1).rearrange("p (k n) -> p k n", k=KC)
        v1 = part(2).rearrange("p (t c) -> p t c", t=NT)
        routed = part(3).rearrange("p (t c) -> p t c", t=NT)
        roT = part(4).rearrange("p (k n) -> p k n", k=KC)
        g1 = part(5).rearrange("p (t c) -> p t c", t=NT)

        def bank(name):
            return ctx.enter_context(nc.psum_tensor(name, [P, N], F32))
        S = [bank(f"S{i}") for i in range(NS)]
        T = [bank(f"T{i}") for i in range(2)]
        Th = [t[:, :].bitcast(BF16) for t in T]
        A = [bank(f"A{i}") for i in range(2)]
        O = bank("O")
        OB = [O, A[0]]

        def prog(name, per, pre=(0, 0, 0, 0), start=0, unit=1):
            return Progress(sem(name), per, pre, start, unit)
        tiles = [2 * 64, 4, 2 * 64, H + 64]
        soft = [2 * 64, 0, 2 * 64, 0]
        other = [0, 4, 0, H + 64]
        atts = [2, 0, 2, 2]
        lns = [3, 1, 4, 3]
        qkvs = [2, 0, 2, 2]
        loaded = prog("loaded", [0] * 4, [4] * 4, start=0, unit=16)
        first_in = sem("first_in")
        consts = sem("consts")
        cond_ready = sem("cond_ready")
        condB_ready = prog("condB_ready", [0] * 4, [1 if g else 0 for g in GATE])
        prep_psum = prog("prep_psum", [0] * 4, [1 + (B if g else 0) for g in GATE])
        prep_read = prog("prep_read", [0] * 4, [1 + (B if g else 0) for g in GATE])
        modc_ready = prog("modc_ready", [1] * 4)
        cx_loaded = prog("cx_loaded", [1] * 4, unit=16)
        cx_used = prog("cx_used", [1] * 4, start=1)
        stats_ready = prog("stats_ready", [NT * n for n in lns])
        rstd_ready = prog("rstd_ready", lns)
        xn_ready = prog("xn_ready", [NT * n for n in lns])
        xT_psum = prog("xT_psum", lns)
        xT_dve = prog("xT_dve", lns)
        xT_act = prog("xT_act", lns)
        qk_psum = prog("qk_psum", [NT * n for n in qkvs])
        qk_read = prog("qk_read", [NT * n for n in qkvs])
        v_psum = prog("v_psum", [NT, NT, NT, NT] and [NT * 2, NT, NT * 2, NT * 2])
        v_ready = prog("v_ready", [NT * 2, NT, NT * 2, NT * 2])
        parts_ready = prog("parts_ready", [2 * NT * n for n in qkvs])
        stack_dve = prog("stack_dve", [NT * n for n in qkvs])
        stack_pool = prog("stack_pool", [NT * n for n in qkvs])
        stackT_psum = prog("stackT_psum", [4 * NT * n for n in qkvs])
        stackT_ready = prog("stackT_ready", [4 * NT * n for n in qkvs])
        scores_ready = prog("scores_ready", other)
        first_psum = prog("first_psum", soft)
        second_psum = prog("second_psum", soft)
        max_ready = prog("max_ready", tiles)
        mparts_ready = prog("mparts_ready", [H // G * n if s_ else 0 for n, s_ in zip(atts, soft)])
        mrow_psum = prog("mrow_psum", [H // 2 * n if s_ else 0 for n, s_ in zip(atts, soft)])
        mrow_ready = prog("mrow_ready", [H // 2 * n if s_ else 0 for n, s_ in zip(atts, soft)])
        ones_ready = prog("ones_ready", [0] * 4, [1, 0, 1, 0])
        exp_ready = prog("exp_ready", tiles)
        rest_ready = prog("rest_ready", [0, 0, 0, 64])
        rsum_ready = prog("rsum_ready", [0, 4, 0, 0])
        pn_ready = prog("pn_ready", [0, 4, 0, 64])
        pT_psum = prog("pT_psum", other)
        pT_dve = prog("pT_dve", [0, 2, 0, H // 2])
        pT_act = prog("pT_act", [0, 2, 0, H // 2 + 64])
        pv_done = prog("pv_done", [2 * 64, KC, 2 * 64, 2 * H])
        ou_ready = prog("ou_ready", [H // G * n for n in atts])
        tok_psum = prog("tok_psum", [H // G * n for n in atts])
        tok_ready = prog("tok_ready", [H // G * n for n in atts])
        atT_psum = prog("atT_psum", atts)
        atT_dve = prog("atT_dve", atts)
        atT_act = prog("atT_act", [2, 2, 2, 2])
        out_psum = prog("out_psum", [2 * NT, NT, 2 * NT, 2 * NT])
        out_read = prog("out_read", [2 * NT, NT, 2 * NT, 2 * NT])
        hid_psum = prog("hid_psum", [NH, 0, NH, 2 * NH])
        hid_ready = prog("hid_ready", [NH, 0, NH, NH])
        sil_ready = prog("sil_ready", [0, 0, 0, NH])
        ffn_psum = prog("ffn_psum", [NT, 0, NT, NT])
        ffn_read = prog("ffn_read", [NT, 0, NT, NT])
        qk1_psum = prog("qk1_psum", [0, 2 * KC, 0, 0])
        qk1_ready = prog("qk1_ready", [0, 2 * KC, 0, 0])
        rl_psum = prog("rl_psum", [0, 1, 0, 0])
        rl_shift = prog("rl_shift", [0, 1, 0, 0])
        rl_exp = prog("rl_exp", [0, 1, 0, 0])
        eh_psum = prog("eh_psum", [0, E * NR + KC, 0, 0])
        eh_ready = prog("eh_ready", [0, E * NR + KC, 0, 0])
        eo_psum = prog("eo_psum", [0, (E + 1) * NT, 0, 0])
        eo_read = prog("eo_read", [0, (E + 1) * NT, 0, 0])
        gate_ready = prog("gate_ready", [0, NT, 0, 0])
        roT_psum = prog("roT_psum", [0, 1, 0, 0])
        roT_ready = prog("roT_ready", [0, 1, 0, 0])
        x_done = prog("x_done", [1] * 4)
        stored = sem("stored")
        passed = sem("passed")
        dve_step, act_step, pool_step = sem("dve_step"), sem("act_step"), sem("pool_step")

        block = ctx.enter_context(nc.Block())

        def w(L, name, k, lo=0, hi=C, width=C):
            o = WCOLS[L][name] + k * width
            return W[:, o + lo:o + hi]

        def n_ev(L, variant, j):
            return variant != "topk" and j % 2 == 0

        def evs(variant, j):
            return (0, j) if variant == "topk" else ((j + 1) // 2, j // 2)

        def att(v, n, t0=0, n0=0, h0=0, d0=0, a0=0):
            return dict(v=v, n=n, t0=t0, n0=n0, h0=h0, d0=d0, a0=a0)
        ATT = [
            [att("soft", 0), att("soft", 1, t0=64, h0=64)],
            [att("one", 0)],
            [att("soft", 0), att("soft", 1, t0=64, h0=64)],
            [att("window", 0), att("topk", 1, t0=H, h0=H, d0=H // 2, a0=H // 2)],
        ]
        NTILES = dict(topk=64, one=4, window=H)
        PER = dict(topk=NT, one=NT, window=1)

        def group_end(per, g):
            return G * per * (g + 1) + per - 1

        def scale_shift(L, mi, half):
            if mi is None:
                return None, None
            if L == 1:
                o = SCOLS[1]["ln"]
                return SV[:, o + half:o + half + 1], SV[:, o + 2 + half:o + 3 + half]
            return modc[:, 4 * mi + half:4 * mi + half + 1], modc[:, 4 * mi + 2 + half:4 * mi + 3 + half]

        def copy_probs(eng, L, b, att, j):
            variant, per = att["v"], PER[att["v"]]
            h = j // per
            eng.wait_ge(pT_psum.handle, pT_psum.at(L, b, att["t0"] + j + 1))
            if h >= 2:
                eng.wait_ge(pv_done.handle, pv_done.at(L, b, att["h0"] + h - 1))
            src = T[j % 2][:, :].rearrange("p (k q) -> p k q", k=NT)
            q = (j % per) * P
            dst = pT[:, h % 2, :, q:q + P]
            if n_ev(L, variant, j):
                eng.tensor_copy(dst, src).then_inc(pT_dve.handle, 1)
            else:
                eng.activation(dst, src, ACT.Copy).then_inc(pT_act.handle, 1)

        @block.sync
        def _(sp):
            for t in range(B):
                sp.dma_start(x_all[:, t * NT:(t + 1) * NT, :], ins["x"][t].rearrange("(t p) c -> p t c", p=P)).then_inc(first_in, 16)
            sp.dma_start(condT[:, :, :], ins["condT"]).then_inc(first_in, 16)
            sp.dma_start(rope[:, :, :, :, :].rearrange("p a t q d -> p (a t q d)"), ins["rope"]).then_inc(first_in, 16)
            sp.sem_inc(cx_used.handle, 1)
            for L in range(LAYERS):
                pw = KC * (MOD[L] * P + GATE[L])
                if L:
                    sp.wait_ge(x_done.handle, x_done.at(L - 1, B - 1, 1))
                sp.dma_start(SV[:, 0:SCOLS[L]["end"]], ins[f"sv{L}"]).then_inc(loaded.handle, 16)
                sp.dma_start(stk[:, 0:pw], ins[f"pw{L}"]).then_inc(loaded.handle, 16)
                sp.dma_start(BB[:, 0:BCOLS[L]["end"]], ins[f"bb{L}"].to_broadcast([P, BCOLS[L]["end"]])).then_inc(loaded.handle, 16)
                sp.dma_start(W[:, 0:WCOLS[L]["end"]], ins[f"w{L}"]).then_inc(loaded.handle, 16)
                with sp.Fori(0, B) as b:
                    sp.wait_ge(cx_used.handle, cx_used.at(L, b, 0))
                    if L == 2:
                        sp.dma_start(cxt, ins["ctx"][bass.ds(b * NT, NT)].rearrange("t p c -> p t c")).then_inc(cx_loaded.handle, 16)
                    else:
                        sp.dma_start(cxT, ins["ctxT"][bass.ds(b * KC, KC)].rearrange("k p n -> p k n")).then_inc(cx_loaded.handle, 16)
                    if L == LAYERS - 1:
                        sp.wait_ge(x_done.handle, x_done.at(L, b, 1))
                        sp.dma_start(out[bass.ds(b * NT, NT)].rearrange("t p c -> p t c"),
                                     x_all[:, bass.ds(b * NT, NT), :]).then_inc(stored, 16)
            sp.wait_ge(stored, 16 * B)

        @block.gpsimd
        def _(pool):
            pool.memset(ident[:, :], 0.0).then_inc(consts, 1)
            pool.memset(identh[:, :], 0.0).then_inc(consts, 1)
            pool.memset(mhalf[:, :], -0.5).then_inc(consts, 1)
            pool.memset(vz[:, :, :, :], 0.0).then_inc(consts, 1)
            pool.wait_ge(consts, 4)
            pool.memset(vz[:, :, :, D:D + 1], 1.0).then_inc(consts, 1)
            for m in (ident, identh):
                pool.affine_select(out=m[:, :], in_=m[:, :], compare_op=ALU.not_equal, fill=1.0, base=0,
                                   pattern=[[-1, P]], channel_multiplier=1).then_inc(consts, 1)
            step = Steps(pool, pool_step)

            def ln(L, b, n):
                pool.wait_ge(stats_ready.handle, stats_ready.at(L, b, NT * (n + 1)))
                pool.sem_inc(passed, 1)
                step.did(pool.tensor_scalar(rstd[:, 0, :], mv[:, :, 1], EPS[L], None, ALU.add))
                step.wait()
                pool.tensor_tensor(rstd[:, 1, :], rstd[:, 0, :], mhalf[:, :], ALU.pow).then_inc(rstd_ready.handle, 1)

            def stacks(L, b, n):
                for t in range(NT):
                    i = NT * n + t
                    q, k = (qk_tok[:, t % 2, h0:h0 + H, :].rearrange("p h (s d) -> p s h d", d=D) for h0 in (0, H))
                    two = [P, 2, H, D]
                    pool.wait_ge(parts_ready.handle, parts_ready.at(L, b, 2 * i + 1))
                    pool.sem_inc(passed, 1)
                    step.did(pool.tensor_scalar(q[:, 2:6:2], q[:, 0:1].to_broadcast(two), 1.0, 1.0, ALU.mult, ALU.mult))
                    step.did(pool.tensor_scalar(k[:, 3:6:2], k[:, 0:1].to_broadcast(two), 1.0, 1.0, ALU.mult, ALU.mult))
                    pool.wait_ge(parts_ready.handle, parts_ready.at(L, b, 2 * i + 2))
                    pool.sem_inc(passed, 1)
                    step.did(pool.tensor_scalar(q[:, 3], q[:, 1], 1.0, 1.0, ALU.mult, ALU.mult))
                    step.did(pool.tensor_scalar(k[:, 2], k[:, 1], 1.0, 1.0, ALU.mult, ALU.mult))
                    step.wait()
                    pool.sem_inc(stack_pool.handle, 1)

            def attention(L, b, att):
                variant, t0, n0 = att["v"], att["t0"], att["n0"]
                if variant in ("soft", "window"):
                    return
                for i in range(NTILES[variant]):
                    if i >= 3:
                        pool.wait_ge(pT_psum.handle, pT_psum.at(L, b, t0 + i - 2))
                    if variant == "topk":
                        pool.wait_ge(exp_ready.handle, exp_ready.at(L, b, t0 + i + 1))
                        pool.tensor_tensor(pn[:, i % 3, :], probs[:, i % 2, :], probs2[:, i % 2, :], ALU.subtract).then_inc(pn_ready.handle, 1)
                    else:
                        pool.wait_ge(rsum_ready.handle, rsum_ready.at(L, b, t0 + i + 1))
                        pool.sem_inc(passed, 1)
                        pool.tensor_scalar(pn[:, i % 3, :], probs[:, i % 2, :], rsum[:, i:i + 1], 1.0, ALU.mult, ALU.mult).then_inc(pn_ready.handle, 1)

            for L in range(LAYERS):
                if L in (0, 2):
                    pool.wait_ge(prep_read.handle, prep_read.before(L, 1 + (B if GATE[L] else 0)))
                    pool.memset(qkst[STACK:STACK + AUG, H:2 * H, :], 1.0).then_inc(ones_ready.handle, 1)
                    pool.wait_ge(ones_ready.handle, ones_ready.before(L, 1))
                with pool.Fori(0, B) as b:
                    for a, att in enumerate(ATT[L]):
                        ln(L, b, a if L != 2 or a == 0 else 1)
                        if L == 2 and a == 1:
                            ln(L, b, 2)
                        if L != 1:
                            stacks(L, b, a)
                        attention(L, b, att)
                    if L != 1:
                        ln(L, b, lns[L] - 1)
                    step.reset()

        @block.scalar
        def _(act):
            act.wait_ge(first_in, 16 * 6)
            act.activation(condS[:, :, :], condT[:, :, :], ACT.Silu).then_inc(cond_ready, 1)

            def ln(L, b, n, dst, mi, roll=0):
                act.wait_ge(xT_psum.handle, xT_psum.at(L, b, n + 1))
                sc, sh = scale_shift(L, mi, 1)
                pieces = [(0, N, 0)] if not roll else [(roll, N, 0), (0, roll, N - roll)]
                for i, (lo, hi, to) in enumerate(pieces):
                    o, s = dst[:, 1, to:to + hi - lo], A[1][:, lo:hi]
                    if sc is None:
                        x = act.activation(o, s, ACT.Copy)
                    else:
                        x = act.activation(o, s, ACT.Identity, bias=sh, scale=sc)
                x.then_inc(xT_act.handle, 1)

            def stacks(L, b, n):
                for t in range(NT):
                    for j in range(4):
                        i = NT * 4 * n + 4 * t + j
                        act.wait_ge(stackT_psum.handle, stackT_psum.at(L, b, i + 1))
                        act.activation(qkst[0:STACK, 8 * j:8 * j + 8, t * P:(t + 1) * P],
                                       Th[j % 2][0:STACK, :].rearrange("p (h n) -> p h n", h=8), ACT.Copy).then_inc(stackT_ready.handle, 1)

            def finish(L, b, att):
                act.wait_ge(atT_psum.handle, atT_psum.at(L, b, att["n"] + 1))
                pieces = [(0, N, 0)] if att["v"] != "window" else [(0, N - ROLL, ROLL), (N - ROLL, N, 0)]
                for lo, hi, to in pieces:
                    x = act.activation(atT[:, 1, to:to + hi - lo], A[1][:, lo:hi], ACT.Copy)
                x.then_inc(atT_act.handle, 1)

            def group_out(L, b, att, g, count):
                act.wait_ge(pv_done.handle, pv_done.at(L, b, att["h0"] + count))
                if g >= 2:
                    act.wait_ge(tok_psum.handle, tok_psum.at(L, b, H // G * att["n"] + g - 1))
                act.activation(ou[:, g % 2, :], OB[g % 2][:, :], ACT.Copy).then_inc(ou_ready.handle, 1)

            def soft_attention(L, b, att):
                t0, h0 = att["t0"], att["h0"]
                for s in range(NT * H // G + 1):
                    if s < NT * H // G:
                        for r in range(G):
                            i = G * s + r
                            if i >= 8:
                                act.wait_ge(pv_done.handle, pv_done.at(L, b, h0 + i - 7))
                            act.wait_ge(second_psum.handle, second_psum.at(L, b, t0 + i + 1))
                            act.activation(hT[:, i % 8, :], S[i % NS][:, :], ACT.Exp).then_inc(exp_ready.handle, 1)
                    if s and s % NT == 0:
                        group_out(L, b, att, s // NT - 1, G * s)
                finish(L, b, att)

            def attention(L, b, att):
                variant, t0 = att["v"], att["t0"]
                if variant == "soft":
                    return soft_attention(L, b, att)
                nt, per = NTILES[variant], PER[variant]
                ends = {group_end(per, g) + 1: g for g in range(H // G)} if variant != "one" else {}
                for i in range(nt + LAG + per + 3):
                    if i < nt:
                        act.wait_ge(max_ready.handle, max_ready.at(L, b, t0 + i + 1))
                        if variant == "window":
                            if i >= 3:
                                act.wait_ge(pT_psum.handle, pT_psum.at(L, b, t0 + i - 2))
                            act.activation(pn[:, i % 3, :], rest[:, 0, i % 2, :], ACT.Exp).then_inc(exp_ready.handle, 1)
                        else:
                            if i >= 2:
                                act.wait_ge(pn_ready.handle, pn_ready.at(L, b, att["n0"] + i - 1))
                            if variant == "topk":
                                act.activation(probs[:, i % 2, :], S[i % NS][:, :], ACT.Exp, bias=nmax[:, i:i + 1]).then_inc(act_step, 1)
                                act.wait_ge(rest_ready.handle, rest_ready.at(L, b, i + 1))
                                act.activation(probs2[:, i % 2, :], rest[:, 1, i % 2, :], ACT.Exp, bias=nmax[:, i:i + 1]).then_inc(exp_ready.handle, 1)
                            else:
                                act.activation(probs[:, i % 2, :], S[i % NS][:, :], ACT.Exp, bias=nmax[:, i:i + 1],
                                               accum_out=ssum[:, i:i + 1]).then_inc(exp_ready.handle, 1)
                    j = i - LAG
                    if 0 <= j < nt and not n_ev(L, variant, j):
                        copy_probs(act, L, b, att, j)
                    if j in ends:
                        group_out(L, b, att, ends[j], G * (ends[j] + 1))
                if variant == "one":
                    for m in range(KC):
                        act.wait_ge(pv_done.handle, pv_done.at(L, b, m + 1))
                        act.activation(atT[:, m, :], OB[m][:, :], ACT.Copy).then_inc(atT_act.handle, 1)
                else:
                    finish(L, b, att)

            def ffn(L, b):
                fn = {0: ACT.Gelu, 2: ACT.Gelu_apprx_tanh, 3: ACT.Silu}[L]
                m1 = SCOLS[L]["m1"]
                for j in range(NH):
                    if L == 3:
                        act.wait_ge(hid_psum.handle, hid_psum.at(L, b, 2 * j + 1))
                        if j >= 2:
                            act.wait_ge(hid_ready.handle, hid_ready.at(L, b, j - 1))
                        act.activation(sil[:, j % 2, :], A[0][:, :], fn, bias=SV[:, m1 + j:m1 + j + 1]).then_inc(sil_ready.handle, 1)
                    else:
                        act.wait_ge(hid_psum.handle, hid_psum.at(L, b, j + 1))
                        act.activation(hT[:, j, :], A[j % 2][:, :], fn, bias=SV[:, m1 + j:m1 + j + 1]).then_inc(hid_ready.handle, 1)

            def router_layer(b):
                L = 1
                for m in range(KC):
                    act.wait_ge(qk1_psum.handle, qk1_psum.at(L, b, 2 * m + 1))
                    act.activation(q1T[:, m, :], A[m][:, :], ACT.Copy, scale=QSC1).then_inc(qk1_ready.handle, 1)
                    act.wait_ge(qk1_psum.handle, qk1_psum.at(L, b, 2 * m + 2))
                    act.activation(k1T[:, m, :], S[m][:, :], ACT.Copy).then_inc(qk1_ready.handle, 1)
                attention(L, b, ATT[1][0])
                act.wait_ge(rl_shift.handle, rl_shift.at(L, b, 1))
                act.activation(rpr[:, :, 0:E], rlog[:, :, 0:E], ACT.Exp).then_inc(rl_exp.handle, 1)
                for i in range(E * NR + KC):
                    act.wait_ge(eh_psum.handle, eh_psum.at(L, b, i + 1))
                    if i >= 2 * NR and i % NR == 0:
                        act.wait_ge(eo_psum.handle, eo_psum.at(L, b, NT * (i // NR - 1)))
                    act.activation(hT[:, i % (2 * NR), :], A[i % 2][:, :], ACT.Silu, bias=modc[:, i:i + 1]).then_inc(eh_ready.handle, 1)
                for t in range(NT):
                    act.wait_ge(eo_read.handle, eo_read.at(L, b, E * NT + t + 1))
                    act.activation(g1[:, t, :], g1[:, t, :], ACT.Sigmoid).then_inc(gate_ready.handle, 1)

            for L in range(LAYERS):
                with act.Fori(0, B) as b:
                    act.wait_ge(modc_ready.handle, modc_ready.at(L, b, 1))
                    ln(L, b, 0, xnT, 0, roll=ROLL if L == 3 else 0)
                    if L == 1:
                        router_layer(b)
                    else:
                        stacks(L, b, 0)
                        attention(L, b, ATT[L][0])
                        ln(L, b, 1, xnT, None if L == 2 else 1)
                        if L == 2:
                            ln(L, b, 2, cnT, None)
                        stacks(L, b, 1)
                        attention(L, b, ATT[L][1])
                        ln(L, b, lns[L] - 1, xnT, 1 if L == 2 else 2)
                        ffn(L, b)

        @block.tensor
        def _(pe):
            mm = pe.matmul

            def prepare(L):
                pe.wait_ge(loaded.handle, loaded.before(L, 4))
                cols = MOD[L] * P + GATE[L]
                c = condT if L < 2 else condS
                for m in range(MOD[L]):
                    for k in range(KC):
                        x = mm(S[0][:, m * B:(m + 1) * B], stk[:, k * cols + m * P:k * cols + (m + 1) * P], c[:, k, :],
                               start=k == 0, stop=k == KC - 1)
                x.then_inc(prep_psum.handle, 1)
                if GATE[L]:
                    pe.wait_ge(condB_ready.handle, condB_ready.before(L, 1))
                for b in range(B if GATE[L] else 0):
                    pe.wait_ge(prep_read.handle, prep_read.before(L, b + 1))
                    lo = MOD[L] * P
                    for g in range(0, GATE[L], 512):
                        g1_ = min(g + 512, GATE[L])
                        for k in range(KC):
                            x = mm(S[1 + g // 512][:, 0:g1_ - g], condB[:, k, b, :],
                                   stk[:, k * cols + lo + g:k * cols + lo + g1_], start=k == 0, stop=k == KC - 1)
                    x.then_inc(prep_psum.handle, 1)
                pe.wait_ge(prep_read.handle, prep_read.before(L, 1 + (B if GATE[L] else 0)))

            def ln(L, b, n):
                for t in range(NT):
                    pe.wait_ge(xn_ready.handle, xn_ready.at(L, b, NT * n + t + 1))
                    for k in range(KC):
                        x = pe.transpose(A[k][:, t * P:(t + 1) * P], xn[:, t, k * P:(k + 1) * P], ident[:, :])
                x.then_inc(xT_psum.handle, 1)
                pe.wait_ge(xT_dve.handle, xT_dve.at(L, b, n + 1))
                pe.wait_ge(xT_act.handle, xT_act.at(L, b, n + 1))

            def qkv(L, b, n, src_kv):
                sfx = "2" if n else ""
                for t in range(NT + TLAG):
                    if t < NT:
                        if t >= 2:
                            pe.wait_ge(qk_read.handle, qk_read.at(L, b, NT * n + t - 1))
                        tok = slice(t * P, (t + 1) * P)
                        for name, src, o in (("q", xnT, 0), ("k", src_kv, C)):
                            for k in range(KC):
                                x = mm(A[t % 2][:, o:o + C], src[:, k, tok], w(L, name + sfx, k), start=k == 0, stop=k == KC - 1)
                        x.then_inc(qk_psum.handle, 1)
                        if t >= 2:
                            pe.wait_ge(v_ready.handle, v_ready.at(L, b, NT * n + t - 1))
                        for k in range(KC):
                            x = mm(S[t % 2][:, 0:C], src_kv[:, k, tok], w(L, "v" + sfx, k), start=k == 0, stop=k == KC - 1)
                        x.then_inc(v_psum.handle, 1)
                    u = t - TLAG
                    if u >= 0:
                        pe.wait_ge(stack_dve.handle, stack_dve.at(L, b, NT * n + u + 1))
                        pe.wait_ge(stack_pool.handle, stack_pool.at(L, b, NT * n + u + 1))
                        for j in range(4):
                            i = NT * 4 * n + 4 * u + j
                            if 4 * u + j >= 2:
                                pe.wait_ge(stackT_ready.handle, stackT_ready.at(L, b, i - 1))
                            for h in range(8):
                                x = pe.transpose(Th[j % 2][0:STACK, h * P:(h + 1) * P], qk_tok[:, u % 2, 8 * j + h, :], identh[:, :])
                            x.then_inc(stackT_psum.handle, 1)
                pe.wait_ge(stackT_ready.handle, stackT_ready.at(L, b, NT * 4 * (n + 1)))
                pe.wait_ge(v_ready.handle, v_ready.at(L, b, NT * (n + 1)))

            def to_tokens(L, b, att, g, bank):
                pe.wait_ge(ou_ready.handle, ou_ready.at(L, b, H // G * att["n"] + g + 1))
                if g:
                    pe.wait_ge(tok_ready.handle, tok_ready.at(L, b, H // G * att["n"] + g))
                for t in range(NT):
                    x = pe.transpose(bank[:, t * P:(t + 1) * P], ou[:, g % 2, t * P:(t + 1) * P], ident[:, :])
                x.then_inc(tok_psum.handle, 1)

            def finish(L, b, att):
                n = att["n"]
                pe.wait_ge(tok_ready.handle, tok_ready.at(L, b, H // G * (n + 1)))
                for t in range(NT):
                    for k in range(KC):
                        x = pe.transpose(A[k][:, t * P:(t + 1) * P], xn[:, t, k * P:(k + 1) * P], ident[:, :])
                x.then_inc(atT_psum.handle, 1)
                pe.wait_ge(atT_dve.handle, atT_dve.at(L, b, n + 1))
                pe.wait_ge(atT_act.handle, atT_act.at(L, b, n + 1))

            def soft_attention(L, b, att):
                t0, h0, n = att["t0"], att["h0"], att["n"]
                first = [T[1], A[1]]
                steps = NT * H // G

                def first_scores(c):
                    g, t = c // NT, c % NT
                    for r in range(G):
                        i = G * c + r
                        if i >= 2:
                            pe.wait_ge(max_ready.handle, max_ready.at(L, b, t0 + i - 1))
                        h = G * g + r
                        mm(first[i % 2][:, :], qkst[0:STACK, h, t * P:(t + 1) * P], qkst[0:STACK, H + h, :],
                           start=True, stop=True).then_inc(first_psum.handle, 1)

                def max_rows(g):
                    pe.wait_ge(mparts_ready.handle, mparts_ready.at(L, b, H // G * n + g + 1))
                    if g >= 2:
                        pe.wait_ge(tok_ready.handle, tok_ready.at(L, b, H // G * n + g - 1))
                    for half in range(2):
                        if half:
                            pe.wait_ge(mrow_ready.handle, mrow_ready.at(L, b, H // 2 * n + 2 * g + 1))
                        h = G * g + 2 * half
                        for c in range(2 * NT):
                            x = pe.transpose(Th[0][STACK:STACK + AUG, c * P:(c + 1) * P], mparts[:, h * NT + c, :], identh[:, :])
                        x.then_inc(mrow_psum.handle, 1)

                def second_scores(s, r):
                    g, k = s // NT, s % NT
                    i = G * s + r
                    if i >= NS:
                        pe.wait_ge(exp_ready.handle, exp_ready.at(L, b, t0 + i - NS + 1))
                    h = G * g + r
                    mm(S[i % NS][:, :], qkst[0:STACK + AUG, H + h, k * P:(k + 1) * P], qkst[0:STACK + AUG, h, :],
                       start=True, stop=True).then_inc(second_psum.handle, 1)

                def products(s):
                    g, k = s // NT, s % NT
                    if k == 0 and g >= 2:
                        pe.wait_ge(ou_ready.handle, ou_ready.at(L, b, H // G * n + g - 1))
                    for r in range(G):
                        i = G * s + r
                        pe.wait_ge(exp_ready.handle, exp_ready.at(L, b, t0 + i + 1))
                        mm(OB[g % 2][32 * r:32 * r + 32, :], vz[:, k, G * g + r, :], hT[:, i % 8, :],
                           start=k == 0, stop=k == NT - 1).then_inc(pv_done.handle, 1)

                for c in range(AHEAD):
                    first_scores(c)
                    if c % NT == 0 and c:
                        max_rows(c // NT - 1)
                for s in range(steps + 2):
                    if s < steps:
                        if s % NT == 0:
                            pe.wait_ge(mrow_ready.handle, mrow_ready.at(L, b, H // 2 * n + 2 * (s // NT + 1)))
                        for r in range(G - 1):
                            second_scores(s, r)
                    if 1 <= s <= steps:
                        products(s - 1)
                    if s < steps:
                        second_scores(s, G - 1)
                        if s + AHEAD < steps:
                            first_scores(s + AHEAD)
                        if s + AHEAD <= steps and (s + AHEAD) % NT == 0:
                            max_rows((s + AHEAD) // NT - 1)
                    if s > NT and s % NT == 1:
                        to_tokens(L, b, att, s // NT - 1, T[0])
                finish(L, b, att)

            def attention(L, b, att):
                variant, t0, n = att["v"], att["t0"], att["n"]
                if variant == "soft":
                    return soft_attention(L, b, att)
                nt, per = NTILES[variant], PER[variant]

                def wait_copied(j):
                    d, a = evs(variant, j + 1)
                    if n_ev(L, variant, j):
                        pe.wait_ge(pT_dve.handle, pT_dve.at(L, b, att["d0"] + d))
                    else:
                        pe.wait_ge(pT_act.handle, pT_act.at(L, b, att["a0"] + a))

                def scores(i):
                    if i >= NS:
                        r = max_ready if variant == "window" else exp_ready
                        pe.wait_ge(r.handle, r.at(L, b, t0 + i - NS + 1))
                    s = S[i % NS]
                    if variant == "one":
                        for k in range(KC):
                            x = mm(s[:, :], q1T[:, k, i * P:(i + 1) * P], k1T[:, k, :], start=k == 0, stop=k == KC - 1)
                    elif variant == "window":
                        for v in range(NT):
                            blk = slice(v * P, (v + 1) * P)
                            x = mm(s[:, blk], qkst[0:STACK, i, blk], qkst[0:STACK, H + i, blk], start=True, stop=True)
                    else:
                        h, t = i // NT, i % NT
                        x = mm(s[:, :], qkst[0:STACK, h, t * P:(t + 1) * P], qkst[0:STACK, H + h, :], start=True, stop=True)
                    x.then_inc(scores_ready.handle, 1)

                def product(h, ks):
                    if ks[0] == 0:
                        last = (h + 1) * per - 1
                        wait_copied(last)
                        if last:
                            wait_copied(last - 1)
                    g, r = h // G, h % G
                    if ks[0] == 0 and r == 0 and g >= 2:
                        pe.wait_ge(ou_ready.handle, ou_ready.at(L, b, H // G * n + g - 1))
                    o = OB[g % 2][32 * r:32 * r + 32, :]
                    for k in ks:
                        v = vz[:, k, h, :]
                        if variant == "window":
                            x = mm(o[:, k * P:(k + 1) * P], v, pT[:, h % 2, k, 0:P], start=True, stop=True)
                        else:
                            x = mm(o, v, pT[:, h % 2, k, :], start=k == 0, stop=k == NT - 1)
                    if ks[-1] == NT - 1:
                        x.then_inc(pv_done.handle, 1)

                ends = {group_end(per, g) + 2: g for g in range(H // G)} if variant != "one" else {}
                for i in range(nt + LAG + per + 3):
                    if i < nt:
                        scores(i)
                    j = i - LAG
                    if 0 <= j < nt:
                        if variant == "window":
                            pe.wait_ge(exp_ready.handle, exp_ready.at(L, b, t0 + j + 1))
                        else:
                            pe.wait_ge(pn_ready.handle, pn_ready.at(L, b, att["n0"] + j + 1))
                        if j >= 2:
                            wait_copied(j - 2)
                        for k in range(NT):
                            x = pe.transpose(T[j % 2][:, k * P:(k + 1) * P], pn[:, j % 3, k * P:(k + 1) * P], ident[:, :])
                        x.then_inc(pT_psum.handle, 1)
                    if variant != "one" and per <= j < nt + per:
                        product(j // per - 1, list(range(NT)) if per == 1 else [j % per])
                    if j in ends:
                        to_tokens(L, b, att, ends[j], A[1])
                if variant == "one":
                    wait_copied(nt - 1)
                    wait_copied(nt - 2)
                    for m in range(KC):
                        for k in range(NT):
                            x = mm(OB[m][:, :], v1[:, k, m * P:(m + 1) * P], pT[:, 0, k, :], start=k == 0, stop=k == NT - 1)
                        x.then_inc(pv_done.handle, 1)
                    pe.wait_ge(atT_act.handle, atT_act.at(L, b, KC))
                else:
                    finish(L, b, att)

            def project_out(L, b, n):
                for t in range(NT):
                    if t >= 2:
                        pe.wait_ge(out_read.handle, out_read.at(L, b, NT * n + t - 1))
                    for k in range(KC):
                        x = mm(A[t % 2][:, 0:C], atT[:, k, t * P:(t + 1) * P], w(L, "o2" if n else "o", k), start=k == 0, stop=k == KC - 1)
                    x.then_inc(out_psum.handle, 1)

            def ffn(L, b):
                if L == 3:
                    for j in range(NH):
                        for half in range(2):
                            if j >= 1:
                                if half == 0:
                                    pe.wait_ge(sil_ready.handle, sil_ready.at(L, b, j))
                                else:
                                    pe.wait_ge(hid_ready.handle, hid_ready.at(L, b, j))
                            lo = half * HID + j * P
                            for k in range(KC):
                                x = mm(A[half][:, :], w(L, "w1", k, lo, lo + P, 2 * HID), xnT[:, k, :], start=k == 0, stop=k == KC - 1)
                            x.then_inc(hid_psum.handle, 1)
                else:
                    for j in range(NH):
                        if j >= 2:
                            pe.wait_ge(hid_ready.handle, hid_ready.at(L, b, j - 1))
                        for k in range(KC):
                            x = mm(A[j % 2][:, :], w(L, "w1", k, j * P, (j + 1) * P, HID), xnT[:, k, :], start=k == 0, stop=k == KC - 1)
                        x.then_inc(hid_psum.handle, 1)
                pe.wait_ge(hid_ready.handle, hid_ready.at(L, b, NH))
                for t in range(NT):
                    if t >= 2:
                        pe.wait_ge(ffn_read.handle, ffn_read.at(L, b, t - 1))
                    for j in range(NH):
                        x = mm(T[t % 2][:, 0:C], hT[:, j, t * P:(t + 1) * P], w(L, "w2", j), start=j == 0, stop=j == NH - 1)
                    x.then_inc(ffn_psum.handle, 1)

            def router_layer(b):
                L = 1
                for m in range(KC):
                    for name, src, dst in (("q", xnT, A[m]), ("k", cxT, S[m])):
                        for k in range(KC):
                            x = mm(dst[:, :], w(L, name, k, m * P, (m + 1) * P), src[:, k, :], start=k == 0, stop=k == KC - 1)
                        x.then_inc(qk1_psum.handle, 1)
                for t in range(NT):
                    if t >= 2:
                        pe.wait_ge(v_ready.handle, v_ready.at(L, b, t - 1))
                    for k in range(KC):
                        x = mm(T[t % 2][:, 0:C], cxT[:, k, t * P:(t + 1) * P], w(L, "v", k), start=k == 0, stop=k == KC - 1)
                    x.then_inc(v_psum.handle, 1)
                pe.wait_ge(qk1_ready.handle, qk1_ready.at(L, b, 2 * KC))
                pe.wait_ge(v_ready.handle, v_ready.at(L, b, NT))
                pe.nop().then_inc(cx_used.handle, 1)
                attention(L, b, ATT[1][0])
                comb = [xnT[:, 0, :], xnT[:, 1, :], atT[:, 0, :], atT[:, 1, :]]
                for t in range(NT):
                    for k in range(4):
                        x = mm(S[0][:, 4 * t:4 * t + E], comb[k][:, t * P:(t + 1) * P], w(L, "r", k, 0, E, E), start=k == 0, stop=k == 3)
                x.then_inc(rl_psum.handle, 1)

                def hidden(i, name, off, width):
                    if i >= 2:
                        pe.wait_ge(eh_ready.handle, eh_ready.at(L, b, i - 1))
                    for k in range(4):
                        o = WCOLS[1][name] + k * width + off
                        x = mm(A[i % 2][:, :], W[:, o:o + P], comb[k], start=k == 0, stop=k == 3)
                    x.then_inc(eh_psum.handle, 1)

                def down(e, chunks, name, col):
                    for t in range(NT):
                        i = e * NT + t
                        if i >= 2:
                            pe.wait_ge(eo_read.handle, eo_read.at(L, b, i - 1))
                        for j in range(chunks):
                            o = WCOLS[1][name] + col + j * C
                            x = mm(T[t % 2][:, 0:C], hT[:, (e % 2) * NR + j, t * P:(t + 1) * P], W[:, o:o + C], start=j == 0, stop=j == chunks - 1)
                        x.then_inc(eo_psum.handle, 1)

                for e in range(E + 1):
                    for j in range(NR if e < E else KC):
                        if e < E:
                            hidden(e * NR + j, "e1", e * 4 * RH + j * P, RH)
                        else:
                            hidden(e * NR + j, "g1", j * P, C)
                    if e:
                        pe.wait_ge(eh_ready.handle, eh_ready.at(L, b, e * NR))
                        down(e - 1, NR, "e2", (e - 1) * NR * C)
                pe.wait_ge(eh_ready.handle, eh_ready.at(L, b, E * NR + KC))
                down(E, KC, "g2", 0)
                pe.wait_ge(eo_read.handle, eo_read.at(L, b, (E + 1) * NT))
                for t in range(NT):
                    for k in range(KC):
                        x = pe.transpose(A[k][:, t * P:(t + 1) * P], routed[:, t, k * P:(k + 1) * P], ident[:, :])
                x.then_inc(roT_psum.handle, 1)
                pe.wait_ge(roT_ready.handle, roT_ready.at(L, b, 1))
                for t in range(NT):
                    if t >= 2:
                        pe.wait_ge(out_read.handle, out_read.at(L, b, t - 1))
                    for k in range(KC):
                        x = mm(A[t % 2][:, 0:C], roT[:, k, t * P:(t + 1) * P], w(L, "o", k), start=k == 0, stop=k == KC - 1)
                    x.then_inc(out_psum.handle, 1)

            pe.wait_ge(consts, 7)
            pe.wait_ge(cond_ready, 1)
            for L in range(LAYERS):
                prepare(L)
                if L in (0, 2):
                    pe.wait_ge(ones_ready.handle, ones_ready.before(L, 1))
                with pe.Fori(0, B) as b:
                    ln(L, b, 0)
                    if L == 1:
                        pe.wait_ge(cx_loaded.handle, cx_loaded.at(L, b, 1))
                        router_layer(b)
                    else:
                        qkv(L, b, 0, xnT)
                        attention(L, b, ATT[L][0])
                        project_out(L, b, 0)
                        ln(L, b, 1)
                        if L == 2:
                            ln(L, b, 2)
                            qkv(L, b, 1, cnT)
                        else:
                            pe.wait_ge(cx_loaded.handle, cx_loaded.at(L, b, 1))
                            qkv(L, b, 1, cxT)
                        pe.nop().then_inc(cx_used.handle, 1)
                        attention(L, b, ATT[L][1])
                        project_out(L, b, 1)
                        ln(L, b, lns[L] - 1)
                        ffn(L, b)

        @block.vector
        def _(dve):
            step = Steps(dve, dve_step)

            def prepare(L):
                dve.wait_ge(loaded.handle, loaded.before(L, 4))
                if GATE[L]:
                    c = condT if L < 2 else condS
                    dve.tensor_copy(condB, c[:, :, :].rearrange("p k (b o) -> p k b o", o=1).to_broadcast([P, KC, B, P])).then_inc(condB_ready.handle, 1)
                if L >= 2:
                    for name in ("qkv", "qkv2"):
                        o = BCOLS[L][name]
                        step.did(dve.tensor_scalar(BB[:, o:o + C], BB[:, o:o + C], QSC, None, ALU.mult))
                dve.wait_ge(prep_psum.handle, prep_psum.before(L, 1))
                step.did(dve.tensor_tensor(mod[:, :, 0:MOD[L]], S[0][:, 0:MOD[L] * B].rearrange("p (m b) -> p b m", b=B),
                                           SV[:, 0:MOD[L]].rearrange("p (o m) -> p o m", o=1).to_broadcast([P, B, MOD[L]]), ALU.add))
                step.wait()
                if L != 1:
                    v = mod[:, :, 0:MOD[L]].rearrange("p b (n s) -> p b n s", s=4)[:, :, :, 0:2]
                    dve.tensor_scalar(v, v, 1.0, None, ALU.add).then_inc(prep_read.handle, 1)
                else:
                    dve.engine_nop().then_inc(prep_read.handle, 1)
                for b in range(B if GATE[L] else 0):
                    dve.wait_ge(prep_psum.handle, prep_psum.before(L, b + 2))
                    bo = BCOLS[L]["gate"]
                    for g in range(0, GATE[L], 512):
                        hi = min(g + 512, GATE[L])
                        x = dve.tensor_tensor(gates[:, b, g:hi], S[1 + g // 512][:, 0:hi - g], BB[:, bo + g:bo + hi], ALU.add)
                        if hi < GATE[L]:
                            step.did(x)
                            step.wait()
                    x.then_inc(prep_read.handle, 1)
                dve.wait_ge(prep_read.handle, prep_read.before(L, 1 + (B if GATE[L] else 0)))
                step.reset()

            def ln(L, b, n, src, dst, mi, roll=0):
                step.wait()
                dve.sem_inc(passed, 1)
                for t in range(NT):
                    step.did(dve.bn_stats(st[:, t, :], src(t)))
                step.wait()
                for t in range(NT):
                    dve.bn_aggr(mv[:, t, :], st[:, t, :]).then_inc(stats_ready.handle, 1)
                dve.wait_ge(rstd_ready.handle, rstd_ready.at(L, b, n + 1))
                for t in range(NT):
                    dve.tensor_scalar(xn[:, t, :], src(t), mv[:, t, 0:1], rstd[:, 1, t:t + 1], ALU.subtract, ALU.mult).then_inc(xn_ready.handle, 1)
                dve.wait_ge(xT_psum.handle, xT_psum.at(L, b, n + 1))
                sc, sh = scale_shift(L, mi, 0)
                pieces = [(0, N, 0)] if not roll else [(roll, N, 0), (0, roll, N - roll)]
                for lo, hi, to in pieces:
                    o, s = dst[:, 0, to:to + hi - lo], A[0][:, lo:hi]
                    x = dve.tensor_copy(o, s) if sc is None else dve.tensor_scalar(o, s, sc, sh, ALU.mult, ALU.add)
                x.then_inc(xT_dve.handle, 1)

            def v_view(t):
                return vz[:, t, :, 0:D]

            def qkv(L, b, n):
                for t in range(NT):
                    i = NT * n + t
                    a, f, rem = A[t % 2], qkf[:, t % 2, :], left[:, t % 2, :]
                    dve.wait_ge(qk_psum.handle, qk_psum.at(L, b, i + 1))
                    if L == 0:
                        def heads4(ap):
                            return ap.rearrange("p (q h d) -> p q h d", q=2, d=D)
                        def table(s, lo, hi):
                            tb = rope[:, s, t, :, lo:hi].rearrange("p q (o d) -> p q o d", o=1)
                            return tb.to_broadcast([P, 2, H, hi - lo])
                        hd = D // 2
                        step.did(dve.tensor_tensor(heads4(f), heads4(a[:, :]), table(0, 0, D), ALU.mult))
                        step.did(dve.tensor_tensor(heads4(rem)[:, :, :, 0:hd], heads4(a[:, :])[:, :, :, hd:D], table(1, 0, hd), ALU.mult))
                        dve.tensor_tensor(heads4(rem)[:, :, :, hd:D], heads4(a[:, :])[:, :, :, 0:hd], table(1, hd, D), ALU.mult).then_inc(qk_read.handle, 1)
                    else:
                        bo = BCOLS[L]["qkv2" if n else "qkv"]
                        step.did(dve.scalar_tensor_tensor(out=f[:, 0:C], in0=a[:, 0:C], scalar=QSC, in1=BB[:, bo:bo + C], op0=ALU.mult, op1=ALU.add))
                        dve.tensor_tensor(f[:, C:2 * C], a[:, C:2 * C], BB[:, bo + C:bo + 2 * C], ALU.add).then_inc(qk_read.handle, 1)
                    dve.wait_ge(v_psum.handle, v_psum.at(L, b, i + 1))
                    sv = S[t % 2][:, 0:C].rearrange("p (h d) -> p h d", d=D)
                    if L == 0:
                        dve.tensor_copy(v_view(t), sv).then_inc(v_ready.handle, 1)
                    else:
                        bv = BB[:, bo + 2 * C:bo + 3 * C].rearrange("p (h d) -> p h d", d=D)
                        dve.tensor_tensor(v_view(t), sv, bv, ALU.add).then_inc(v_ready.handle, 1)
                    step.wait()
                    dve.wait_ge(qk_read.handle, qk_read.at(L, b, i + 1))
                    if L == 0:
                        step.did(dve.tensor_tensor(f, f, rem, ALU.add))
                        step.wait()
                    tok = qk_tok[:, t % 2, :, :].rearrange("p h (s d) -> p s h d", d=D)
                    f3, rem3 = (ap.rearrange("p (h d) -> p h d", d=D) for ap in (f, rem))
                    if t >= 2:
                        dve.wait_ge(stackT_psum.handle, stackT_psum.at(L, b, NT * 4 * n + 4 * (t - 1)))
                    dve.tensor_copy(tok[:, 0], f3).then_inc(parts_ready.handle, 1)
                    dve.wait_ge(parts_ready.handle, parts_ready.at(L, b, 2 * i + 1))
                    step.did(dve.tensor_tensor(rem3, f3, tok[:, 0], ALU.subtract))
                    step.wait()
                    dve.tensor_copy(tok[:, 1], rem3).then_inc(parts_ready.handle, 1)
                    dve.wait_ge(parts_ready.handle, parts_ready.at(L, b, 2 * i + 2))
                    step.did(dve.tensor_tensor(tok[:, 5, 0:H], rem3[:, 0:H], tok[:, 1, 0:H], ALU.subtract))
                    dve.tensor_tensor(tok[:, 4, H:2 * H], rem3[:, H:2 * H], tok[:, 1, H:2 * H], ALU.subtract).then_inc(stack_dve.handle, 1)
                    step.wait()

            def normalise(L, b, att, g, bank):
                dve.wait_ge(tok_psum.handle, tok_psum.at(L, b, H // G * att["n"] + g + 1))
                o = bank[:, :].rearrange("p (t r c) -> p t r c", t=NT, c=32)
                step.did(dve.reciprocal(rden[:, :, :], o[:, :, :, D]))
                step.wait()
                dst = xn[:, :, G * D * g:G * D * (g + 1)].rearrange("p t (r c) -> p t r c", c=D)
                dve.tensor_tensor(dst, o[:, :, :, 0:D], rden[:, :, :].rearrange("p t (r o) -> p t r o", o=1).to_broadcast([P, NT, G, D]),
                                  ALU.mult).then_inc(tok_ready.handle, 1)

            def finish(L, b, att):
                dve.wait_ge(atT_psum.handle, atT_psum.at(L, b, att["n"] + 1))
                pieces = [(0, N, 0)] if att["v"] != "window" else [(0, N - ROLL, ROLL), (N - ROLL, N, 0)]
                for lo, hi, to in pieces:
                    x = dve.tensor_copy(atT[:, 0, to:to + hi - lo], A[0][:, lo:hi])
                x.then_inc(atT_dve.handle, 1)

            def soft_attention(L, b, att):
                t0, n = att["t0"], att["n"]
                first = [T[1], A[1]]
                steps = NT * H // G

                def maxima(c):
                    g, t = c // NT, c % NT
                    for r in range(G):
                        i = G * c + r
                        dve.wait_ge(first_psum.handle, first_psum.at(L, b, t0 + i + 1))
                        m = (G * g + r) * NT + t
                        dve.tensor_reduce(nmax[:, m:m + 1], first[i % 2][:, :], AX.X, ALU.max, negate=True).then_inc(max_ready.handle, 1)

                def max_parts(g):
                    cols = slice(G * NT * g, G * NT * (g + 1))
                    dve.wait_ge(max_ready.handle, max_ready.at(L, b, t0 + G * NT * (g + 1)))
                    step.did(dve.tensor_copy(mparts[:, cols, 0], nmax[:, cols]))
                    step.wait()
                    step.did(dve.tensor_tensor(mrest[:, :], nmax[:, cols], mparts[:, cols, 0], ALU.subtract))
                    step.wait()
                    dve.tensor_copy(mparts[:, cols, 1], mrest[:, :]).then_inc(mparts_ready.handle, 1)

                def max_rows(g):
                    for half in range(2):
                        dve.wait_ge(mrow_psum.handle, mrow_psum.at(L, b, H // 2 * n + 2 * g + half + 1))
                        h = G * g + 2 * half
                        dve.tensor_copy(qkst[STACK:STACK + AUG, h:h + 2, :],
                                        Th[0][STACK:STACK + AUG, :].rearrange("p (h n) -> p h n", h=2)).then_inc(mrow_ready.handle, 1)

                for c in range(AHEAD):
                    maxima(c)
                    if c % NT == NT - 1:
                        max_parts(c // NT)
                    if c % NT == 0 and c:
                        max_rows(c // NT - 1)
                for s in range(steps + 2):
                    if s + AHEAD < steps:
                        maxima(s + AHEAD)
                        if (s + AHEAD) % NT == NT - 1:
                            max_parts((s + AHEAD) // NT)
                    if s + AHEAD <= steps and (s + AHEAD) % NT == 0:
                        max_rows((s + AHEAD) // NT - 1)
                    if s > NT and s % NT == 1:
                        normalise(L, b, att, s // NT - 1, T[0])
                finish(L, b, att)

            def attention(L, b, att):
                variant, t0 = att["v"], att["t0"]
                if variant == "soft":
                    return soft_attention(L, b, att)
                nt, per = NTILES[variant], PER[variant]
                ends = {group_end(per, g) + 2: g for g in range(H // G)} if variant != "one" else {}
                for i in range(nt + LAG + per + 3):
                    if i < nt:
                        s = S[i % NS]
                        dve.wait_ge(scores_ready.handle, scores_ready.at(L, b, t0 + i + 1))
                        if variant == "window":
                            s4 = s[:, :].rearrange("p (w k) -> p w k", w=NT)
                            step.did(dve.tensor_reduce(nmax[:, NT * i:NT * i + NT], s4, AX.X, ALU.max))
                            if i >= 2:
                                dve.wait_ge(exp_ready.handle, exp_ready.at(L, b, t0 + i - 1))
                            step.wait()
                            m = nmax[:, NT * i:NT * i + NT].rearrange("p (w o) -> p w o", o=1).to_broadcast([P, NT, P])
                            dve.tensor_tensor(rest[:, 0, i % 2, :].rearrange("p (w k) -> p w k", w=NT), s4, m, ALU.subtract).then_inc(max_ready.handle, 1)
                        elif variant == "topk":
                            r1, r2, tp = rest[:, 0, i % 2, :], rest[:, 1, i % 2, :], top[:, i % 2, :]
                            dve.sem_inc(passed, 1)
                            step.did(dve.max(tp[:, 0:8], s[:, :]))
                            step.wait()
                            step.did(dve.match_replace(r1, tp[:, 0:8], s[:, :], LOWEST))
                            dve.tensor_scalar(nmax[:, i:i + 1], tp[:, 0:1], -1.0, None, ALU.mult).then_inc(max_ready.handle, 1)
                            step.wait()
                            step.did(dve.max(tp[:, 8:16], r1))
                            if i >= 2:
                                dve.wait_ge(exp_ready.handle, exp_ready.at(L, b, t0 + i - 1))
                                dve.sem_inc(passed, 1)
                            step.wait()
                            dve.match_replace(r2, tp[:, 8:16], r1, LOWEST).then_inc(rest_ready.handle, 1)
                        else:
                            dve.tensor_reduce(nmax[:, i:i + 1], s[:, :], AX.X, ALU.max, negate=True).then_inc(max_ready.handle, 1)
                    j = i - 1
                    if variant == "one" and 0 <= j < nt:
                        dve.wait_ge(exp_ready.handle, exp_ready.at(L, b, t0 + j + 1))
                        dve.reciprocal(rsum[:, j:j + 1], ssum[:, j:j + 1]).then_inc(rsum_ready.handle, 1)
                    j = i - LAG
                    if 0 <= j < nt and n_ev(L, variant, j):
                        copy_probs(dve, L, b, att, j)
                    if j in ends:
                        normalise(L, b, att, ends[j], A[1])
                if variant != "one":
                    finish(L, b, att)

            def project_out(L, b, n):
                for t in range(NT):
                    dve.wait_ge(out_psum.handle, out_psum.at(L, b, NT * n + t + 1))
                    bias = BB[:, BCOLS[L]["o2" if n else "o"]:][:, 0:C] if L else None
                    gate = None
                    if L == 2 and n == 0:
                        gate = gates[:, b, 0:C]
                    if L == 3:
                        gate = gates[:, b, n * C:(n + 1) * C]
                    x = x_all[:, b * NT + t, :]
                    r = res[:, t % 2, :]
                    if bias is None:
                        dve.tensor_tensor(x, A[t % 2][:, 0:C], x, ALU.add).then_inc(out_read.handle, 1)
                        dve.wait_ge(out_read.handle, out_read.at(L, b, NT * n + t + 1))
                        continue
                    dve.tensor_tensor(r, A[t % 2][:, 0:C], bias, ALU.add).then_inc(out_read.handle, 1)
                    dve.wait_ge(out_read.handle, out_read.at(L, b, NT * n + t + 1))
                    if gate is not None:
                        step.did(dve.tensor_tensor(r, r, gate, ALU.mult))
                        step.wait()
                    step.did(dve.tensor_tensor(x, x, r, ALU.add))
                    step.wait()

            def ffn(L, b):
                if L == 3:
                    m1 = SCOLS[L]["m1"] + NH
                    for j in range(NH):
                        dve.wait_ge(hid_psum.handle, hid_psum.at(L, b, 2 * j + 2))
                        dve.wait_ge(sil_ready.handle, sil_ready.at(L, b, j + 1))
                        dve.scalar_tensor_tensor(out=hT[:, j, :], in0=A[1][:, :], scalar=SV[:, m1 + j:m1 + j + 1],
                                                 in1=sil[:, j % 2, :], op0=ALU.add, op1=ALU.mult).then_inc(hid_ready.handle, 1)
                for t in range(NT):
                    dve.wait_ge(ffn_psum.handle, ffn_psum.at(L, b, t + 1))
                    o = BCOLS[L]["m2"]
                    x = x_all[:, b * NT + t, :]
                    r = res[:, t % 2, :]
                    dve.tensor_tensor(r, T[t % 2][:, 0:C], BB[:, o:o + C], ALU.add).then_inc(ffn_read.handle, 1)
                    dve.wait_ge(ffn_read.handle, ffn_read.at(L, b, t + 1))
                    if L:
                        g = (1 if L == 2 else 2) * C
                        step.did(dve.tensor_tensor(r, r, gates[:, b, g:g + C], ALU.mult))
                        step.wait()
                    if t == NT - 1:
                        step.wait()
                        dve.tensor_tensor(x, x, r, ALU.add).then_inc(x_done.handle, 1)
                    else:
                        step.did(dve.tensor_tensor(x, x, r, ALU.add))
                        step.wait()

            def router_layer(b):
                L = 1
                for t in range(NT):
                    dve.wait_ge(v_psum.handle, v_psum.at(L, b, t + 1))
                    dve.tensor_copy(v1[:, t, :], T[t % 2][:, 0:C]).then_inc(v_ready.handle, 1)
                attention(L, b, ATT[1][0])
                dve.wait_ge(rl_psum.handle, rl_psum.at(L, b, 1))
                rl, rp = rlog[:, :, 0:E], rpr[:, :, 0:E]

                def over(ap, n=E):
                    return ap.rearrange("p (t o) -> p t o", o=1).to_broadcast([P, NT, n])
                step.did(dve.tensor_tensor(rl, S[0][:, 0:4 * NT].rearrange("p (t e) -> p t e", e=4)[:, :, 0:E],
                                           gates[:, bass.ds(b, 1), 0:E].to_broadcast([P, NT, E]), ALU.add))
                step.wait()
                step.did(dve.tensor_reduce(rsm[:, 0, :], rl, AX.X, ALU.max))
                step.wait()
                dve.tensor_tensor(rl, rl, over(rsm[:, 0, :]), ALU.subtract).then_inc(rl_shift.handle, 1)
                dve.wait_ge(rl_exp.handle, rl_exp.at(L, b, 1))
                step.did(dve.tensor_reduce(rsm[:, 0, :], rp, AX.X, ALU.add))
                step.wait()
                step.did(dve.reciprocal(rsm[:, 1, :], rsm[:, 0, :]))
                step.wait()
                step.did(dve.tensor_tensor(rp, rp, over(rsm[:, 1, :]), ALU.mult))
                step.wait()
                for e in range(E):
                    for t in range(NT):
                        bo = BCOLS[L]["e2"] + e * C
                        pe_ = rpr[:, t, e:e + 1]
                        if e == 0:
                            step.did(dve.tensor_scalar(routed[:, t, :], BB[:, bo:bo + C], pe_, None, ALU.mult))
                        else:
                            step.did(dve.scalar_tensor_tensor(out=routed[:, t, :], in0=BB[:, bo:bo + C], scalar=pe_, in1=routed[:, t, :], op0=ALU.mult, op1=ALU.add))
                    step.wait()
                for e in range(E):
                    for t in range(NT):
                        i = e * NT + t
                        dve.wait_ge(eo_psum.handle, eo_psum.at(L, b, i + 1))
                        if e:
                            dve.wait_ge(eo_read.handle, eo_read.at(L, b, i - NT + 1))
                        dve.scalar_tensor_tensor(out=routed[:, t, :], in0=T[t % 2][:, 0:C], scalar=rpr[:, t, e:e + 1],
                                                 in1=routed[:, t, :], op0=ALU.mult, op1=ALU.add).then_inc(eo_read.handle, 1)
                for t in range(NT):
                    i = E * NT + t
                    dve.wait_ge(eo_psum.handle, eo_psum.at(L, b, i + 1))
                    bo = BCOLS[L]["g2"]
                    dve.tensor_tensor(g1[:, t, :], T[t % 2][:, 0:C], BB[:, bo:bo + C], ALU.add).then_inc(eo_read.handle, 1)
                dve.wait_ge(roT_psum.handle, roT_psum.at(L, b, 1))
                step.did(dve.tensor_copy(roT[:, 0, :], A[0][:, :]))
                step.wait()
                dve.tensor_copy(roT[:, 1, :], A[1][:, :]).then_inc(roT_ready.handle, 1)
                for t in range(NT):
                    dve.wait_ge(out_psum.handle, out_psum.at(L, b, t + 1))
                    bo = BCOLS[L]["o"]
                    r = res[:, t % 2, :]
                    x = x_all[:, b * NT + t, :]
                    dve.tensor_tensor(r, A[t % 2][:, 0:C], BB[:, bo:bo + C], ALU.add).then_inc(out_read.handle, 1)
                    dve.wait_ge(out_read.handle, out_read.at(L, b, t + 1))
                    dve.wait_ge(gate_ready.handle, gate_ready.at(L, b, t + 1))
                    step.did(dve.tensor_tensor(r, r, g1[:, t, :], ALU.mult))
                    step.wait()
                    if t == NT - 1:
                        dve.tensor_tensor(x, x, r, ALU.add).then_inc(x_done.handle, 1)
                    else:
                        step.did(dve.tensor_tensor(x, x, r, ALU.add))
                        step.wait()

            dve.wait_ge(first_in, 16 * 6)
            dve.wait_ge(consts, 7)
            dve.wait_ge(cond_ready, 1)
            for L in range(LAYERS):
                prepare(L)
                with dve.Fori(0, B) as b:
                    def x_tile(t):
                        return x_all[:, b * NT + t, :]
                    dve.tensor_copy(modc[:, 0:MOD[L]], mod[:, b, 0:MOD[L]]).then_inc(modc_ready.handle, 1)
                    dve.wait_ge(modc_ready.handle, modc_ready.at(L, b, 1))
                    ln(L, b, 0, x_tile, xnT, 0, roll=ROLL if L == 3 else 0)
                    if L == 1:
                        router_layer(b)
                    else:
                        qkv(L, b, 0)
                        attention(L, b, ATT[L][0])
                        project_out(L, b, 0)
                        ln(L, b, 1, x_tile, xnT, None if L == 2 else 1)
                        if L == 2:
                            dve.wait_ge(cx_loaded.handle, cx_loaded.at(L, b, 1))
                            ln(L, b, 2, lambda t: cxt[:, t, :], cnT, None)
                        qkv(L, b, 1)
                        attention(L, b, ATT[L][1])
                        project_out(L, b, 1)
                        ln(L, b, lns[L] - 1, x_tile, xnT, 1 if L == 2 else 2)
                        ffn(L, b)
                    step.wait()
                    dve.wait_ge(x_done.handle, x_done.at(L, b, 1))
                    step.reset(waited=True)


def kernel(**inputs):
    import numpy as _np
    import concourse.bacc as _bacc
    from concourse import mybir as _mybir
    from concourse.bass_utils import run_bass_kernel_spmd as _run

    g = {k: _np.asarray(v) for k, v in inputs.items()}

    def t(name):
        return g[name]

    def cm(a):
        r, c = a.shape
        return a.reshape(r // P, P, c).transpose(1, 0, 2).reshape(P, -1)

    def cv(v):
        return v.reshape(-1, P).T

    def cat(parts):
        return _np.ascontiguousarray(_np.concatenate(parts, axis=1))

    def row(parts):
        return _np.ascontiguousarray(_np.concatenate([p.reshape(-1) for p in parts]).reshape(1, -1))

    a = {"x": _np.ascontiguousarray(t("x"))}
    a["ctx"] = _np.ascontiguousarray(t("ctx_1024").reshape(B * NT, P, C))
    a["ctxT"] = _np.ascontiguousarray(t("ctx_1024").transpose(0, 2, 1).reshape(B * KC, P, N))
    a["condT"] = _np.ascontiguousarray(t("cond_1024").T.reshape(KC, P, B).transpose(1, 0, 2))
    half = D // 2
    f32 = _np.float32
    inv = (f32(1.0) / _np.power(f32(10000.0), _np.arange(half, dtype=f32) / f32(half))).astype(f32)
    ang = (_np.arange(N, dtype=f32)[:, None] * inv[None, :]).astype(f32)
    cos, sin = _np.cos(ang), _np.sin(ang)
    tab = _np.stack([_np.concatenate([cos, cos], 1), _np.concatenate([-sin, sin], 1)])
    tab = _np.stack([tab * f32(QSC), tab], 2).astype(f32)
    a["rope"] = _np.ascontiguousarray(tab.reshape(2, NT, P, 2, D).transpose(2, 0, 1, 3, 4).reshape(P, -1))

    L0, L1, L2, L3 = (f"L{i}_xcond_" for i in range(4))
    qkv = t(L0 + "qkv_w").T
    a["w0"] = cat([cm(qkv[:, 0:C]), cm(qkv[:, C:2 * C]), cm(qkv[:, 2 * C:]), cm(t(L0 + "sa_out_w").T), cm(t(L0 + "q_w").T), cm(t(L0 + "k_w").T),
                   cm(t(L0 + "v_w").T), cm(t(L0 + "ca_out_w").T), cm(t(L0 + "ffn_w1").T), cm(t(L0 + "ffn_w2").T)])
    a["pw0"] = cat([cm(_np.concatenate([t(L0 + f"ln{i}_w").T for i in (1, 2, 3)], axis=1))])
    a["bb0"] = row([t(L0 + "ffn_b2")])
    a["sv0"] = cat([cv(t(L0 + f"ln{i}_b")) for i in (1, 2, 3)] + [cv(t(L0 + "ffn_b1"))])

    e1, g1w, rw = t(L1 + "e_w1"), t(L1 + "gate_w1"), t(L1 + "router_W")
    a["w1"] = cat([cm(t(L1 + "Wq")), cm(t(L1 + "Wk")), cm(t(L1 + "Wv"))] + [cm(e1[e, 0:2 * C]) for e in range(E)]
                  + [cm(t(L1 + "e_w2")[e]) for e in range(E)] + [cm(g1w[0:2 * C]), cm(t(L1 + "gate_w2")), cm(t(L1 + "out_w")), cm(rw[0:2 * C])])
    a["pw1"] = cat([cm(_np.concatenate([e1[e, 2 * C:] for e in range(E)] + [g1w[2 * C:], rw[2 * C:]], axis=1))])
    a["bb1"] = row([t(L1 + "e_b2"), t(L1 + "gate_b2"), t(L1 + "out_b"), t(L1 + "router_b")])
    a["sv1"] = cat([cv(t(L1 + "e_b1").reshape(-1)), cv(t(L1 + "gate_b1")), cv(t(L1 + "ln_gamma")), cv(t(L1 + "ln_beta"))])

    def cols(m, order):
        return _np.concatenate([m[..., i * C:(i + 1) * C] for i in order], axis=-1)

    wq, kv = t(L2 + "W_qkv"), t(L2 + "W_kvc")
    a["w2"] = cat([cm(wq[:, 0:C]), cm(wq[:, C:2 * C]), cm(wq[:, 2 * C:]), cm(t(L2 + "W_proj")), cm(t(L2 + "W_qc")), cm(kv[:, 0:C]), cm(kv[:, C:]),
                   cm(t(L2 + "W_cproj")), cm(t(L2 + "W_mlp1")), cm(t(L2 + "W_mlp2"))])
    a["pw2"] = cat([cm(cols(t(L2 + "W_mod"), (1, 0, 4, 3, 2, 5)))])
    bm = t(L2 + "b_mod")
    a["bb2"] = row([t(L2 + "b_qkv"), t(L2 + "b_qc"), t(L2 + "b_kvc"), t(L2 + "b_proj"), t(L2 + "b_cproj"), t(L2 + "b_mlp2"), cols(bm, (2, 5))])
    a["sv2"] = cat([cv(cols(bm, (1, 0, 4, 3))), cv(t(L2 + "b_mlp1"))])

    wq, kv = t(L3 + "w_qkv"), t(L3 + "w_kv")
    a["w3"] = cat([cm(wq[:, 0:C]), cm(wq[:, C:2 * C]), cm(wq[:, 2 * C:]), cm(t(L3 + "w_so")), cm(t(L3 + "w_q")), cm(kv[:, 0:C]), cm(kv[:, C:]),
                   cm(t(L3 + "w_co")), cm(t(L3 + "w_m1")), cm(t(L3 + "w_m2"))])
    a["pw3"] = cat([cm(cols(t(L3 + "w_ada"), (1, 0, 4, 3, 7, 6, 2, 5, 8)))])
    bm = t(L3 + "b_ada")
    a["bb3"] = row([t(L3 + "b_qkv"), t(L3 + "b_q"), t(L3 + "b_kv"), t(L3 + "b_so"), t(L3 + "b_co"), t(L3 + "b_m2"), cols(bm, (2, 5, 8))])
    a["sv3"] = cat([cv(cols(bm, (1, 0, 4, 3, 7, 6))), cv(t(L3 + "b_m1"))])

    nc = _bacc.Bacc("TRN2", target_bir_lowering=False, num_devices=1)
    ins = {k: nc.dram_tensor(f"in_{k}", v.shape, _mybir.dt.from_np(v.dtype), kind="ExternalInput").ap() for k, v in a.items()}
    out = nc.dram_tensor("out_0", (B * NT, P, C), _mybir.dt.float32, kind="ExternalOutput").ap()
    four_layers(nc, ins, out)
    r = _run(nc, [{f"in_{k}": v for k, v in a.items()}], core_ids=[0])
    return r.results[0]["out_0"].reshape(B, N, C)
```

```python
import numpy as np
import concourse.bass as bass
from concourse import mybir
from contextlib import ExitStack

F32 = mybir.dt.float32
BF16 = mybir.dt.bfloat16
ACT = mybir.ActivationFunctionType
ALU = mybir.AluOpType
AX = mybir.AxisListType

P = 128
B = 4
N = 512
C = 256
KC = C // P
NT = N // P
H = 16
D = C // H
HID = 1024
NH = HID // P
E = 3
RH = 2 * C
NR = RH // P
ROLL = 64
STACK = 6 * D
QSC = D ** -0.5
QSC1 = C ** -0.5
LOWEST = -3.0e38
NS = 3
LAG = 3
G = 4
TLAG = 2
AHEAD = 5
EIGHT = [0, 2, 1, 3]
ROWS = [1, 3]
AUG = 2
U = KC * C

WCOLS = [dict(q=0, k=U, v=2 * U, o=3 * U, q2=4 * U, k2=5 * U, v2=6 * U, o2=7 * U, w1=8 * U, w2=12 * U, end=16 * U)] * 4
WCOLS = [dict(w) for w in WCOLS]
WCOLS[1] = dict(q=0, k=U, v=2 * U, e1=3 * U, e2=15 * U, g1=21 * U, g2=23 * U, o=24 * U, r=25 * U, end=25 * U + 4 * E)
WCOLS[3] = dict(WCOLS[0], w2=16 * U, end=20 * U)
WMAX = max(w["end"] for w in WCOLS)
EARLY = [8 * U, 8 * U, 3 * U, 8 * U]
MOD = [12, 14, 8, 12]
GATE = [0, E, 2 * C, 3 * C]
BCOLS = [dict(m2=0, end=C),
         dict(e2=0, g2=E * C, o=(E + 1) * C, gate=(E + 2) * C, end=(E + 2) * C + E),
         dict(qkv=0, qkv2=3 * C, o=6 * C, o2=7 * C, m2=8 * C, gate=9 * C, end=11 * C),
         dict(qkv=0, qkv2=3 * C, o=6 * C, o2=7 * C, m2=8 * C, gate=9 * C, end=12 * C)]
BMAX = max(w["end"] for w in BCOLS)
SCOLS = [dict(mod=0, m1=12, end=20), dict(mod=0, ln=14, end=18), dict(mod=0, m1=8, end=16), dict(mod=0, m1=12, end=28)]
SMAX = max(w["end"] for w in SCOLS)
LAYERS = 4
EPS = [1e-5, 1e-5, 1e-6, 1e-6]


class Progress:

    def __init__(self, handle, per, pre=(0, 0, 0, 0), start=0, unit=1):
        self.handle, self.per, self.pre, self.start, self.unit = handle, per, pre, start, unit

    def base(self, L):
        return self.start + sum(self.pre[i] + B * self.per[i] for i in range(L))

    def before(self, L, k):
        return (self.base(L) + k) * self.unit

    def at(self, L, b, k):
        if b is None:
            return self.before(L, k)
        return b * (self.per[L] * self.unit) + (self.base(L) + self.pre[L] + k) * self.unit


class Steps:

    def __init__(self, eng, handle):
        self.eng, self.handle, self.n = eng, handle, 0

    def did(self, ins):
        self.n += 1
        ins.then_inc(self.handle, 1)

    def wait(self):
        if self.n:
            self.eng.wait_ge(self.handle, self.n)

    def reset(self):
        if self.n:
            self.eng.wait_ge(self.handle, self.n)
            self.eng.sem_clear(self.handle)
            self.n = 0


def four_layers(nc, ins, out):
    ctx = ExitStack()
    with ctx:
        def sb(name, shape, dt=F32):
            return ctx.enter_context(nc.sbuf_tensor(name, shape, dt))

        def sem(name):
            return ctx.enter_context(nc.semaphore(name))

        x_all = sb("x_all", [P, (B + 1) * NT, C])
        W = sb("W", [P, WMAX])
        BB = sb("BB", [P, BMAX])
        SV = sb("SV", [P, SMAX])
        mod = sb("mod", [P, B + 1, max(MOD)])
        modc = sb("modc", [P, max(MOD)])
        gates = sb("gates", [P, B, max(GATE)])
        stk = sb("stk", [P, 2 * H * N // 2])
        qkst = stk[:, :].bitcast(BF16).rearrange("p (h n) -> p h n", h=2 * H)
        qk_tok = sb("qk_tok", [P, 2, 2 * H, STACK], BF16)
        tmp = sb("tmp", [P, 8 * C])
        qkf = tmp[:, 0:4 * C].rearrange("p (i n) -> p i n", i=2)
        left = tmp[:, 4 * C:8 * C].rearrange("p (i n) -> p i n", i=2)
        rest = tmp[:, 0:8 * C].rearrange("p (a i n) -> p a i n", a=2, i=2)
        vz = sb("vz", [P, NT, H, 32])
        xn = sb("xn", [P, NT, C])
        xnT = sb("xnT", [P, KC, N])
        cx = sb("cx", [P, KC * N])
        cxT = cx[:, :].rearrange("p (k n) -> p k n", k=KC)
        cxt = cx[:, :].rearrange("p (t c) -> p t c", t=NT)
        atT = sb("atT", [P, KC, N])
        probs = sb("probs", [P, 2, N])
        probs2 = sb("probs2", [P, 2, N])
        cnT = probs2[:, :, :]
        pn = sb("pn", [P, 3, N])
        pT = sb("pT", [P, 2, NT, N])
        hT = pT[:, :, :, :].rearrange("p a t n -> p (a t) n")
        mparts = sb("mparts", [P, H * NT, AUG], BF16)
        ou = atT[:, :, :]
        rden = sb("rden", [P, NT, G])
        condB = hT[:, 0:2, :].rearrange("p k (b n) -> p k b n", b=B)
        top = sb("top", [P, 2, 16])
        nmax = sb("nmax", [P, H * NT])
        ssum = sb("ssum", [P, NT])
        rsum = sb("rsum", [P, NT])
        st = sb("st", [P, NT, 6])
        mv = sb("mv", [P, NT, 2])
        rstd = sb("rstd", [P, 2, NT])
        mhalf = sb("mhalf", [P, NT])
        sil = probs[:, :, :]
        res = sb("res", [P, 2, C])
        rlog = sb("rlog", [P, NT, 4])
        rpr = sb("rpr", [P, NT, 4])
        rsm = sb("rsm", [P, 2, NT])
        condT = sb("condT", [P, KC, B])
        condS = sb("condS", [P, KC, B])
        rope = sb("rope", [P, 2, NT, 2, D])
        ident = sb("ident", [P, P])
        identh = sb("identh", [P, P], BF16)
        def part(i):
            return stk[:, i * KC * N:(i + 1) * KC * N]
        q1T = part(0).rearrange("p (k n) -> p k n", k=KC)
        k1T = part(1).rearrange("p (k n) -> p k n", k=KC)
        v1 = part(2).rearrange("p (t c) -> p t c", t=NT)
        routed = part(3).rearrange("p (t c) -> p t c", t=NT)
        roT = part(4).rearrange("p (k n) -> p k n", k=KC)
        g1 = part(5).rearrange("p (t c) -> p t c", t=NT)

        def bank(name):
            return ctx.enter_context(nc.psum_tensor(name, [P, N], F32))
        S = [bank(f"S{i}") for i in range(NS)]
        T = [bank(f"T{i}") for i in range(2)]
        Th = [t[:, :].bitcast(BF16) for t in T]
        A = [bank(f"A{i}") for i in range(2)]
        O = bank("O")
        OB = [O, A[0]]
        STB = [Th[0], Th[1], Th[0], O[:, :].bitcast(BF16)]

        def prog(name, per, pre=(0, 0, 0, 0), start=0, unit=1):
            return Progress(sem(name), per, pre, start, unit)
        tiles = [2 * 64, 4, 2 * 64, H + 64]
        soft = [2 * 64, 0, 2 * 64, 0]
        other = [0, 4, 0, H + 64]
        atts = [2, 0, 2, 2]
        lns = [3, 1, 4, 3]
        qkvs = [2, 0, 2, 2]
        loaded = prog("loaded", [0] * 4, [3] * 4, unit=16)
        w_loaded = prog("w_loaded", [0] * 4, [1] * 4, unit=16)
        w_rest = prog("w_rest", [0] * 4, [1] * 4, unit=16)
        first_in = sem("first_in")
        rows_in = sem("rows_in")
        consts = sem("consts")
        cond_ready = sem("cond_ready")
        condB_ready = prog("condB_ready", [0] * 4, [1 if g else 0 for g in GATE])
        prep_psum = prog("prep_psum", [0] * 4, [1 + (B if g else 0) for g in GATE])
        prep_read = prog("prep_read", [0] * 4, [1 + (B if g else 0) for g in GATE])
        modc_ready = prog("modc_ready", [1] * 4, [1] * 4)
        cx_loaded = prog("cx_loaded", [1] * 4, unit=16)
        cx_used = prog("cx_used", [1] * 4, start=1)
        stats_ready = prog("stats_ready", [NT * n for n in lns], [NT] * 4)
        rstd_ready = prog("rstd_ready", lns, [1] * 4)
        xn_ready = prog("xn_ready", [NT * n for n in lns], [NT] * 4)
        xT_psum = prog("xT_psum", lns, [1] * 4)
        xT_dve = prog("xT_dve", lns, [1] * 4)
        xT_act = prog("xT_act", lns, [1] * 4)
        qk_psum = prog("qk_psum", [NT * n for n in qkvs])
        qk_read = prog("qk_read", [NT * n for n in qkvs])
        v_psum = prog("v_psum", [NT * 2, NT, NT * 2, NT * 2])
        v_ready = prog("v_ready", [NT * 2, NT, NT * 2, NT * 2])
        parts_ready = prog("parts_ready", [2 * NT * n for n in qkvs])
        stack_dve = prog("stack_dve", [NT * n for n in qkvs])
        stack_pool = prog("stack_pool", [NT * n for n in qkvs])
        stackT_psum = prog("stackT_psum", [4 * NT * n for n in qkvs])
        stackT_ready = prog("stackT_ready", [4 * NT * n for n in qkvs])
        scores_ready = prog("scores_ready", other)
        first_psum = prog("first_psum", soft)
        second_psum = prog("second_psum", soft)
        max_ready = prog("max_ready", tiles)
        mparts_ready = prog("mparts_ready", [H // G * n if s_ else 0 for n, s_ in zip(atts, soft)])
        mrow_psum = prog("mrow_psum", [H // 2 * n if s_ else 0 for n, s_ in zip(atts, soft)])
        mrow_ready = prog("mrow_ready", [H // 2 * n if s_ else 0 for n, s_ in zip(atts, soft)])
        ones_ready = prog("ones_ready", [0] * 4, [1, 0, 1, 0])
        exp_ready = prog("exp_ready", tiles)
        rest_ready = prog("rest_ready", [0, 0, 0, 64])
        rsum_ready = prog("rsum_ready", [0, 4, 0, 0])
        pn_ready = prog("pn_ready", [0, 4, 0, 64])
        pT_psum = prog("pT_psum", other)
        pT_dve = prog("pT_dve", [0, 2, 0, H // 2])
        pT_act = prog("pT_act", [0, 2, 0, H // 2 + 64])
        pv_done = prog("pv_done", [2 * 64, KC, 2 * 64, 2 * H])
        ou_ready = prog("ou_ready", [H // G * n for n in atts])
        tok_psum = prog("tok_psum", [H // G * n for n in atts])
        tok_ready = prog("tok_ready", [H // G * n for n in atts])
        atT_psum = prog("atT_psum", atts)
        atT_dve = prog("atT_dve", atts)
        atT_act = prog("atT_act", [2, 2, 2, 2])
        out_psum = prog("out_psum", [2 * NT, NT, 2 * NT, 2 * NT])
        out_read = prog("out_read", [2 * NT, NT, 2 * NT, 2 * NT])
        hid_psum = prog("hid_psum", [NH, 0, NH, 2 * NH])
        hid_ready = prog("hid_ready", [NH, 0, NH, NH])
        sil_ready = prog("sil_ready", [0, 0, 0, NH])
        ffn_psum = prog("ffn_psum", [NT, 0, NT, NT])
        ffn_read = prog("ffn_read", [NT, 0, NT, NT])
        qk1_psum = prog("qk1_psum", [0, 2 * KC, 0, 0])
        qk1_ready = prog("qk1_ready", [0, 2 * KC, 0, 0])
        rl_psum = prog("rl_psum", [0, 1, 0, 0])
        rl_shift = prog("rl_shift", [0, 1, 0, 0])
        rl_exp = prog("rl_exp", [0, 1, 0, 0])
        eh_psum = prog("eh_psum", [0, E * NR + KC, 0, 0])
        eh_ready = prog("eh_ready", [0, E * NR + KC, 0, 0])
        eo_psum = prog("eo_psum", [0, (E + 1) * NT, 0, 0])
        eo_read = prog("eo_read", [0, (E + 1) * NT, 0, 0])
        gate_ready = prog("gate_ready", [0, NT, 0, 0])
        roT_psum = prog("roT_psum", [0, 1, 0, 0])
        roT_ready = prog("roT_ready", [0, 1, 0, 0])
        x_done = prog("x_done", [1] * 4)
        stored = sem("stored")
        passed = sem("passed")
        dve_step, pool_step = sem("dve_step"), sem("pool_step")

        block = ctx.enter_context(nc.Block())

        def w(L, name, k, lo=0, hi=C, width=C):
            o = WCOLS[L][name] + k * width
            return W[:, o + lo:o + hi]

        def n_ev(L, variant, j):
            return variant != "topk" and j % 2 == 0

        def evs(variant, j):
            return (0, j) if variant == "topk" else ((j + 1) // 2, j // 2)

        def att(v, n, t0=0, n0=0, h0=0, d0=0, a0=0):
            return dict(v=v, n=n, t0=t0, n0=n0, h0=h0, d0=d0, a0=a0)
        ATT = [
            [att("soft", 0), att("soft", 1, t0=64, h0=64)],
            [att("one", 0)],
            [att("soft", 0), att("soft", 1, t0=64, h0=64)],
            [att("window", 0), att("topk", 1, t0=H, h0=H, d0=H // 2, a0=H // 2)],
        ]
        NTILES = dict(topk=64, one=4, window=H)
        PER = dict(topk=NT, one=NT, window=1)

        def group_end(per, g):
            return G * per * (g + 1) + per

        def scale_shift(L, mi, half):
            if mi is None:
                return None, None
            if L == 1:
                o = SCOLS[1]["ln"]
                return SV[:, o + half:o + half + 1], SV[:, o + 2 + half:o + 3 + half]
            return modc[:, 4 * mi + half:4 * mi + half + 1], modc[:, 4 * mi + 2 + half:4 * mi + 3 + half]

        def copy_probs(eng, L, b, att, j):
            variant, per = att["v"], PER[att["v"]]
            h = j // per
            eng.wait_ge(pT_psum.handle, pT_psum.at(L, b, att["t0"] + j + 1))
            if h >= 2:
                eng.wait_ge(pv_done.handle, pv_done.at(L, b, att["h0"] + h - 1))
            src = T[j % 2][:, :].rearrange("p (k q) -> p k q", k=NT)
            q = (j % per) * P
            dst = pT[:, h % 2, :, q:q + P]
            if n_ev(L, variant, j):
                eng.tensor_copy(dst, src).then_inc(pT_dve.handle, 1)
            else:
                eng.activation(dst, src, ACT.Copy).then_inc(pT_act.handle, 1)

        @block.sync
        def _(sp):
            def load_row(t):
                return sp.dma_start(x_all[:, t * NT:(t + 1) * NT, :], ins["x"][t].rearrange("(t p) c -> p t c", p=P))
            load_row(0).then_inc(first_in, 16)
            sp.dma_start(condT[:, :, :], ins["condT"]).then_inc(first_in, 16)
            sp.dma_start(rope[:, :, :, :, :].rearrange("p a t q d -> p (a t q d)"), ins["rope"]).then_inc(first_in, 16)
            sp.sem_inc(cx_used.handle, 1)
            for L in range(LAYERS):
                pw = KC * (MOD[L] * P + GATE[L])
                first = EARLY[L]
                if L in (1, 3):
                    sp.wait_ge(out_psum.handle, out_psum.at(L - 1, B - 1, 2 * NT))
                if L == 2:
                    sp.wait_ge(pv_done.handle, pv_done.at(1, B - 1, KC))
                    sp.dma_start(W[:, 0:first], ins["w2"][:, 0:first]).then_inc(w_loaded.handle, 16)
                    sp.wait_ge(x_done.handle, x_done.at(1, B - 1, 1))
                sp.dma_start(stk[:, 0:pw], ins[f"pw{L}"]).then_inc(loaded.handle, 16)
                if L in (1, 3):
                    sp.dma_start(W[:, 0:first], ins[f"w{L}"][:, 0:first]).then_inc(w_loaded.handle, 16)
                    sp.wait_ge(x_done.handle, x_done.at(L - 1, B - 1, 1))
                if L == 2:
                    sp.wait_ge(xT_dve.handle, xT_dve.at(1, B - 1, lns[1]))
                    sp.wait_ge(xT_act.handle, xT_act.at(1, B - 1, lns[1]))
                sp.dma_start(SV[:, 0:SCOLS[L]["end"]], ins[f"sv{L}"]).then_inc(loaded.handle, 16)
                sp.dma_start(BB[:, 0:BCOLS[L]["end"]], ins[f"bb{L}"].to_broadcast([P, BCOLS[L]["end"]])).then_inc(loaded.handle, 16)
                if L == 0:
                    sp.dma_start(W[:, 0:first], ins["w0"][:, 0:first]).then_inc(w_loaded.handle, 16)
                    for t in range(1, B):
                        load_row(t).then_inc(rows_in, 16)
                sp.dma_start(W[:, first:WCOLS[L]["end"]], ins[f"w{L}"][:, first:WCOLS[L]["end"]]).then_inc(w_rest.handle, 16)
                with sp.Fori(0, B) as b:
                    sp.wait_ge(cx_used.handle, cx_used.at(L, b, 0))
                    if L == 2:
                        sp.dma_start(cxt, ins["ctx"][bass.ds(b * NT, NT)].rearrange("t p c -> p t c")).then_inc(cx_loaded.handle, 16)
                    else:
                        sp.dma_start(cxT, ins["ctxT"][bass.ds(b * KC, KC)].rearrange("k p n -> p k n")).then_inc(cx_loaded.handle, 16)
                    if L == LAYERS - 1:
                        sp.wait_ge(x_done.handle, x_done.at(L, b, 1))
                        sp.dma_start(out[bass.ds(b * NT, NT)].rearrange("t p c -> p t c"),
                                     x_all[:, bass.ds(b * NT, NT), :]).then_inc(stored, 16)
            sp.wait_ge(stored, 16 * B)

        @block.gpsimd
        def _(pool):
            pool.memset(ident[:, :], 0.0).then_inc(consts, 1)
            pool.memset(identh[:, :], 0.0).then_inc(consts, 1)
            pool.memset(mhalf[:, :], -0.5).then_inc(consts, 1)
            pool.memset(vz[:, :, :, :], 0.0).then_inc(consts, 1)
            pool.memset(x_all[:, B * NT:(B + 1) * NT, :], 0.0).then_inc(consts, 1)
            pool.memset(mod[:, B, :], 0.0).then_inc(consts, 1)
            pool.wait_ge(consts, 6)
            pool.memset(vz[:, :, :, D:D + 1], 1.0).then_inc(consts, 1)
            for m in (ident, identh):
                pool.affine_select(out=m[:, :], in_=m[:, :], compare_op=ALU.not_equal, fill=1.0, base=0,
                                   pattern=[[-1, P]], channel_multiplier=1).then_inc(consts, 1)
            step = Steps(pool, pool_step)

            def ln(L, b, n):
                pool.wait_ge(stats_ready.handle, stats_ready.at(L, b, NT * n))
                pool.sem_inc(passed, 1)
                step.did(pool.tensor_scalar(rstd[:, 0, :], mv[:, :, 1], EPS[L], None, ALU.add))
                step.wait()
                pool.tensor_tensor(rstd[:, 1, :], rstd[:, 0, :], mhalf[:, :], ALU.pow).then_inc(rstd_ready.handle, 1)

            def stacks(L, b, n):
                for t in range(NT):
                    i = NT * n + t
                    q, k = (qk_tok[:, t % 2, h0:h0 + H, :].rearrange("p h (s d) -> p s h d", d=D) for h0 in (0, H))
                    two = [P, 2, H, D]
                    pool.wait_ge(parts_ready.handle, parts_ready.at(L, b, 2 * i + 1))
                    pool.sem_inc(passed, 1)
                    step.did(pool.tensor_scalar(q[:, 2:6:2], q[:, 0:1].to_broadcast(two), 1.0, 1.0, ALU.mult, ALU.mult))
                    step.did(pool.tensor_scalar(k[:, 3:6:2], k[:, 0:1].to_broadcast(two), 1.0, 1.0, ALU.mult, ALU.mult))
                    pool.wait_ge(parts_ready.handle, parts_ready.at(L, b, 2 * i + 2))
                    pool.sem_inc(passed, 1)
                    step.did(pool.tensor_scalar(q[:, 3], q[:, 1], 1.0, 1.0, ALU.mult, ALU.mult))
                    step.did(pool.tensor_scalar(k[:, 2], k[:, 1], 1.0, 1.0, ALU.mult, ALU.mult))
                    step.wait()
                    pool.sem_inc(stack_pool.handle, 1)

            def attention(L, b, att):
                variant, t0, n0 = att["v"], att["t0"], att["n0"]
                if variant in ("soft", "window"):
                    return
                for i in range(NTILES[variant]):
                    if i >= 3:
                        pool.wait_ge(pT_psum.handle, pT_psum.at(L, b, t0 + i - 2))
                    if variant == "topk":
                        pool.wait_ge(exp_ready.handle, exp_ready.at(L, b, t0 + i + 1))
                        pool.tensor_tensor(pn[:, i % 3, :], probs[:, i % 2, :], probs2[:, i % 2, :], ALU.subtract).then_inc(pn_ready.handle, 1)
                    else:
                        pool.wait_ge(rsum_ready.handle, rsum_ready.at(L, b, t0 + i + 1))
                        pool.sem_inc(passed, 1)
                        pool.tensor_scalar(pn[:, i % 3, :], probs[:, i % 2, :], rsum[:, i:i + 1], 1.0, ALU.mult, ALU.mult).then_inc(pn_ready.handle, 1)

            for L in range(LAYERS):
                ln(L, None, 1)
                step.reset()
                if L in (0, 2):
                    pool.wait_ge(prep_read.handle, prep_read.before(L, 1 + (B if GATE[L] else 0)))
                    pool.memset(qkst[STACK:STACK + AUG, H:2 * H, :], 1.0).then_inc(ones_ready.handle, 1)
                    pool.wait_ge(ones_ready.handle, ones_ready.before(L, 1))
                with pool.Fori(0, B) as b:
                    for a, att in enumerate(ATT[L]):
                        if a:
                            ln(L, b, 1)
                        if L == 2 and a == 1:
                            ln(L, b, 2)
                        if L != 1:
                            stacks(L, b, a)
                        attention(L, b, att)
                    if L != 1:
                        ln(L, b, lns[L] - 1)
                    ln(L, b, lns[L])
                    step.reset()

        @block.scalar
        def _(act):
            act.wait_ge(first_in, 16 * 3)
            act.activation(condS[:, :, :], condT[:, :, :], ACT.Silu).then_inc(cond_ready, 1)

            def ln(L, b, n, dst, mi, roll=0):
                act.wait_ge(xT_psum.handle, xT_psum.at(L, b, n))
                sc, sh = scale_shift(L, mi, 1)
                pieces = [(0, N, 0)] if not roll else [(roll, N, 0), (0, roll, N - roll)]
                for i, (lo, hi, to) in enumerate(pieces):
                    o, s = dst[:, 1, to:to + hi - lo], A[1][:, lo:hi]
                    if sc is None:
                        x = act.activation(o, s, ACT.Copy)
                    else:
                        x = act.activation(o, s, ACT.Identity, bias=sh, scale=sc)
                x.then_inc(xT_act.handle, 1)

            def stacks(L, b, n):
                for t in range(NT):
                    for j in range(4):
                        i = NT * 4 * n + 4 * t + j
                        act.wait_ge(stackT_psum.handle, stackT_psum.at(L, b, i + 1))
                        h = 8 * EIGHT[j]
                        act.activation(qkst[0:STACK, h:h + 8, t * P:(t + 1) * P],
                                       STB[j][0:STACK, :].rearrange("p (h n) -> p h n", h=8), ACT.Copy).then_inc(stackT_ready.handle, 1)

            def finish(L, b, att):
                act.wait_ge(atT_psum.handle, atT_psum.at(L, b, att["n"] + 1))
                pieces = [(0, N, 0)] if att["v"] != "window" else [(0, N - ROLL, ROLL), (N - ROLL, N, 0)]
                for lo, hi, to in pieces:
                    x = act.activation(atT[:, 1, to:to + hi - lo], A[1][:, lo:hi], ACT.Copy)
                x.then_inc(atT_act.handle, 1)

            def group_out(L, b, att, g, count):
                act.wait_ge(pv_done.handle, pv_done.at(L, b, att["h0"] + count))
                if g >= 2:
                    act.wait_ge(tok_psum.handle, tok_psum.at(L, b, H // G * att["n"] + g - 1))
                act.activation(ou[:, g % 2, :], OB[g % 2][:, :], ACT.Copy).then_inc(ou_ready.handle, 1)

            def soft_attention(L, b, att):
                t0, h0 = att["t0"], att["h0"]
                for s in range(NT * H // G + 1):
                    if s < NT * H // G:
                        for r in range(G):
                            i = G * s + r
                            if i >= 8:
                                act.wait_ge(pv_done.handle, pv_done.at(L, b, h0 + i - 7))
                            act.wait_ge(second_psum.handle, second_psum.at(L, b, t0 + i + 1))
                            act.activation(hT[:, i % 8, :], S[i % NS][:, :], ACT.Exp).then_inc(exp_ready.handle, 1)
                    if s and s % NT == 0:
                        group_out(L, b, att, s // NT - 1, G * s)
                finish(L, b, att)

            def attention(L, b, att):
                variant, t0 = att["v"], att["t0"]
                if variant == "soft":
                    return soft_attention(L, b, att)
                nt, per = NTILES[variant], PER[variant]
                ends = {group_end(per, g) + 1: g for g in range(H // G)} if variant != "one" else {}
                for i in range(nt + LAG + per + 6):
                    if i < nt:
                        act.wait_ge(max_ready.handle, max_ready.at(L, b, t0 + i + 1))
                        if variant == "window":
                            if i >= 3:
                                act.wait_ge(pT_psum.handle, pT_psum.at(L, b, t0 + i - 2))
                            act.activation(pn[:, i % 3, :], rest[:, 0, i % 2, :], ACT.Exp).then_inc(exp_ready.handle, 1)
                        else:
                            if i >= 2:
                                act.wait_ge(pn_ready.handle, pn_ready.at(L, b, att["n0"] + i - 1))
                            if variant == "topk":
                                act.activation(probs[:, i % 2, :], S[i % NS][:, :], ACT.Exp, bias=nmax[:, i:i + 1])
                                act.wait_ge(rest_ready.handle, rest_ready.at(L, b, i + 1))
                                act.activation(probs2[:, i % 2, :], rest[:, 1, i % 2, :], ACT.Exp, bias=nmax[:, i:i + 1]).then_inc(exp_ready.handle, 1)
                            else:
                                act.activation(probs[:, i % 2, :], S[i % NS][:, :], ACT.Exp, bias=nmax[:, i:i + 1],
                                               accum_out=ssum[:, i:i + 1]).then_inc(exp_ready.handle, 1)
                    j = i - LAG
                    if 0 <= j < nt and not n_ev(L, variant, j):
                        copy_probs(act, L, b, att, j)
                    if j in ends:
                        group_out(L, b, att, ends[j], G * (ends[j] + 1))
                if variant == "one":
                    for m in range(KC):
                        act.wait_ge(pv_done.handle, pv_done.at(L, b, m + 1))
                        act.activation(atT[:, m, :], OB[m][:, :], ACT.Copy).then_inc(atT_act.handle, 1)
                else:
                    finish(L, b, att)

            def ffn(L, b):
                fn = {0: ACT.Gelu, 2: ACT.Gelu_apprx_tanh, 3: ACT.Silu}[L]
                m1 = SCOLS[L]["m1"]
                for j in range(NH):
                    if L == 3:
                        act.wait_ge(hid_psum.handle, hid_psum.at(L, b, 2 * j + 1))
                        if j >= 2:
                            act.wait_ge(hid_ready.handle, hid_ready.at(L, b, j - 1))
                        act.activation(sil[:, j % 2, :], A[0][:, :], fn, bias=SV[:, m1 + j:m1 + j + 1]).then_inc(sil_ready.handle, 1)
                    else:
                        act.wait_ge(hid_psum.handle, hid_psum.at(L, b, j + 1))
                        act.activation(hT[:, j, :], A[j % 2][:, :], fn, bias=SV[:, m1 + j:m1 + j + 1]).then_inc(hid_ready.handle, 1)

            def router_layer(b):
                L = 1
                for m in range(KC):
                    act.wait_ge(qk1_psum.handle, qk1_psum.at(L, b, 2 * m + 1))
                    act.activation(q1T[:, m, :], A[m][:, :], ACT.Copy, scale=QSC1).then_inc(qk1_ready.handle, 1)
                    act.wait_ge(qk1_psum.handle, qk1_psum.at(L, b, 2 * m + 2))
                    act.activation(k1T[:, m, :], S[m][:, :], ACT.Copy).then_inc(qk1_ready.handle, 1)
                attention(L, b, ATT[1][0])
                act.wait_ge(rl_shift.handle, rl_shift.at(L, b, 1))
                act.activation(rpr[:, :, 0:E], rlog[:, :, 0:E], ACT.Exp).then_inc(rl_exp.handle, 1)
                for i in range(E * NR + KC):
                    act.wait_ge(eh_psum.handle, eh_psum.at(L, b, i + 1))
                    if i >= 2 * NR and i % NR == 0:
                        act.wait_ge(eo_psum.handle, eo_psum.at(L, b, NT * (i // NR - 1)))
                    act.activation(hT[:, i % (2 * NR), :], A[i % 2][:, :], ACT.Silu, bias=modc[:, i:i + 1]).then_inc(eh_ready.handle, 1)
                for t in range(NT):
                    act.wait_ge(eo_read.handle, eo_read.at(L, b, E * NT + t + 1))
                    act.activation(g1[:, t, :], g1[:, t, :], ACT.Sigmoid).then_inc(gate_ready.handle, 1)

            def first_ln(L, b, n):
                act.wait_ge(modc_ready.handle, modc_ready.at(L, b, 1))
                ln(L, b, n, xnT, 0, roll=ROLL if L == 3 else 0)

            for L in range(LAYERS):
                first_ln(L, None, 1)
                with act.Fori(0, B) as b:
                    if L == 1:
                        router_layer(b)
                    else:
                        stacks(L, b, 0)
                        attention(L, b, ATT[L][0])
                        ln(L, b, 1, xnT, None if L == 2 else 1)
                        if L == 2:
                            ln(L, b, 2, cnT, None)
                        stacks(L, b, 1)
                        attention(L, b, ATT[L][1])
                        ln(L, b, lns[L] - 1, xnT, 1 if L == 2 else 2)
                        ffn(L, b)
                    first_ln(L, b, lns[L])

        @block.tensor
        def _(pe):
            mm = pe.matmul

            def prepare(L):
                pe.wait_ge(loaded.handle, loaded.before(L, 3))
                cols = MOD[L] * P + GATE[L]
                c = condT if L < 2 else condS
                for m in range(MOD[L]):
                    for k in range(KC):
                        x = mm(S[0][:, m * B:(m + 1) * B], stk[:, k * cols + m * P:k * cols + (m + 1) * P], c[:, k, :],
                               start=k == 0, stop=k == KC - 1)
                x.then_inc(prep_psum.handle, 1)
                if GATE[L]:
                    pe.wait_ge(condB_ready.handle, condB_ready.before(L, 1))
                for b in range(B if GATE[L] else 0):
                    pe.wait_ge(prep_read.handle, prep_read.before(L, b + 1))
                    lo = MOD[L] * P
                    for g in range(0, GATE[L], 512):
                        g1_ = min(g + 512, GATE[L])
                        for k in range(KC):
                            x = mm(S[1 + g // 512][:, 0:g1_ - g], condB[:, k, b, :],
                                   stk[:, k * cols + lo + g:k * cols + lo + g1_], start=k == 0, stop=k == KC - 1)
                    x.then_inc(prep_psum.handle, 1)
                pe.wait_ge(prep_read.handle, prep_read.before(L, 1 + (B if GATE[L] else 0)))

            def ln(L, b, n):
                for t in range(NT):
                    pe.wait_ge(xn_ready.handle, xn_ready.at(L, b, NT * (n - 1) + t + 1))
                    for k in range(KC):
                        x = pe.transpose(A[k][:, t * P:(t + 1) * P], xn[:, t, k * P:(k + 1) * P], ident[:, :])
                x.then_inc(xT_psum.handle, 1)

            def ln_read(L, b, n):
                pe.wait_ge(xT_dve.handle, xT_dve.at(L, b, n))
                pe.wait_ge(xT_act.handle, xT_act.at(L, b, n))

            def qkv(L, b, n, src_kv):
                sfx = "2" if n else ""
                for t in range(NT + TLAG):
                    if t < NT:
                        if t >= 2:
                            pe.wait_ge(qk_read.handle, qk_read.at(L, b, NT * n + t - 1))
                        tok = slice(t * P, (t + 1) * P)
                        for name, src, o in (("q", xnT, 0), ("k", src_kv, C)):
                            for k in range(KC):
                                x = mm(A[t % 2][:, o:o + C], src[:, k, tok], w(L, name + sfx, k), start=k == 0, stop=k == KC - 1)
                        x.then_inc(qk_psum.handle, 1)
                        if t >= 2:
                            pe.wait_ge(v_ready.handle, v_ready.at(L, b, NT * n + t - 1))
                        for k in range(KC):
                            x = mm(S[t % 2][:, 0:C], src_kv[:, k, tok], w(L, "v" + sfx, k), start=k == 0, stop=k == KC - 1)
                        x.then_inc(v_psum.handle, 1)
                    u = t - TLAG
                    if u >= 0:
                        pe.wait_ge(stack_dve.handle, stack_dve.at(L, b, NT * n + u + 1))
                        pe.wait_ge(stack_pool.handle, stack_pool.at(L, b, NT * n + u + 1))
                        for j, bank in enumerate(STB):
                            i = 4 * u + j - (2 if j % 2 == 0 else 4)
                            if i >= 0:
                                pe.wait_ge(stackT_ready.handle, stackT_ready.at(L, b, NT * 4 * n + i + 1))
                            for h in range(8):
                                x = pe.transpose(bank[0:STACK, h * P:(h + 1) * P], qk_tok[:, u % 2, 8 * EIGHT[j] + h, :], identh[:, :])
                            x.then_inc(stackT_psum.handle, 1)
                pe.wait_ge(stackT_ready.handle, stackT_ready.at(L, b, NT * 4 * (n + 1) - 2))
                pe.wait_ge(v_ready.handle, v_ready.at(L, b, NT * (n + 1)))

            def all_stacks(L, b, n):
                pe.wait_ge(stackT_ready.handle, stackT_ready.at(L, b, NT * 4 * (n + 1)))

            def to_tokens(L, b, att, g, bank):
                pe.wait_ge(ou_ready.handle, ou_ready.at(L, b, H // G * att["n"] + g + 1))
                if g:
                    pe.wait_ge(tok_ready.handle, tok_ready.at(L, b, H // G * att["n"] + g))
                for t in range(NT):
                    x = pe.transpose(bank[:, t * P:(t + 1) * P], ou[:, g % 2, t * P:(t + 1) * P], ident[:, :])
                x.then_inc(tok_psum.handle, 1)

            def finish(L, b, att):
                n = att["n"]
                pe.wait_ge(tok_ready.handle, tok_ready.at(L, b, H // G * (n + 1)))
                for t in range(NT):
                    for k in range(KC):
                        x = pe.transpose(A[k][:, t * P:(t + 1) * P], xn[:, t, k * P:(k + 1) * P], ident[:, :])
                x.then_inc(atT_psum.handle, 1)
                pe.wait_ge(atT_dve.handle, atT_dve.at(L, b, n + 1))
                pe.wait_ge(atT_act.handle, atT_act.at(L, b, n + 1))

            def soft_attention(L, b, att):
                t0, h0, n = att["t0"], att["h0"], att["n"]
                first = [T[1], A[1]]
                steps = NT * H // G

                def first_scores(c, r):
                    g, t = c // NT, c % NT
                    i = G * c + r
                    if i >= 2:
                        pe.wait_ge(max_ready.handle, max_ready.at(L, b, t0 + i - 1))
                    h = G * g + r
                    mm(first[i % 2][:, :], qkst[0:STACK, h, t * P:(t + 1) * P], qkst[0:STACK, H + h, :],
                       start=True, stop=True).then_inc(first_psum.handle, 1)

                def max_rows(g, half):
                    if half == 0:
                        pe.wait_ge(mparts_ready.handle, mparts_ready.at(L, b, H // G * n + g + 1))
                        if g >= 2:
                            pe.wait_ge(tok_ready.handle, tok_ready.at(L, b, H // G * n + g - 1))
                    else:
                        pe.wait_ge(mrow_ready.handle, mrow_ready.at(L, b, H // 2 * n + 2 * g + 1))
                    h = G * g + 2 * half
                    for c in range(2 * NT):
                        x = pe.transpose(Th[0][STACK:STACK + AUG, c * P:(c + 1) * P], mparts[:, h * NT + c, :], identh[:, :])
                    x.then_inc(mrow_psum.handle, 1)

                def second_scores(s, r):
                    g, k = s // NT, s % NT
                    i = G * s + r
                    if k == 0 and r % 2 == 0:
                        pe.wait_ge(mrow_ready.handle, mrow_ready.at(L, b, H // 2 * n + 2 * g + r // 2 + 1))
                    if i >= NS:
                        pe.wait_ge(exp_ready.handle, exp_ready.at(L, b, t0 + i - NS + 1))
                    h = G * g + r
                    mm(S[i % NS][:, :], qkst[0:STACK + AUG, H + h, k * P:(k + 1) * P], qkst[0:STACK + AUG, h, :],
                       start=True, stop=True).then_inc(second_psum.handle, 1)

                def product(s, r):
                    g, k = s // NT, s % NT
                    if k == 0 and g >= 2 and r == 0:
                        pe.wait_ge(ou_ready.handle, ou_ready.at(L, b, H // G * n + g - 1))
                    i = G * s + r
                    pe.wait_ge(exp_ready.handle, exp_ready.at(L, b, t0 + i + 1))
                    mm(OB[g % 2][32 * r:32 * r + 32, :], vz[:, k, G * g + r, :], hT[:, i % 8, :],
                       start=k == 0, stop=k == NT - 1).then_inc(pv_done.handle, 1)

                for s in range(-AHEAD, steps + 2):
                    for r in range(G):
                        c = s + AHEAD
                        if 0 <= s < steps:
                            second_scores(s, r)
                        if c < steps:
                            first_scores(c, r)
                        if 1 <= s <= steps:
                            product(s - 1, r)
                        if c and c <= steps and c % NT == 0 and r in ROWS:
                            if c == NT and r == ROWS[0]:
                                all_stacks(L, b, n)
                            max_rows(c // NT - 1, ROWS.index(r))
                    if s > NT and s % NT == 1:
                        to_tokens(L, b, att, s // NT - 1, T[0])
                finish(L, b, att)

            def attention(L, b, att):
                variant, t0, n = att["v"], att["t0"], att["n"]
                if variant == "soft":
                    return soft_attention(L, b, att)
                nt, per = NTILES[variant], PER[variant]

                def wait_copied(j):
                    d, a = evs(variant, j + 1)
                    if n_ev(L, variant, j):
                        pe.wait_ge(pT_dve.handle, pT_dve.at(L, b, att["d0"] + d))
                    else:
                        pe.wait_ge(pT_act.handle, pT_act.at(L, b, att["a0"] + a))

                def scores(i):
                    if i >= NS:
                        r = max_ready if variant == "window" else exp_ready
                        pe.wait_ge(r.handle, r.at(L, b, t0 + i - NS + 1))
                    s = S[i % NS]
                    if variant == "one":
                        for k in range(KC):
                            x = mm(s[:, :], q1T[:, k, i * P:(i + 1) * P], k1T[:, k, :], start=k == 0, stop=k == KC - 1)
                    elif variant == "window":
                        for v in range(NT):
                            blk = slice(v * P, (v + 1) * P)
                            x = mm(s[:, blk], qkst[0:STACK, i, blk], qkst[0:STACK, H + i, blk], start=True, stop=True)
                    else:
                        h, t = i // NT, i % NT
                        x = mm(s[:, :], qkst[0:STACK, h, t * P:(t + 1) * P], qkst[0:STACK, H + h, :], start=True, stop=True)
                    x.then_inc(scores_ready.handle, 1)

                def product(h, ks):
                    if ks[0] == 0:
                        last = (h + 1) * per - 1
                        wait_copied(last)
                        if last:
                            wait_copied(last - 1)
                    g, r = h // G, h % G
                    if ks[0] == 0 and r == 0 and g >= 2:
                        pe.wait_ge(ou_ready.handle, ou_ready.at(L, b, H // G * n + g - 1))
                    o = OB[g % 2][32 * r:32 * r + 32, :]
                    for k in ks:
                        v = vz[:, k, h, :]
                        if variant == "window":
                            x = mm(o[:, k * P:(k + 1) * P], v, pT[:, h % 2, k, 0:P], start=True, stop=True)
                        else:
                            x = mm(o, v, pT[:, h % 2, k, :], start=k == 0, stop=k == NT - 1)
                    if ks[-1] == NT - 1:
                        x.then_inc(pv_done.handle, 1)

                ends = {group_end(per, g) + 3: g for g in range(H // G)} if variant != "one" else {}
                for i in range(nt + LAG + per + 6):
                    if i < nt:
                        scores(i)
                    j = i - LAG
                    if j == 0 and variant != "one":
                        all_stacks(L, b, n)
                    if 0 <= j < nt:
                        if variant == "window":
                            pe.wait_ge(exp_ready.handle, exp_ready.at(L, b, t0 + j + 1))
                        else:
                            pe.wait_ge(pn_ready.handle, pn_ready.at(L, b, att["n0"] + j + 1))
                        if j >= 2:
                            wait_copied(j - 2)
                        for k in range(NT):
                            x = pe.transpose(T[j % 2][:, k * P:(k + 1) * P], pn[:, j % 3, k * P:(k + 1) * P], ident[:, :])
                        x.then_inc(pT_psum.handle, 1)
                    if variant != "one" and per <= j - 1 < nt + per:
                        product((j - 1) // per - 1, list(range(NT)) if per == 1 else [(j - 1) % per])
                    if j in ends:
                        to_tokens(L, b, att, ends[j], A[1])
                if variant == "one":
                    wait_copied(nt - 1)
                    wait_copied(nt - 2)
                    for m in range(KC):
                        for k in range(NT):
                            x = mm(OB[m][:, :], v1[:, k, m * P:(m + 1) * P], pT[:, 0, k, :], start=k == 0, stop=k == NT - 1)
                        x.then_inc(pv_done.handle, 1)
                    pe.wait_ge(atT_act.handle, atT_act.at(L, b, KC))
                else:
                    finish(L, b, att)

            def project_out(L, b, n):
                for t in range(NT):
                    if t >= 2:
                        pe.wait_ge(out_read.handle, out_read.at(L, b, NT * n + t - 1))
                    for k in range(KC):
                        x = mm(A[t % 2][:, 0:C], atT[:, k, t * P:(t + 1) * P], w(L, "o2" if n else "o", k), start=k == 0, stop=k == KC - 1)
                    x.then_inc(out_psum.handle, 1)

            def ffn(L, b):
                if L == 3:
                    for j in range(NH):
                        for half in range(2):
                            if j >= 1:
                                if half == 0:
                                    pe.wait_ge(sil_ready.handle, sil_ready.at(L, b, j))
                                else:
                                    pe.wait_ge(hid_ready.handle, hid_ready.at(L, b, j))
                            lo = half * HID + j * P
                            for k in range(KC):
                                x = mm(A[half][:, :], w(L, "w1", k, lo, lo + P, 2 * HID), xnT[:, k, :], start=k == 0, stop=k == KC - 1)
                            x.then_inc(hid_psum.handle, 1)
                else:
                    for j in range(NH):
                        if j >= 2:
                            pe.wait_ge(hid_ready.handle, hid_ready.at(L, b, j - 1))
                        for k in range(KC):
                            x = mm(A[j % 2][:, :], w(L, "w1", k, j * P, (j + 1) * P, HID), xnT[:, k, :], start=k == 0, stop=k == KC - 1)
                        x.then_inc(hid_psum.handle, 1)
                pe.wait_ge(hid_ready.handle, hid_ready.at(L, b, NH))
                for t in range(NT):
                    if t >= 2:
                        pe.wait_ge(ffn_read.handle, ffn_read.at(L, b, t - 1))
                    for j in range(NH):
                        x = mm(T[t % 2][:, 0:C], hT[:, j, t * P:(t + 1) * P], w(L, "w2", j), start=j == 0, stop=j == NH - 1)
                    x.then_inc(ffn_psum.handle, 1)
                    if t == 0:
                        ln(L, b, lns[L])

            def router_layer(b):
                L = 1
                for m in range(KC):
                    for name, src, dst in (("q", xnT, A[m]), ("k", cxT, S[m])):
                        for k in range(KC):
                            x = mm(dst[:, :], w(L, name, k, m * P, (m + 1) * P), src[:, k, :], start=k == 0, stop=k == KC - 1)
                        x.then_inc(qk1_psum.handle, 1)
                for t in range(NT):
                    if t >= 2:
                        pe.wait_ge(v_ready.handle, v_ready.at(L, b, t - 1))
                    for k in range(KC):
                        x = mm(T[t % 2][:, 0:C], cxT[:, k, t * P:(t + 1) * P], w(L, "v", k), start=k == 0, stop=k == KC - 1)
                    x.then_inc(v_psum.handle, 1)
                pe.wait_ge(qk1_ready.handle, qk1_ready.at(L, b, 2 * KC))
                pe.wait_ge(v_ready.handle, v_ready.at(L, b, NT))
                pe.nop().then_inc(cx_used.handle, 1)
                attention(L, b, ATT[1][0])
                pe.wait_ge(w_rest.handle, w_rest.before(L, 1))
                comb = [xnT[:, 0, :], xnT[:, 1, :], atT[:, 0, :], atT[:, 1, :]]
                for t in range(NT):
                    for k in range(4):
                        x = mm(S[0][:, 4 * t:4 * t + E], comb[k][:, t * P:(t + 1) * P], w(L, "r", k, 0, E, E), start=k == 0, stop=k == 3)
                x.then_inc(rl_psum.handle, 1)

                def hidden(i, name, off, width):
                    if i >= 2:
                        pe.wait_ge(eh_ready.handle, eh_ready.at(L, b, i - 1))
                    for k in range(4):
                        o = WCOLS[1][name] + k * width + off
                        x = mm(A[i % 2][:, :], W[:, o:o + P], comb[k], start=k == 0, stop=k == 3)
                    x.then_inc(eh_psum.handle, 1)

                def down(e, chunks, name, col):
                    for t in range(NT):
                        i = e * NT + t
                        if i >= 2:
                            pe.wait_ge(eo_read.handle, eo_read.at(L, b, i - 1))
                        for j in range(chunks):
                            o = WCOLS[1][name] + col + j * C
                            x = mm(T[t % 2][:, 0:C], hT[:, (e % 2) * NR + j, t * P:(t + 1) * P], W[:, o:o + C], start=j == 0, stop=j == chunks - 1)
                        x.then_inc(eo_psum.handle, 1)

                for e in range(E + 1):
                    for j in range(NR if e < E else KC):
                        if e < E:
                            hidden(e * NR + j, "e1", e * 4 * RH + j * P, RH)
                        else:
                            hidden(e * NR + j, "g1", j * P, C)
                    if e:
                        pe.wait_ge(eh_ready.handle, eh_ready.at(L, b, e * NR))
                        down(e - 1, NR, "e2", (e - 1) * NR * C)
                pe.wait_ge(eh_ready.handle, eh_ready.at(L, b, E * NR + KC))
                down(E, KC, "g2", 0)
                pe.wait_ge(eo_read.handle, eo_read.at(L, b, (E + 1) * NT))
                for t in range(NT):
                    for k in range(KC):
                        x = pe.transpose(A[k][:, t * P:(t + 1) * P], routed[:, t, k * P:(k + 1) * P], ident[:, :])
                x.then_inc(roT_psum.handle, 1)
                pe.wait_ge(roT_ready.handle, roT_ready.at(L, b, 1))
                for t in range(NT):
                    if t >= 2:
                        pe.wait_ge(out_read.handle, out_read.at(L, b, t - 1))
                    for k in range(KC):
                        x = mm(A[t % 2][:, 0:C], roT[:, k, t * P:(t + 1) * P], w(L, "o", k), start=k == 0, stop=k == KC - 1)
                    x.then_inc(out_psum.handle, 1)
                pe.wait_ge(out_read.handle, out_read.at(L, b, NT))
                ln(L, b, lns[L])

            pe.wait_ge(consts, 9)
            pe.wait_ge(cond_ready, 1)
            for L in range(LAYERS):
                prepare(L)
                if L in (0, 2):
                    pe.wait_ge(ones_ready.handle, ones_ready.before(L, 1))
                if L:
                    ln_read(L - 1, B - 1, lns[L - 1])
                ln(L, None, 1)
                pe.wait_ge(w_loaded.handle, w_loaded.before(L, 1))
                with pe.Fori(0, B) as b:
                    ln_read(L, b, 0)
                    if L == 1:
                        pe.wait_ge(cx_loaded.handle, cx_loaded.at(L, b, 1))
                        router_layer(b)
                    else:
                        qkv(L, b, 0, xnT)
                        attention(L, b, ATT[L][0])
                        pe.wait_ge(w_rest.handle, w_rest.before(L, 1))
                        project_out(L, b, 0)
                        ln(L, b, 1)
                        ln_read(L, b, 1)
                        if L == 2:
                            ln(L, b, 2)
                            ln_read(L, b, 2)
                            qkv(L, b, 1, cnT)
                        else:
                            pe.wait_ge(cx_loaded.handle, cx_loaded.at(L, b, 1))
                            qkv(L, b, 1, cxT)
                        pe.nop().then_inc(cx_used.handle, 1)
                        attention(L, b, ATT[L][1])
                        project_out(L, b, 1)
                        ln(L, b, lns[L] - 1)
                        ln_read(L, b, lns[L] - 1)
                        ffn(L, b)

        @block.vector
        def _(dve):
            step = Steps(dve, dve_step)

            def prepare(L):
                dve.wait_ge(loaded.handle, loaded.before(L, 3))
                if GATE[L]:
                    c = condT if L < 2 else condS
                    dve.tensor_copy(condB, c[:, :, :].rearrange("p k (b o) -> p k b o", o=1).to_broadcast([P, KC, B, P])).then_inc(condB_ready.handle, 1)
                ln_stats(lambda t: x_all[:, t, :])
                ln_apply(L, None, 1, lambda t: x_all[:, t, :])
                if L >= 2:
                    for name in ("qkv", "qkv2"):
                        o = BCOLS[L][name]
                        step.did(dve.tensor_scalar(BB[:, o:o + C], BB[:, o:o + C], QSC, None, ALU.mult))
                dve.wait_ge(prep_psum.handle, prep_psum.before(L, 1))
                step.did(dve.tensor_tensor(mod[:, 0:B, 0:MOD[L]], S[0][:, 0:MOD[L] * B].rearrange("p (m b) -> p b m", b=B),
                                           SV[:, 0:MOD[L]].rearrange("p (o m) -> p o m", o=1).to_broadcast([P, B, MOD[L]]), ALU.add))
                step.wait()
                if L != 1:
                    v = mod[:, 0:B, 0:MOD[L]].rearrange("p b (n s) -> p b n s", s=4)[:, :, :, 0:2]
                    dve.tensor_scalar(v, v, 1.0, None, ALU.add).then_inc(prep_read.handle, 1)
                else:
                    dve.engine_nop().then_inc(prep_read.handle, 1)
                for b in range(B if GATE[L] else 0):
                    dve.wait_ge(prep_psum.handle, prep_psum.before(L, b + 2))
                    bo = BCOLS[L]["gate"]
                    for g in range(0, GATE[L], 512):
                        hi = min(g + 512, GATE[L])
                        x = dve.tensor_tensor(gates[:, b, g:hi], S[1 + g // 512][:, 0:hi - g], BB[:, bo + g:bo + hi], ALU.add)
                        if hi < GATE[L]:
                            step.did(x)
                            step.wait()
                    x.then_inc(prep_read.handle, 1)
                dve.wait_ge(prep_read.handle, prep_read.before(L, 1 + (B if GATE[L] else 0)))
                if L:
                    dve.wait_ge(xT_dve.handle, xT_dve.at(L - 1, B - 1, lns[L - 1]))
                    dve.wait_ge(xT_act.handle, xT_act.at(L - 1, B - 1, lns[L - 1]))
                next_modc(L, None)
                ln_out(L, None, 1, xnT, 0, roll=ROLL if L == 3 else 0)
                step.reset()

            def ln_stats(src):
                step.wait()
                dve.sem_inc(passed, 1)
                for t in range(NT):
                    step.did(dve.bn_stats(st[:, t, :], src(t)))
                step.wait()
                for t in range(NT):
                    dve.bn_aggr(mv[:, t, :], st[:, t, :]).then_inc(stats_ready.handle, 1)

            def ln_apply(L, b, n, src):
                dve.wait_ge(rstd_ready.handle, rstd_ready.at(L, b, n))
                for t in range(NT):
                    dve.tensor_scalar(xn[:, t, :], src(t), mv[:, t, 0:1], rstd[:, 1, t:t + 1], ALU.subtract, ALU.mult).then_inc(xn_ready.handle, 1)

            def ln_out(L, b, n, dst, mi, roll=0):
                dve.wait_ge(xT_psum.handle, xT_psum.at(L, b, n))
                sc, sh = scale_shift(L, mi, 0)
                pieces = [(0, N, 0)] if not roll else [(roll, N, 0), (0, roll, N - roll)]
                for lo, hi, to in pieces:
                    o, s = dst[:, 0, to:to + hi - lo], A[0][:, lo:hi]
                    x = dve.tensor_copy(o, s) if sc is None else dve.tensor_scalar(o, s, sc, sh, ALU.mult, ALU.add)
                x.then_inc(xT_dve.handle, 1)

            def ln(L, b, n, src, dst, mi):
                ln_stats(src)
                ln_apply(L, b, n, src)
                ln_out(L, b, n, dst, mi)

            def next_modc(L, b):
                row = mod[:, 0, 0:MOD[L]] if b is None else mod[:, b + 1, 0:MOD[L]]
                dve.tensor_copy(modc[:, 0:MOD[L]], row).then_inc(modc_ready.handle, 1)
                dve.wait_ge(modc_ready.handle, modc_ready.at(L, b, 1))

            def v_view(t):
                return vz[:, t, :, 0:D]

            def qkv(L, b, n):
                for t in range(NT):
                    i = NT * n + t
                    a, f, rem = A[t % 2], qkf[:, t % 2, :], left[:, t % 2, :]
                    dve.wait_ge(qk_psum.handle, qk_psum.at(L, b, i + 1))
                    if L == 0:
                        def heads4(ap):
                            return ap.rearrange("p (q h d) -> p q h d", q=2, d=D)
                        def table(s, lo, hi):
                            tb = rope[:, s, t, :, lo:hi].rearrange("p q (o d) -> p q o d", o=1)
                            return tb.to_broadcast([P, 2, H, hi - lo])
                        hd = D // 2
                        step.did(dve.tensor_tensor(heads4(f), heads4(a[:, :]), table(0, 0, D), ALU.mult))
                        step.did(dve.tensor_tensor(heads4(rem)[:, :, :, 0:hd], heads4(a[:, :])[:, :, :, hd:D], table(1, 0, hd), ALU.mult))
                        dve.tensor_tensor(heads4(rem)[:, :, :, hd:D], heads4(a[:, :])[:, :, :, 0:hd], table(1, hd, D), ALU.mult).then_inc(qk_read.handle, 1)
                    else:
                        bo = BCOLS[L]["qkv2" if n else "qkv"]
                        step.did(dve.scalar_tensor_tensor(out=f[:, 0:C], in0=a[:, 0:C], scalar=QSC, in1=BB[:, bo:bo + C], op0=ALU.mult, op1=ALU.add))
                        dve.tensor_tensor(f[:, C:2 * C], a[:, C:2 * C], BB[:, bo + C:bo + 2 * C], ALU.add).then_inc(qk_read.handle, 1)
                    dve.wait_ge(v_psum.handle, v_psum.at(L, b, i + 1))
                    sv = S[t % 2][:, 0:C].rearrange("p (h d) -> p h d", d=D)
                    if L == 0:
                        dve.tensor_copy(v_view(t), sv).then_inc(v_ready.handle, 1)
                    else:
                        bv = BB[:, bo + 2 * C:bo + 3 * C].rearrange("p (h d) -> p h d", d=D)
                        dve.tensor_tensor(v_view(t), sv, bv, ALU.add).then_inc(v_ready.handle, 1)
                    step.wait()
                    dve.wait_ge(qk_read.handle, qk_read.at(L, b, i + 1))
                    if L == 0:
                        step.did(dve.tensor_tensor(f, f, rem, ALU.add))
                        step.wait()
                    tok = qk_tok[:, t % 2, :, :].rearrange("p h (s d) -> p s h d", d=D)
                    f3, rem3 = (ap.rearrange("p (h d) -> p h d", d=D) for ap in (f, rem))
                    if t >= 2:
                        dve.wait_ge(stackT_psum.handle, stackT_psum.at(L, b, NT * 4 * n + 4 * (t - 1)))
                    dve.tensor_copy(tok[:, 0], f3).then_inc(parts_ready.handle, 1)
                    dve.wait_ge(parts_ready.handle, parts_ready.at(L, b, 2 * i + 1))
                    step.did(dve.tensor_tensor(rem3, f3, tok[:, 0], ALU.subtract))
                    step.wait()
                    dve.tensor_copy(tok[:, 1], rem3).then_inc(parts_ready.handle, 1)
                    dve.wait_ge(parts_ready.handle, parts_ready.at(L, b, 2 * i + 2))
                    step.did(dve.tensor_tensor(tok[:, 5, 0:H], rem3[:, 0:H], tok[:, 1, 0:H], ALU.subtract))
                    dve.tensor_tensor(tok[:, 4, H:2 * H], rem3[:, H:2 * H], tok[:, 1, H:2 * H], ALU.subtract).then_inc(stack_dve.handle, 1)
                    step.wait()

            def normalise(L, b, att, g, bank):
                dve.wait_ge(tok_psum.handle, tok_psum.at(L, b, H // G * att["n"] + g + 1))
                o = bank[:, :].rearrange("p (t r c) -> p t r c", t=NT, c=32)
                step.did(dve.reciprocal(rden[:, :, :], o[:, :, :, D]))
                step.wait()
                dst = xn[:, :, G * D * g:G * D * (g + 1)].rearrange("p t (r c) -> p t r c", c=D)
                dve.tensor_tensor(dst, o[:, :, :, 0:D], rden[:, :, :].rearrange("p t (r o) -> p t r o", o=1).to_broadcast([P, NT, G, D]),
                                  ALU.mult).then_inc(tok_ready.handle, 1)

            def finish(L, b, att):
                dve.wait_ge(atT_psum.handle, atT_psum.at(L, b, att["n"] + 1))
                pieces = [(0, N, 0)] if att["v"] != "window" else [(0, N - ROLL, ROLL), (N - ROLL, N, 0)]
                for lo, hi, to in pieces:
                    x = dve.tensor_copy(atT[:, 0, to:to + hi - lo], A[0][:, lo:hi])
                x.then_inc(atT_dve.handle, 1)

            def soft_attention(L, b, att):
                t0, n = att["t0"], att["n"]
                first = [T[1], A[1]]
                steps = NT * H // G

                def maximum(c, r):
                    g, t = c // NT, c % NT
                    i = G * c + r
                    dve.wait_ge(first_psum.handle, first_psum.at(L, b, t0 + i + 1))
                    m = (G * g + r) * NT + t
                    dve.tensor_reduce(nmax[:, m:m + 1], first[i % 2][:, :], AX.X, ALU.max, negate=True).then_inc(max_ready.handle, 1)

                def max_parts(g):
                    cols = slice(G * NT * g, G * NT * (g + 1))
                    dve.wait_ge(max_ready.handle, max_ready.at(L, b, t0 + G * NT * (g + 1)))
                    step.did(dve.tensor_copy(mparts[:, cols, 0], nmax[:, cols]))
                    step.wait()
                    dve.tensor_tensor(mparts[:, cols, 1], nmax[:, cols], mparts[:, cols, 0], ALU.subtract).then_inc(mparts_ready.handle, 1)

                def max_rows(g, half):
                    dve.wait_ge(mrow_psum.handle, mrow_psum.at(L, b, H // 2 * n + 2 * g + half + 1))
                    h = G * g + 2 * half
                    dve.tensor_copy(qkst[STACK:STACK + AUG, h:h + 2, :],
                                    Th[0][STACK:STACK + AUG, :].rearrange("p (h n) -> p h n", h=2)).then_inc(mrow_ready.handle, 1)

                for c in range(steps + AHEAD + 2):
                    for r in range(G):
                        if c < steps:
                            maximum(c, r)
                        if c and c <= steps and c % NT == 0 and r in ROWS:
                            max_rows(c // NT - 1, ROWS.index(r))
                    if c < steps and c % NT == NT - 1:
                        max_parts(c // NT)
                    s = c - AHEAD
                    if s > NT and s % NT == 1:
                        normalise(L, b, att, s // NT - 1, T[0])
                finish(L, b, att)

            def second_removal(L, b, t0, i, found):
                if i >= 2:
                    dve.wait_ge(exp_ready.handle, exp_ready.at(L, b, t0 + i - 1))
                    dve.sem_inc(passed, 1)
                dve.wait_ge(dve_step, found)
                dve.match_replace(rest[:, 1, i % 2, :], top[:, i % 2, 8:16], rest[:, 0, i % 2, :], LOWEST).then_inc(rest_ready.handle, 1)

            def attention(L, b, att):
                variant, t0 = att["v"], att["t0"]
                if variant == "soft":
                    return soft_attention(L, b, att)
                nt, per = NTILES[variant], PER[variant]
                ends = {group_end(per, g) + 4: g for g in range(H // G)} if variant != "one" else {}
                for i in range(nt + LAG + per + 6):
                    if i < nt:
                        s = S[i % NS]
                        dve.wait_ge(scores_ready.handle, scores_ready.at(L, b, t0 + i + 1))
                        if variant == "window":
                            s4 = s[:, :].rearrange("p (w k) -> p w k", w=NT)
                            step.did(dve.tensor_reduce(nmax[:, NT * i:NT * i + NT], s4, AX.X, ALU.max))
                            if i >= 2:
                                dve.wait_ge(exp_ready.handle, exp_ready.at(L, b, t0 + i - 1))
                            step.wait()
                            m = nmax[:, NT * i:NT * i + NT].rearrange("p (w o) -> p w o", o=1).to_broadcast([P, NT, P])
                            dve.tensor_tensor(rest[:, 0, i % 2, :].rearrange("p (w k) -> p w k", w=NT), s4, m, ALU.subtract).then_inc(max_ready.handle, 1)
                        elif variant == "topk":
                            r1, tp = rest[:, 0, i % 2, :], top[:, i % 2, :]
                            if i >= 2:
                                dve.wait_ge(rest_ready.handle, rest_ready.at(L, b, i - 1))
                            dve.sem_inc(passed, 1)
                            step.did(dve.max(tp[:, 0:8], s[:, :]))
                            first8 = step.n
                            if i:
                                second_removal(L, b, t0, i - 1, second8)
                            dve.wait_ge(dve_step, first8)
                            step.did(dve.match_replace(r1, tp[:, 0:8], s[:, :], LOWEST))
                            dve.tensor_scalar(nmax[:, i:i + 1], tp[:, 0:1], -1.0, None, ALU.mult).then_inc(max_ready.handle, 1)
                            step.wait()
                            step.did(dve.max(tp[:, 8:16], r1))
                            second8 = step.n
                        else:
                            dve.tensor_reduce(nmax[:, i:i + 1], s[:, :], AX.X, ALU.max, negate=True).then_inc(max_ready.handle, 1)
                    if variant == "topk" and i == nt:
                        second_removal(L, b, t0, nt - 1, second8)
                    j = i - 1
                    if variant == "one" and 0 <= j < nt:
                        dve.wait_ge(exp_ready.handle, exp_ready.at(L, b, t0 + j + 1))
                        dve.reciprocal(rsum[:, j:j + 1], ssum[:, j:j + 1]).then_inc(rsum_ready.handle, 1)
                    j = i - LAG
                    if 0 <= j < nt and n_ev(L, variant, j):
                        copy_probs(dve, L, b, att, j)
                    if j in ends:
                        normalise(L, b, att, ends[j], A[1])
                if variant != "one":
                    finish(L, b, att)

            def project_out(L, b, n):
                for t in range(NT):
                    dve.wait_ge(out_psum.handle, out_psum.at(L, b, NT * n + t + 1))
                    bias = BB[:, BCOLS[L]["o2" if n else "o"]:][:, 0:C] if L else None
                    gate = None
                    if L == 2 and n == 0:
                        gate = gates[:, b, 0:C]
                    if L == 3:
                        gate = gates[:, b, n * C:(n + 1) * C]
                    x = x_all[:, b * NT + t, :]
                    r = res[:, t % 2, :]
                    if bias is None:
                        dve.tensor_tensor(x, A[t % 2][:, 0:C], x, ALU.add).then_inc(out_read.handle, 1)
                        dve.wait_ge(out_read.handle, out_read.at(L, b, NT * n + t + 1))
                        continue
                    dve.tensor_tensor(r, A[t % 2][:, 0:C], bias, ALU.add).then_inc(out_read.handle, 1)
                    dve.wait_ge(out_read.handle, out_read.at(L, b, NT * n + t + 1))
                    if gate is not None:
                        step.did(dve.tensor_tensor(r, r, gate, ALU.mult))
                        step.wait()
                    step.did(dve.tensor_tensor(x, x, r, ALU.add))
                    step.wait()

            def ffn(L, b, next_tile):
                dve.wait_ge(xT_dve.handle, xT_dve.at(L, b, lns[L] - 1))
                dve.wait_ge(xT_act.handle, xT_act.at(L, b, lns[L] - 1))
                next_modc(L, b)
                ln_stats(next_tile)
                if L == 3:
                    m1 = SCOLS[L]["m1"] + NH
                    for j in range(NH):
                        dve.wait_ge(hid_psum.handle, hid_psum.at(L, b, 2 * j + 2))
                        dve.wait_ge(sil_ready.handle, sil_ready.at(L, b, j + 1))
                        dve.scalar_tensor_tensor(out=hT[:, j, :], in0=A[1][:, :], scalar=SV[:, m1 + j:m1 + j + 1],
                                                 in1=sil[:, j % 2, :], op0=ALU.add, op1=ALU.mult).then_inc(hid_ready.handle, 1)
                ln_apply(L, b, lns[L], next_tile)
                for t in range(NT):
                    dve.wait_ge(ffn_psum.handle, ffn_psum.at(L, b, t + 1))
                    o = BCOLS[L]["m2"]
                    x = x_all[:, b * NT + t, :]
                    r = res[:, t % 2, :]
                    dve.tensor_tensor(r, T[t % 2][:, 0:C], BB[:, o:o + C], ALU.add).then_inc(ffn_read.handle, 1)
                    if t == 0:
                        ln_out(L, b, lns[L], xnT, 0, roll=ROLL if L == 3 else 0)
                    dve.wait_ge(ffn_read.handle, ffn_read.at(L, b, t + 1))
                    if L:
                        g = (1 if L == 2 else 2) * C
                        step.did(dve.tensor_tensor(r, r, gates[:, b, g:g + C], ALU.mult))
                        step.wait()
                    if t == NT - 1:
                        step.wait()
                        dve.tensor_tensor(x, x, r, ALU.add).then_inc(x_done.handle, 1)
                    else:
                        step.did(dve.tensor_tensor(x, x, r, ALU.add))
                        step.wait()

            def router_layer(b, next_tile):
                L = 1
                for t in range(NT):
                    dve.wait_ge(v_psum.handle, v_psum.at(L, b, t + 1))
                    dve.tensor_copy(v1[:, t, :], T[t % 2][:, 0:C]).then_inc(v_ready.handle, 1)
                attention(L, b, ATT[1][0])
                dve.wait_ge(rl_psum.handle, rl_psum.at(L, b, 1))
                rl, rp = rlog[:, :, 0:E], rpr[:, :, 0:E]

                def over(ap, n=E):
                    return ap.rearrange("p (t o) -> p t o", o=1).to_broadcast([P, NT, n])
                step.did(dve.tensor_tensor(rl, S[0][:, 0:4 * NT].rearrange("p (t e) -> p t e", e=4)[:, :, 0:E],
                                           gates[:, bass.ds(b, 1), 0:E].to_broadcast([P, NT, E]), ALU.add))
                step.wait()
                step.did(dve.tensor_reduce(rsm[:, 0, :], rl, AX.X, ALU.max))
                step.wait()
                dve.tensor_tensor(rl, rl, over(rsm[:, 0, :]), ALU.subtract).then_inc(rl_shift.handle, 1)
                dve.wait_ge(rl_exp.handle, rl_exp.at(L, b, 1))
                step.did(dve.tensor_reduce(rsm[:, 0, :], rp, AX.X, ALU.add))
                step.wait()
                step.did(dve.reciprocal(rsm[:, 1, :], rsm[:, 0, :]))
                step.wait()
                step.did(dve.tensor_tensor(rp, rp, over(rsm[:, 1, :]), ALU.mult))
                step.wait()
                ln_stats(next_tile)
                ln_apply(L, b, lns[L], next_tile)
                for e in range(E):
                    for t in range(NT):
                        bo = BCOLS[L]["e2"] + e * C
                        pe_ = rpr[:, t, e:e + 1]
                        if e == 0:
                            step.did(dve.tensor_scalar(routed[:, t, :], BB[:, bo:bo + C], pe_, None, ALU.mult))
                        else:
                            step.did(dve.scalar_tensor_tensor(out=routed[:, t, :], in0=BB[:, bo:bo + C], scalar=pe_, in1=routed[:, t, :], op0=ALU.mult, op1=ALU.add))
                    step.wait()
                for e in range(E):
                    for t in range(NT):
                        i = e * NT + t
                        dve.wait_ge(eo_psum.handle, eo_psum.at(L, b, i + 1))
                        if e:
                            dve.wait_ge(eo_read.handle, eo_read.at(L, b, i - NT + 1))
                        dve.scalar_tensor_tensor(out=routed[:, t, :], in0=T[t % 2][:, 0:C], scalar=rpr[:, t, e:e + 1],
                                                 in1=routed[:, t, :], op0=ALU.mult, op1=ALU.add).then_inc(eo_read.handle, 1)
                for t in range(NT):
                    i = E * NT + t
                    dve.wait_ge(eo_psum.handle, eo_psum.at(L, b, i + 1))
                    bo = BCOLS[L]["g2"]
                    dve.tensor_tensor(g1[:, t, :], T[t % 2][:, 0:C], BB[:, bo:bo + C], ALU.add).then_inc(eo_read.handle, 1)
                dve.wait_ge(roT_psum.handle, roT_psum.at(L, b, 1))
                step.did(dve.tensor_copy(roT[:, 0, :], A[0][:, :]))
                step.wait()
                dve.tensor_copy(roT[:, 1, :], A[1][:, :]).then_inc(roT_ready.handle, 1)
                for t in range(NT):
                    dve.wait_ge(out_psum.handle, out_psum.at(L, b, t + 1))
                    bo = BCOLS[L]["o"]
                    r = res[:, t % 2, :]
                    x = x_all[:, b * NT + t, :]
                    dve.tensor_tensor(r, A[t % 2][:, 0:C], BB[:, bo:bo + C], ALU.add).then_inc(out_read.handle, 1)
                    dve.wait_ge(out_read.handle, out_read.at(L, b, t + 1))
                    dve.wait_ge(gate_ready.handle, gate_ready.at(L, b, t + 1))
                    step.did(dve.tensor_tensor(r, r, g1[:, t, :], ALU.mult))
                    step.wait()
                    if t == NT - 1:
                        dve.tensor_tensor(x, x, r, ALU.add).then_inc(x_done.handle, 1)
                    else:
                        step.did(dve.tensor_tensor(x, x, r, ALU.add))
                        step.wait()

            dve.wait_ge(first_in, 16 * 3)
            dve.wait_ge(consts, 9)
            dve.wait_ge(cond_ready, 1)
            for L in range(LAYERS):
                prepare(L)
                if L == 0:
                    dve.wait_ge(rows_in, 16 * (B - 1))
                with dve.Fori(0, B) as b:
                    def x_tile(t):
                        return x_all[:, b * NT + t, :]

                    def next_tile(t):
                        return x_all[:, b * NT + NT + t, :]
                    if L == 1:
                        router_layer(b, next_tile)
                        dve.wait_ge(eh_ready.handle, eh_ready.at(L, b, E * NR + KC))
                        next_modc(L, b)
                        ln_out(L, b, lns[L], xnT, 0)
                    else:
                        qkv(L, b, 0)
                        attention(L, b, ATT[L][0])
                        project_out(L, b, 0)
                        ln(L, b, 1, x_tile, xnT, None if L == 2 else 1)
                        if L == 2:
                            dve.wait_ge(cx_loaded.handle, cx_loaded.at(L, b, 1))
                            ln(L, b, 2, lambda t: cxt[:, t, :], cnT, None)
                        qkv(L, b, 1)
                        attention(L, b, ATT[L][1])
                        project_out(L, b, 1)
                        ln(L, b, lns[L] - 1, x_tile, xnT, 1 if L == 2 else 2)
                        ffn(L, b, next_tile)
                    dve.wait_ge(x_done.handle, x_done.at(L, b, 1))
                    dve.sem_inc(passed, 1)
                    step.reset()


def kernel(**inputs):
    import numpy as _np
    import concourse.bacc as _bacc
    from concourse import mybir as _mybir
    from concourse.bass_utils import run_bass_kernel_spmd as _run

    g = {k: _np.asarray(v) for k, v in inputs.items()}

    def t(name):
        return g[name]

    def cm(a):
        r, c = a.shape
        return a.reshape(r // P, P, c).transpose(1, 0, 2).reshape(P, -1)

    def cv(v):
        return v.reshape(-1, P).T

    def cat(parts):
        return _np.ascontiguousarray(_np.concatenate(parts, axis=1))

    def row(parts):
        return _np.ascontiguousarray(_np.concatenate([p.reshape(-1) for p in parts]).reshape(1, -1))

    a = {"x": _np.ascontiguousarray(t("x"))}
    a["ctx"] = _np.ascontiguousarray(t("ctx_1024").reshape(B * NT, P, C))
    a["ctxT"] = _np.ascontiguousarray(t("ctx_1024").transpose(0, 2, 1).reshape(B * KC, P, N))
    a["condT"] = _np.ascontiguousarray(t("cond_1024").T.reshape(KC, P, B).transpose(1, 0, 2))
    half = D // 2
    f32 = _np.float32
    inv = (f32(1.0) / _np.power(f32(10000.0), _np.arange(half, dtype=f32) / f32(half))).astype(f32)
    ang = (_np.arange(N, dtype=f32)[:, None] * inv[None, :]).astype(f32)
    cos, sin = _np.cos(ang), _np.sin(ang)
    tab = _np.stack([_np.concatenate([cos, cos], 1), _np.concatenate([-sin, sin], 1)])
    tab = _np.stack([tab * f32(QSC), tab], 2).astype(f32)
    a["rope"] = _np.ascontiguousarray(tab.reshape(2, NT, P, 2, D).transpose(2, 0, 1, 3, 4).reshape(P, -1))

    L0, L1, L2, L3 = (f"L{i}_xcond_" for i in range(4))
    qkv = t(L0 + "qkv_w").T
    a["w0"] = cat([cm(qkv[:, 0:C]), cm(qkv[:, C:2 * C]), cm(qkv[:, 2 * C:]), cm(t(L0 + "sa_out_w").T), cm(t(L0 + "q_w").T), cm(t(L0 + "k_w").T),
                   cm(t(L0 + "v_w").T), cm(t(L0 + "ca_out_w").T), cm(t(L0 + "ffn_w1").T), cm(t(L0 + "ffn_w2").T)])
    a["pw0"] = cat([cm(_np.concatenate([t(L0 + f"ln{i}_w").T for i in (1, 2, 3)], axis=1))])
    a["bb0"] = row([t(L0 + "ffn_b2")])
    a["sv0"] = cat([cv(t(L0 + f"ln{i}_b")) for i in (1, 2, 3)] + [cv(t(L0 + "ffn_b1"))])

    e1, g1w, rw = t(L1 + "e_w1"), t(L1 + "gate_w1"), t(L1 + "router_W")
    a["w1"] = cat([cm(t(L1 + "Wq")), cm(t(L1 + "Wk")), cm(t(L1 + "Wv"))] + [cm(e1[e, 0:2 * C]) for e in range(E)]
                  + [cm(t(L1 + "e_w2")[e]) for e in range(E)] + [cm(g1w[0:2 * C]), cm(t(L1 + "gate_w2")), cm(t(L1 + "out_w")), cm(rw[0:2 * C])])
    a["pw1"] = cat([cm(_np.concatenate([e1[e, 2 * C:] for e in range(E)] + [g1w[2 * C:], rw[2 * C:]], axis=1))])
    a["bb1"] = row([t(L1 + "e_b2"), t(L1 + "gate_b2"), t(L1 + "out_b"), t(L1 + "router_b")])
    a["sv1"] = cat([cv(t(L1 + "e_b1").reshape(-1)), cv(t(L1 + "gate_b1")), cv(t(L1 + "ln_gamma")), cv(t(L1 + "ln_beta"))])

    def cols(m, order):
        return _np.concatenate([m[..., i * C:(i + 1) * C] for i in order], axis=-1)

    wq, kv = t(L2 + "W_qkv"), t(L2 + "W_kvc")
    a["w2"] = cat([cm(wq[:, 0:C]), cm(wq[:, C:2 * C]), cm(wq[:, 2 * C:]), cm(t(L2 + "W_proj")), cm(t(L2 + "W_qc")), cm(kv[:, 0:C]), cm(kv[:, C:]),
                   cm(t(L2 + "W_cproj")), cm(t(L2 + "W_mlp1")), cm(t(L2 + "W_mlp2"))])
    a["pw2"] = cat([cm(cols(t(L2 + "W_mod"), (1, 0, 4, 3, 2, 5)))])
    bm = t(L2 + "b_mod")
    a["bb2"] = row([t(L2 + "b_qkv"), t(L2 + "b_qc"), t(L2 + "b_kvc"), t(L2 + "b_proj"), t(L2 + "b_cproj"), t(L2 + "b_mlp2"), cols(bm, (2, 5))])
    a["sv2"] = cat([cv(cols(bm, (1, 0, 4, 3))), cv(t(L2 + "b_mlp1"))])

    wq, kv = t(L3 + "w_qkv"), t(L3 + "w_kv")
    a["w3"] = cat([cm(wq[:, 0:C]), cm(wq[:, C:2 * C]), cm(wq[:, 2 * C:]), cm(t(L3 + "w_so")), cm(t(L3 + "w_q")), cm(kv[:, 0:C]), cm(kv[:, C:]),
                   cm(t(L3 + "w_co")), cm(t(L3 + "w_m1")), cm(t(L3 + "w_m2"))])
    a["pw3"] = cat([cm(cols(t(L3 + "w_ada"), (1, 0, 4, 3, 7, 6, 2, 5, 8)))])
    bm = t(L3 + "b_ada")
    a["bb3"] = row([t(L3 + "b_qkv"), t(L3 + "b_q"), t(L3 + "b_kv"), t(L3 + "b_so"), t(L3 + "b_co"), t(L3 + "b_m2"), cols(bm, (2, 5, 8))])
    a["sv3"] = cat([cv(cols(bm, (1, 0, 4, 3, 7, 6))), cv(t(L3 + "b_m1"))])

    nc = _bacc.Bacc("TRN2", target_bir_lowering=False, num_devices=1)
    ins = {k: nc.dram_tensor(f"in_{k}", v.shape, _mybir.dt.from_np(v.dtype), kind="ExternalInput").ap() for k, v in a.items()}
    out = nc.dram_tensor("out_0", (B * NT, P, C), _mybir.dt.float32, kind="ExternalOutput").ap()
    four_layers(nc, ins, out)
    r = _run(nc, [{f"in_{k}": v for k, v in a.items()}], core_ids=[0])
    return r.results[0]["out_0"].reshape(B, N, C)
```
